# Optimizing a Trainium2 kernel written in Bass

```python
import numpy as np
import jax
import jax.numpy as jnp

def _softmax(x, axis=-1):
    return jax.nn.softmax(x, axis=axis)

def _gelu(x):
    return jax.nn.gelu(x, approximate=True)

def _silu(x):
    return jax.nn.silu(x)

def _sigmoid(x):
    return jax.nn.sigmoid(x)

def _layernorm(x, axis=-1, eps=1e-05):
    m = jnp.mean(x, axis=axis, keepdims=True)
    v = jnp.var(x, axis=axis, keepdims=True)
    return (x - m) / jnp.sqrt(v + eps)

def _scatter_add(tgt, idx, src, axis=0):
    return tgt.at[idx].add(src)

def _segment_sum(src, seg, n):
    return jax.ops.segment_sum(src, seg, n)
kernel_name = 'mk_gps_d1_gnn_r8_b4d0e2'

def setup_inputs(seed: int=0):
    np.random.seed(seed)
    _w = jnp.asarray

    def _rec_inputs():
        import jax
        import jax.numpy as jnp
        _gk = jax.random.key(seed)
        x = -0.0002117 + 1 * jax.random.normal(jax.random.fold_in(_gk, 1), (1250, 1024), jnp.float32)
        src = jax.random.randint(jax.random.fold_in(_gk, 2), (20000,), 0, 1250, jnp.int32)
        dst = jax.random.randint(jax.random.fold_in(_gk, 3), (20000,), 0, 1250, jnp.int32)
        _o = jnp.argsort(dst, stable=True)
        src = src[_o]
        dst = dst[_o]
        return (x, src, dst)
    x, src, dst = _rec_inputs()

    def _L0_gnn_setup():
        import jax, jax.numpy as jnp
        import numpy as np
        N_NODES = 3125
        N_EDGES = 50000
        D = 1024

        def _sage_layer(h, edge_src, edge_dst, deg_inv, W_self, W_neigh, b):
            msg = h[edge_src]
            agg = jax.ops.segment_sum(msg, edge_dst, num_segments=h.shape[0])
            mean = agg * deg_inv[:, None]
            return h @ W_self + mean @ W_neigh + b
        key = jax.random.key(seed)
        ks = jax.random.split(key, 8)
        s = 1.0 / np.sqrt(D)
        return {'x': jax.random.normal(ks[0], (N_NODES, D), dtype=jnp.float32), 'edge_src': jax.random.randint(ks[1], (N_EDGES,), 0, N_NODES, dtype=jnp.int32), 'edge_dst': jax.random.randint(ks[2], (N_EDGES,), 0, N_NODES, dtype=jnp.int32), 'W_self0': jax.random.normal(ks[3], (D, D), dtype=jnp.float32) * s, 'W_neigh0': jax.random.normal(ks[4], (D, D), dtype=jnp.float32) * s, 'b0': jnp.zeros((D,), dtype=jnp.float32), 'W_self1': jax.random.normal(ks[5], (D, D), dtype=jnp.float32) * s, 'W_neigh1': jax.random.normal(ks[6], (D, D), dtype=jnp.float32) * s, 'b1': jnp.zeros((D,), dtype=jnp.float32)}
    _L0_gnn_all = _L0_gnn_setup()
    _L0_gnn_in = {k: v for k, v in _L0_gnn_all.items() if k in ('W_self0', 'W_neigh0', 'b0', 'W_self1', 'W_neigh1', 'b1')}
    del _L0_gnn_all

    def _L0_mix_setup():
        import jax, jax.numpy as jnp
        import numpy as np
        DIM = 1024
        NUM_HEADS = 16
        HEAD_DIM = DIM // NUM_HEADS
        NB_FEATURES = 256

        def _kernel_feature_map(x, proj):
            z = jnp.einsum('bhtd,hdf->bhtf', x, proj)
            return jnp.exp(z - jnp.max(z, axis=-1, keepdims=True))
        key = jax.random.key(seed)
        k1, k2, k3, k4, k5 = jax.random.split(key, 5)
        x = jax.random.normal(k1, (4, 512, DIM), dtype=jnp.float32)
        w_qkv = jax.random.normal(k2, (DIM, 3 * DIM), dtype=jnp.float32) / np.sqrt(DIM)
        w_out = jax.random.normal(k3, (DIM, DIM), dtype=jnp.float32) / np.sqrt(DIM)
        b_out = jnp.zeros((DIM,), dtype=jnp.float32)
        proj = 0.05 * jax.random.normal(k4, (NUM_HEADS, HEAD_DIM, NB_FEATURES), dtype=jnp.float32)
        return {'x': x, 'w_qkv': w_qkv, 'w_out': w_out, 'b_out': b_out, 'proj': proj}
    _L0_mix_all = _L0_mix_setup()
    _L0_mix_in = {k: v for k, v in _L0_mix_all.items() if k in ('w_qkv', 'w_out', 'b_out', 'proj')}
    del _L0_mix_all

    def _L0_ffn_setup():
        import jax, jax.numpy as jnp
        import numpy as np
        B, S, D_MODEL, D_HIDDEN = (4, 256, 1024, 512)

        def act_quant(x):
            scale = 127.0 / jnp.clip(jnp.max(jnp.abs(x), axis=-1, keepdims=True), 1e-05)
            return jnp.clip(jnp.round(x * scale), -128, 127) / scale

        def weight_quant(w):
            scale = 1.0 / jnp.clip(jnp.mean(jnp.abs(w)), 1e-05)
            return jnp.clip(jnp.round(w * scale), -1, 1) / scale

        def bit_linear(x, w):
            xq = x + jax.lax.stop_gradient(act_quant(x) - x)
            wq = w + jax.lax.stop_gradient(weight_quant(w) - w)
            return jnp.einsum('bsd,hd->bsh', xq, wq)

        def depthwise_conv1d(x_bcl, w, b):
            y = jax.lax.conv_general_dilated(x_bcl, w, window_strides=(1,), padding=[(1, 1)], dimension_numbers=('NCH', 'OIH', 'NCH'), feature_group_count=x_bcl.shape[1])
            return y + b[None, :, None]
        key = jax.random.key(seed)
        ks = jax.random.split(key, 5)
        lim1 = 1.0 / np.sqrt(D_MODEL)
        lim2 = 1.0 / np.sqrt(D_HIDDEN)
        limc = 1.0 / np.sqrt(3.0)
        return {'x': jax.random.normal(ks[0], (B, S, D_MODEL), dtype=jnp.float32), 'w1': jax.random.uniform(ks[1], (D_HIDDEN, D_MODEL), jnp.float32, -lim1, lim1), 'conv_w': jax.random.uniform(ks[2], (D_HIDDEN, 1, 3), jnp.float32, -limc, limc), 'conv_b': jax.random.uniform(ks[3], (D_HIDDEN,), jnp.float32, -limc, limc), 'w2': jax.random.uniform(ks[4], (D_MODEL, D_HIDDEN), jnp.float32, -lim2, lim2)}
    _L0_ffn_all = _L0_ffn_setup()
    _L0_ffn_in = {k: v for k, v in _L0_ffn_all.items() if k in ('w1', 'conv_w', 'conv_b', 'w2')}
    del _L0_ffn_all
    return {'x': x, 'src': src, 'dst': dst, 'L0_gnn_W_self0': _L0_gnn_in['W_self0'], 'L0_gnn_W_neigh0': _L0_gnn_in['W_neigh0'], 'L0_gnn_b0': _L0_gnn_in['b0'], 'L0_gnn_W_self1': _L0_gnn_in['W_self1'], 'L0_gnn_W_neigh1': _L0_gnn_in['W_neigh1'], 'L0_gnn_b1': _L0_gnn_in['b1'], 'L0_mix_w_qkv': _L0_mix_in['w_qkv'], 'L0_mix_w_out': _L0_mix_in['w_out'], 'L0_mix_b_out': _L0_mix_in['b_out'], 'L0_mix_proj': _L0_mix_in['proj'], 'L0_ffn_w1': _L0_ffn_in['w1'], 'L0_ffn_conv_w': _L0_ffn_in['conv_w'], 'L0_ffn_conv_b': _L0_ffn_in['conv_b'], 'L0_ffn_w2': _L0_ffn_in['w2']}

def reference(x, src, dst, L0_gnn_W_self0, L0_gnn_W_neigh0, L0_gnn_b0, L0_gnn_W_self1, L0_gnn_W_neigh1, L0_gnn_b1, L0_mix_w_qkv, L0_mix_w_out, L0_mix_b_out, L0_mix_proj, L0_ffn_w1, L0_ffn_conv_w, L0_ffn_conv_b, L0_ffn_w2):
    import jax
    import jax.numpy as jnp

    def _L0_gnn_ref(x, edge_src, edge_dst, W_self0, W_neigh0, b0, W_self1, W_neigh1, b1):
        import jax, jax.numpy as jnp
        import numpy as np
        N_NODES = 3125
        N_EDGES = 50000
        D = 1024

        def _sage_layer(h, edge_src, edge_dst, deg_inv, W_self, W_neigh, b):
            msg = h[edge_src]
            agg = jax.ops.segment_sum(msg, edge_dst, num_segments=h.shape[0])
            mean = agg * deg_inv[:, None]
            return h @ W_self + mean @ W_neigh + b
        N = x.shape[0]
        deg = jax.ops.segment_sum(jnp.ones_like(edge_dst, dtype=x.dtype), edge_dst, num_segments=N)
        deg_inv = 1.0 / jnp.maximum(deg, 1.0)
        h = jax.nn.relu(_sage_layer(x, edge_src, edge_dst, deg_inv, W_self0, W_neigh0, b0))
        out = _sage_layer(h, edge_src, edge_dst, deg_inv, W_self1, W_neigh1, b1)
        return out

    def _L0_mix_ref(x, w_qkv, w_out, b_out, proj):
        import jax, jax.numpy as jnp
        import numpy as np
        DIM = 1024
        NUM_HEADS = 16
        HEAD_DIM = DIM // NUM_HEADS
        NB_FEATURES = 256

        def _kernel_feature_map(x, proj):
            z = jnp.einsum('bhtd,hdf->bhtf', x, proj)
            return jnp.exp(z - jnp.max(z, axis=-1, keepdims=True))
        B, T, _ = x.shape
        qkv = x @ w_qkv
        q, k, v = jnp.split(qkv, 3, axis=-1)

        def to_heads(t):
            return t.reshape(B, T, NUM_HEADS, HEAD_DIM).transpose(0, 2, 1, 3)
        q, k, v = (to_heads(q), to_heads(k), to_heads(v))
        q_prime = _kernel_feature_map(q, proj)
        k_prime = _kernel_feature_map(k, proj)
        kv = jnp.einsum('bhtf,bhtd->bhfd', k_prime, v)
        k_sum = jnp.sum(k_prime, axis=2)
        z = 1.0 / (jnp.einsum('bhtf,bhf->bht', q_prime, k_sum) + 1e-06)
        out = jnp.einsum('bhtf,bhfd,bht->bhtd', q_prime, kv, z)
        out = out.transpose(0, 2, 1, 3).reshape(B, T, DIM)
        return out @ w_out + b_out

    def _L0_ffn_ref(x, w1, conv_w, conv_b, w2):
        import jax, jax.numpy as jnp
        import numpy as np
        B, S, D_MODEL, D_HIDDEN = (4, 256, 1024, 512)

        def act_quant(x):
            scale = 127.0 / jnp.clip(jnp.max(jnp.abs(x), axis=-1, keepdims=True), 1e-05)
            return jnp.clip(jnp.round(x * scale), -128, 127) / scale

        def weight_quant(w):
            scale = 1.0 / jnp.clip(jnp.mean(jnp.abs(w)), 1e-05)
            return jnp.clip(jnp.round(w * scale), -1, 1) / scale

        def bit_linear(x, w):
            xq = x + jax.lax.stop_gradient(act_quant(x) - x)
            wq = w + jax.lax.stop_gradient(weight_quant(w) - w)
            return jnp.einsum('bsd,hd->bsh', xq, wq)

        def depthwise_conv1d(x_bcl, w, b):
            y = jax.lax.conv_general_dilated(x_bcl, w, window_strides=(1,), padding=[(1, 1)], dimension_numbers=('NCH', 'OIH', 'NCH'), feature_group_count=x_bcl.shape[1])
            return y + b[None, :, None]
        h = bit_linear(x, w1)
        h = depthwise_conv1d(h.transpose(0, 2, 1), conv_w, conv_b)
        h = h.transpose(0, 2, 1)
        h = jax.nn.silu(h)
        return bit_linear(h, w2)
    xn = _layernorm(x, axis=-1)
    x = x + _L0_gnn_ref(xn, src, dst, L0_gnn_W_self0, L0_gnn_W_neigh0, L0_gnn_b0, L0_gnn_W_self1, L0_gnn_W_neigh1, L0_gnn_b1) + _L0_mix_ref(xn[None], L0_mix_w_qkv, L0_mix_w_out, L0_mix_b_out, L0_mix_proj)[0]
    x = x + _L0_ffn_ref(_layernorm(x, axis=-1)[None], L0_ffn_w1, L0_ffn_conv_w, L0_ffn_conv_b, L0_ffn_w2)[0]
    return x

_drawn_inputs = setup_inputs


def setup_inputs(seed=0):
    import zlib

    import numpy as np

    out = dict(_drawn_inputs(seed))
    spreads = {'L0_gnn_b0': (0.0, 0.1), 'L0_gnn_b1': (0.0, 0.1), 'L0_mix_b_out': (0.0, 0.1)}
    factors = {'L0_mix_w_out': 2.727, 'L0_mix_proj': 8.0}
    for name, (base, spread) in spreads.items():
        noise = np.random.default_rng([zlib.crc32(name.encode()), seed]).standard_normal(out[name].shape)
        drawn = base * np.exp(spread * noise) if base else spread * noise
        out[name] = jnp.asarray(drawn.astype(out[name].dtype))
    for name, factor in factors.items():
        out[name] = (out[name] * factor).astype(out[name].dtype)
    return out
```

```python
from contextlib import ExitStack

import concourse.bass as bass
from concourse import mybir

F32 = mybir.dt.float32
F32R = mybir.dt.float32r
BF16 = mybir.dt.bfloat16
I32 = mybir.dt.int32
ALU = mybir.AluOpType
ACT = mybir.ActivationFunctionType
AX_X = mybir.AxisListType.X
ds = bass.ds

N, D, E = 1250, 1024, 20000
P = 128
M = 125
NT = N // M
KC = D // P
CT = 3
CW = 418
NP = CT * CW
BANK = 512
EPS_LN = 1e-5


class Pool:

    def __init__(self, nc, stack, tag):
        self.nc, self.stack, self.tag, self.sems = nc, stack, tag, []
        stack.callback(self.close)

    def close(self):
        if self.sems:
            self.nc.clear_and_free_semaphores(self.sems)
            self.nc.all_engine_barrier()

    def sb(self, name, shape, dt, side="left"):
        return self.stack.enter_context(self.nc.sbuf_tensor(f"{self.tag}_{name}", shape, dt, side=side))

    def psum(self, name, shape, dt=F32):
        return self.stack.enter_context(self.nc.psum_tensor(f"{self.tag}_{name}", shape, dt))

    def bank(self, name):
        return self.psum(name, [P, BANK])

    def sem(self, name):
        self.sems.append(self.nc.alloc_semaphore(name=f"{self.tag}_{name}"))
        return self.sems[-1]


def stage_norm(nc, x, ident, ident_b, ones_r, xT_hi, xT_lo):
    with ExitStack() as stack:
        m = Pool(nc, stack, "norm")
        x_in = m.sb("x_in", [P, 2, D], F32)
        xn = m.sb("xn", [P, 2, D], F32)
        stats = m.sb("stats", [P, 2, 6], F32)
        mv = m.sb("mv", [P, 2], F32)
        rs = m.sb("rs", [P, 6], F32)
        tp_banks = [m.bank(f"tp{i}") for i in range(4)]
        tp = [b[:, 0:4 * M].rearrange("p (c n) -> p c n", n=M) for b in tp_banks]
        x_loaded = [m.sem(f"x_loaded{b}") for b in range(2)]
        x_read = m.sem("x_read")
        var_ready = m.sem("var_ready")
        root_ready = m.sem("root_ready")
        xn_ready = m.sem("xn_ready")
        xn_read = m.sem("xn_read")
        turned = m.sem("turned")
        turned_hi = m.sem("turned_hi")
        turned_lo = m.sem("turned_lo")
        const_ready = m.sem("const_ready")
        chain = m.sem("chain")
        stats_seen = m.sem("stats_seen")
        block = stack.enter_context(nc.Block())

        @block.sync
        def _(sp):
            sp.sem_inc(x_read, 2)
            with sp.Fori(0, NT // 2) as i:
                for b in range(2):
                    sp.wait_ge(x_read, i * 2 + (b + 1))
                    sp.dma_start(x_in[0:M, b, :], x[ds(i * (2 * M) + b * M, M), :]).then_inc(x_loaded[b], 16)

        @block.gpsimd
        def _(pool):
            pool.memset(ident[:, :], 0.0).then_inc(const_ready, 1)
            pool.wait_ge(const_ready, 1)
            pool.affine_select(out=ident[:, :], in_=ident[:, :], compare_op=ALU.not_equal, fill=1.0,
                               base=0, pattern=[[-1, P]], channel_multiplier=1).then_inc(const_ready, 1)
            pool.wait_ge(const_ready, 2)
            pool.tensor_copy(ident_b[:, :], ident[:, :])

        @block.vector
        def _(dve):
            nc.vector.memset(ones_r[:, :].bitcast(F32), 1.0)
            nc.vector.memset(xT_hi[:, :, N:NP].bitcast(F32), 0.0)
            nc.vector.memset(xT_lo[:, :, N:NP].bitcast(F32), 0.0)
            dve.sem_inc(xn_read, 2)
            with dve.Fori(0, NT // 2) as i:
                for b in range(2):
                    c0 = i * 18 + b * 9
                    dve.wait_ge(x_loaded[b], i * 16 + 16)
                    nc.vector.bn_stats(stats[0:M, 0, :], x_in[0:M, b, 0:512]).then_inc(chain, 1)
                    nc.vector.bn_stats(stats[0:M, 1, :], x_in[0:M, b, 512:D]).then_inc(chain, 1)
                    dve.wait_ge(chain, c0 + 2)
                    dve.sem_inc(stats_seen, 1)
                    nc.vector.bn_aggr(mv[0:M, :], stats[0:M, :, :]).then_inc(chain, 1)
                    dve.wait_ge(chain, c0 + 3)
                    nc.vector.tensor_scalar(rs[0:M, 0:1], mv[0:M, 1:2], EPS_LN, None, ALU.add).then_inc(var_ready, 1)
                    dve.wait_ge(root_ready, i * 2 + (b + 1))
                    nc.vector.reciprocal(rs[0:M, 2:3], rs[0:M, 1:2]).then_inc(chain, 1)
                    dve.wait_ge(chain, c0 + 4)
                    nc.vector.tensor_tensor(rs[0:M, 3:4], rs[0:M, 2:3], rs[0:M, 2:3], ALU.mult).then_inc(chain, 1)
                    dve.wait_ge(chain, c0 + 5)
                    nc.vector.tensor_tensor(rs[0:M, 4:5], rs[0:M, 3:4], rs[0:M, 0:1], ALU.mult).then_inc(chain, 1)
                    dve.wait_ge(chain, c0 + 6)
                    nc.vector.tensor_scalar(rs[0:M, 4:5], rs[0:M, 4:5], -0.5, 1.5, ALU.mult, ALU.add).then_inc(chain, 1)
                    dve.wait_ge(chain, c0 + 7)
                    nc.vector.tensor_tensor(rs[0:M, 5:6], rs[0:M, 4:5], rs[0:M, 2:3], ALU.mult).then_inc(chain, 1)
                    dve.wait_ge(chain, c0 + 8)
                    dve.wait_ge(xn_read, i * 2 + (b + 1))
                    nc.vector.tensor_scalar(xn[0:M, b, :], x_in[0:M, b, :], mv[0:M, 0:1], rs[0:M, 5:6],
                                            ALU.subtract, ALU.mult).then_inc(xn_ready, 1)
                    dve.wait_ge(xn_ready, i * 2 + (b + 1))
                    dve.sem_inc(x_read, 1)
                    dve.sem_inc(chain, 1)
                    for h in range(2):
                        dve.wait_ge(turned_hi, i * 4 + (2 * b + h + 1))
                        nc.vector.tensor_tensor(xT_lo[:, 4 * h:4 * h + 4, ds(i * (2 * M) + b * M, M)],
                                                tp[2 * b + h][:, :, :],
                                                xT_hi[:, 4 * h:4 * h + 4, ds(i * (2 * M) + b * M, M)].bitcast(F32),
                                                ALU.subtract).then_inc(turned_lo, 1)

        @block.scalar
        def _(act):
            with act.Fori(0, NT // 2) as i:
                for b in range(2):
                    act.wait_ge(var_ready, i * 2 + (b + 1))
                    nc.scalar.activation(rs[0:M, 1:2], rs[0:M, 0:1], ACT.Sqrt).then_inc(root_ready, 1)
                    for h in range(2):
                        act.wait_ge(turned, i * 4 + (2 * b + h + 1))
                        nc.scalar.copy(xT_hi[:, 4 * h:4 * h + 4, ds(i * (2 * M) + b * M, M)],
                                       tp[2 * b + h][:, :, :]).then_inc(turned_hi, 1)

        @block.tensor
        def _(pe):
            pe.wait_ge(const_ready, 2)
            pe.sem_inc(turned_lo, 4)
            with pe.Fori(0, NT // 2) as i:
                for b in range(2):
                    pe.wait_ge(xn_ready, i * 2 + (b + 1))
                    for h in range(2):
                        pe.wait_ge(turned_lo, i * 4 + (2 * b + h + 1))
                        for c in range(4):
                            k = 4 * h + c
                            last = nc.tensor.transpose(tp[2 * b + h][:, c, :], xn[0:M, b, k * P:(k + 1) * P],
                                                       ident[0:M, 0:M])
                        last.then_inc(turned, 1)
                    pe.wait_ge(turned, i * 4 + (2 * b + 2))
                    pe.sem_inc(xn_read, 1)


W = 25
NW = N // W
WC = NT * W
EC = 4
ECAP = EC * P
ER = E // M
GC = 8
ROUND = 12582912.0


def stage_graph(nc, src, dst, src_pad, dst_pad, ident, ones_r, adj, inv_row, inv_col):
    with ExitStack() as stack:
        m = Pool(nc, stack, "graph")
        dst_i = m.sb("dst_i", [P, ER], I32)
        src_i = m.sb("src_i", [P, ER], I32)
        next_i = m.sb("next_i", [P, 1], I32)
        dst_f = m.sb("dst_f", [P, ER], F32)
        next_f = m.sb("next_f", [P, 1], F32)
        pad_i = m.sb("pad_i", [1, ECAP], I32)
        below = m.sb("below", [P, NW + 1, ER], BF16)
        back = m.sb("back", [P, ER], F32)
        limit = m.sb("limit", [P, NW + 1], F32)
        part = m.sb("part", [P, NW + 4], F32)
        start_f = m.sb("start_f", [P, NW + 4], F32)
        start_i = m.sb("start_i", [P, NW + 4], I32)
        load_f = m.sb("load_f", [P, NW], F32)
        flag_f = m.sb("flag_f", [P, 2], F32)
        flag_i = m.sb("flag_i", [P, 1], I32)
        iota_b = m.sb("iota_b", [P, P], BF16)
        iota_c = m.sb("iota_c", [P, WC], BF16)
        src_w = m.sb("src_w", [P, NW, EC], I32)
        dst_w = m.sb("dst_w", [P, NW, EC], I32)
        s_f = m.sb("s_f", [P, NW, EC], F32)
        d_f = m.sb("d_f", [P, NW, EC], F32)
        a_f = m.sb("a_f", [P, NW, EC], F32)
        b_f = m.sb("b_f", [P, NW, EC], F32)
        in_f = m.sb("in_f", [P, NW, EC], F32)
        col_f = m.sb("col_f", [P, NW, EC], F32)
        hot_b = m.sb("hot_b", [P, 2 * GC, P], BF16)
        hot_c = m.sb("hot_c", [P, 2 * GC, WC], BF16)
        ps_w = [m.bank(f"ps_w{i}")[:, 0:WC].rearrange("p (a d) -> p a d", d=W) for i in range(2)]
        ps_sum = m.bank("ps_sum")[:, 0:NW + 4]
        ps_deg = [m.bank(f"ps_deg{t}")[:, 0:CW] for t in range(CT)]
        ps_col = m.bank("ps_col")[:, 0:NT]
        edges_in = m.sem("edges_in")
        next_in = m.sem("next_in")
        pad_set = m.sem("pad_set")
        padded = m.sem("padded")
        consts = m.sem("consts")
        counted = m.sem("counted")
        summed = m.sem("summed")
        flag_set = m.sem("flag_set")
        windows_in = m.sem("windows_in")
        chain = [m.sem(f"chain_{n}") for n in ("count", "short", "general", "degree")]
        columns_set = m.sem("columns_set")
        hot_ready = m.sem("hot_ready")
        hot_used = m.sem("hot_used")
        window_done = m.sem("window_done")
        window_kept = m.sem("window_kept")
        zeroed = m.sem("zeroed")
        deg_ready = m.sem("deg_ready")
        inv_ready = m.sem("inv_ready")
        col_ready = m.sem("col_ready")
        block = stack.enter_context(nc.Block())

        rows = lambda t: t.rearrange("(p c) -> p c", c=ER)

        @block.sync
        def _(sp):
            sp.dma_start(dst_i[0:M, :], rows(dst)).then_inc(edges_in, 16)
            sp.dma_start(src_i[0:M, :], rows(src)).then_inc(edges_in, 16)
            with nc.allow_non_contiguous_dma(reason="one word of each row"):
                sp.dma_start(next_i[0:M - 1, :], rows(dst)[1:M, 0:1]).then_inc(next_in, 16)
            sp.dma_start(rows(dst_pad[0:E]), rows(dst)).then_inc(padded, 16)
            sp.dma_start(rows(src_pad[0:E]), rows(src)).then_inc(padded, 16)
            sp.wait_ge(pad_set, 1)
            for t in (dst_pad, src_pad):
                sp.dma_start(t[E:E + ECAP].rearrange("(a c) -> a c", a=1), pad_i[:, :]).then_inc(padded, 16)
            sp.wait_ge(padded, 64)
            sp.wait_ge(flag_set, 1)
            every = sp.value_load(flag_i[0:1, 0:1], min_val=0, max_val=1)
            with sp.If(every < 1):
                with sp.Fori(0, NW) as j:
                    first = sp.value_load(start_i[0:1, ds(j, 1)], min_val=0, max_val=E)
                    sp.dma_start(dst_w[:, ds(j, 1), :].rearrange("p a c -> p (a c)"),
                                 dst_pad[ds(first, ECAP)].rearrange("(p c) -> p c", c=EC)).then_inc(windows_in, 16)
                    sp.dma_start(src_w[:, ds(j, 1), :].rearrange("p a c -> p (a c)"),
                                 src_pad[ds(first, ECAP)].rearrange("(p c) -> p c", c=EC)).then_inc(windows_in, 16)

        @block.gpsimd
        def _(pool):
            pool.iota(pad_i[:, :], [[0, ECAP]], base=-1, channel_multiplier=0).then_inc(pad_set, 1)
            pool.iota(limit[:, :], [[W, NW + 1]], base=0, channel_multiplier=0,
                      allow_small_or_imprecise_dtypes=True).then_inc(consts, 1)
            pool.iota(iota_b[:, :], [[1, P]], base=0, channel_multiplier=0,
                      allow_small_or_imprecise_dtypes=True).then_inc(consts, 1)
            pool.iota(iota_c[:, :], [[1, WC]], base=0, channel_multiplier=0,
                      allow_small_or_imprecise_dtypes=True).then_inc(consts, 1)

        @block.vector
        def _(dve):
            at = [0, 0]

            def link(ins):
                at[1] += 1
                ins.then_inc(chain[at[0]], 1)
                dve.wait_ge(chain[at[0]], at[1])

            nc.vector.memset(adj[:, :, N:NP].bitcast(F32), 0.0).then_inc(zeroed, 1)
            link(nc.vector.memset(part[:, :], 0.0))
            dve.wait_ge(consts, 3)
            dve.wait_ge(edges_in, 32)
            dve.wait_ge(next_in, 16)
            link(nc.vector.tensor_copy(dst_f[0:M, :], dst_i[0:M, :]))
            link(nc.vector.tensor_copy(next_f[0:M - 1, :], next_i[0:M - 1, :]))
            link(nc.vector.tensor_tensor(below[0:M, :, :],
                                         dst_f[0:M, :].unsqueeze(1).to_broadcast([M, NW + 1, ER]),
                                         limit[0:M, :].unsqueeze(2).to_broadcast([M, NW + 1, ER]), ALU.is_lt))
            link(nc.vector.tensor_reduce(part[0:M, 0:NW + 1], below[0:M, :, :], AX_X, ALU.add))
            link(nc.vector.tensor_tensor(back[0:M, 0:ER - 1], dst_f[0:M, 0:ER - 1], dst_f[0:M, 1:ER], ALU.is_gt))
            link(nc.vector.tensor_reduce(part[0:M, NW + 1:NW + 2], back[0:M, 0:ER - 1], AX_X, ALU.add))
            nc.vector.tensor_tensor(part[0:M - 1, NW + 2:NW + 3], dst_f[0:M - 1, ER - 1:ER],
                                    next_f[0:M - 1, :], ALU.is_gt).then_inc(counted, 1)
            dve.wait_ge(summed, 1)
            link(nc.vector.tensor_copy(start_f[:, :], ps_sum[:, :]))
            link(nc.vector.tensor_copy(start_i[:, :], start_f[:, :]))
            link(nc.vector.tensor_tensor(load_f[:, :], start_f[:, 1:NW + 1], start_f[:, 0:NW], ALU.subtract))
            link(nc.vector.tensor_reduce(flag_f[:, 0:1], load_f[:, :], AX_X, ALU.max))
            link(nc.vector.tensor_scalar(flag_f[:, 0:1], flag_f[:, 0:1], float(ECAP), None, ALU.is_gt))
            link(nc.vector.tensor_tensor(flag_f[:, 0:1], flag_f[:, 0:1], start_f[:, NW + 1:NW + 2], ALU.add))
            link(nc.vector.tensor_tensor(flag_f[:, 0:1], flag_f[:, 0:1], start_f[:, NW + 2:NW + 3], ALU.add))
            nc.vector.tensor_scalar(flag_i[:, :], flag_f[:, 0:1], 1.0, None, ALU.min).then_inc(flag_set, 1)
            dve.wait_ge(flag_set, 1)

            def split_source(a, b, s):
                link(nc.vector.tensor_scalar(a, s, 1.0 / M, 0.5 / M - 0.5, ALU.mult, ALU.add))
                link(nc.vector.tensor_scalar(a, a, ROUND, ROUND, ALU.add, ALU.subtract))
                link(nc.vector.scalar_tensor_tensor(b, a, -float(M), s, ALU.mult, ALU.add))

            every = dve.value_load(flag_i[0:1, 0:1], min_val=0, max_val=1)
            dve.sem_inc(hot_used, 2 * GC)
            at[:] = 1, 0
            with dve.If(every < 1):
                dve.wait_ge(windows_in, 32 * NW)
                link(nc.vector.tensor_copy(s_f[:, :, :], src_w[:, :, :]))
                link(nc.vector.tensor_copy(d_f[:, :, :], dst_w[:, :, :]))
                split_source(a_f[:, :, :], b_f[:, :, :], s_f[:, :, :])
                link(nc.vector.tensor_tensor(d_f[:, :, :], d_f[:, :, :],
                                             limit[:, 0:NW].unsqueeze(2).to_broadcast([P, NW, EC]), ALU.subtract))
                link(nc.vector.tensor_scalar(in_f[:, :, :], d_f[:, :, :], 0.0, None, ALU.is_ge))
                link(nc.vector.scalar_tensor_tensor(in_f[:, :, :], d_f[:, :, :], W - 1.0, in_f[:, :, :],
                                                    ALU.is_le, ALU.mult))
                link(nc.vector.scalar_tensor_tensor(col_f[:, :, :], a_f[:, :, :], float(W), d_f[:, :, :],
                                                    ALU.mult, ALU.add))
                link(nc.vector.scalar_tensor_tensor(col_f[:, :, :], col_f[:, :, :], 1.0, in_f[:, :, :],
                                                    ALU.add, ALU.mult))
                link(nc.vector.tensor_scalar(col_f[:, :, :], col_f[:, :, :], -1.0, None, ALU.add))
                with dve.Fori(0, NW // 4) as q:
                    for w in range(4):
                        for c in range(EC):
                            h = w * EC + c
                            dve.wait_ge(hot_used, q * (2 * GC) + (h + 1))
                            nc.vector.tensor_scalar(hot_b[:, h, :], iota_b[:, :],
                                                    b_f[:, ds(q * 4 + w, 1), c:c + 1].rearrange("p a c -> p (a c)"),
                                                    None, ALU.is_equal)
                            nc.vector.tensor_scalar(hot_c[:, h, :], iota_c[:, :],
                                                    col_f[:, ds(q * 4 + w, 1), c:c + 1].rearrange("p a c -> p (a c)"),
                                                    None, ALU.is_equal).then_inc(hot_ready, 1)
                for w in range(NW - NW // 4 * 4):
                    for c in range(EC):
                        h = w * EC + c
                        dve.wait_ge(hot_used, NW // 4 * 2 * GC + h + 1)
                        nc.vector.tensor_scalar(hot_b[:, h, :], iota_b[:, :], b_f[:, NW // 4 * 4 + w, c:c + 1],
                                                None, ALU.is_equal)
                        nc.vector.tensor_scalar(hot_c[:, h, :], iota_c[:, :], col_f[:, NW // 4 * 4 + w, c:c + 1],
                                                None, ALU.is_equal).then_inc(hot_ready, 1)
            at[:] = 2, 0
            with dve.If(every > 0):
                flat = lambda t: t[0:M, :, :].rearrange("p a c -> p (a c)")[:, 0:ER]
                link(nc.vector.tensor_copy(flat(s_f), src_i[0:M, :]))
                split_source(flat(a_f), flat(b_f), flat(s_f))
                with dve.Fori(0, NW) as j:
                    c0 = j * 5 + at[1]
                    nc.vector.tensor_scalar(flat(d_f), dst_f[0:M, :], limit[0:M, ds(j, 1)], None,
                                            ALU.subtract).then_inc(chain[2], 1)
                    dve.wait_ge(chain[2], c0 + 1)
                    nc.vector.tensor_scalar(flat(in_f), flat(d_f), 0.0, None, ALU.is_ge).then_inc(chain[2], 1)
                    dve.wait_ge(chain[2], c0 + 2)
                    nc.vector.scalar_tensor_tensor(flat(in_f), flat(d_f), W - 1.0, flat(in_f),
                                                   ALU.is_le, ALU.mult).then_inc(chain[2], 1)
                    nc.vector.scalar_tensor_tensor(flat(col_f), flat(a_f), float(W), flat(d_f),
                                                   ALU.mult, ALU.add).then_inc(chain[2], 1)
                    dve.wait_ge(chain[2], c0 + 4)
                    nc.vector.scalar_tensor_tensor(flat(col_f), flat(col_f), 1.0, flat(in_f),
                                                   ALU.add, ALU.mult).then_inc(chain[2], 1)
                    dve.wait_ge(chain[2], c0 + 5)
                    dve.sem_inc(columns_set, 1)
                    with dve.Fori(0, ER // (2 * GC)) as g:
                        for h in range(2 * GC):
                            dve.wait_ge(hot_used, j * ER + g * (2 * GC) + (h + 1))
                            nc.vector.tensor_scalar(hot_b[0:M, h, :], iota_b[0:M, :],
                                                    flat(b_f)[:, ds(g * (2 * GC) + h, 1)], None, ALU.is_equal)
                            nc.vector.tensor_scalar(hot_c[0:M, h, :], iota_c[0:M, :], 1.0,
                                                    flat(col_f)[:, ds(g * (2 * GC) + h, 1)],
                                                    ALU.add, ALU.is_equal).then_inc(hot_ready, 1)
            at[:] = 3, 0
            for t in range(CT):
                dve.wait_ge(deg_ready, t + 1)
                link(nc.vector.tensor_scalar(inv_row[:, t * CW:(t + 1) * CW], ps_deg[t][:, :], 1.0, None, ALU.max))
                nc.vector.reciprocal(inv_row[:, t * CW:(t + 1) * CW],
                                     inv_row[:, t * CW:(t + 1) * CW]).then_inc(inv_ready, 1)
            dve.wait_ge(col_ready, 1)
            nc.vector.tensor_copy(inv_col[0:M, :], ps_col[0:M, :]).then_inc(inv_ready, 1)

        @block.tensor
        def _(pe):
            pe.wait_ge(counted, 1)
            nc.tensor.matmul(ps_sum[:, :], ones_r[0:M, :].bitcast(F32), part[0:M, :],
                             start=True, stop=True).then_inc(summed, 1)
            pe.wait_ge(flag_set, 1)
            pe.sem_inc(window_kept, 2)
            every = pe.value_load(flag_i[0:1, 0:1], min_val=0, max_val=1)
            with pe.If(every < 1):
                def window(w, kept, ready):
                    pe.wait_ge(window_kept, kept)
                    for c in range(EC):
                        h = w * EC + c
                        pe.wait_ge(hot_ready, ready + (h + 1))
                        last = nc.tensor.matmul(ps_w[w % 2][:, :, :], hot_b[:, h, :], hot_c[:, h, :],
                                                start=(c == 0), stop=(c == EC - 1)).then_inc(hot_used, 1)
                    pe.wait_ge(hot_used, ready + (2 * GC + w * EC + EC))
                    pe.sem_inc(window_done, 1)

                with pe.Fori(0, NW // 4) as q:
                    for w in range(4):
                        window(w, q * 4 + (w + 1), q * (2 * GC))
                for w in range(NW - NW // 4 * 4):
                    window(w, NW // 4 * 4 + w + 1, NW // 4 * 2 * GC)
            with pe.If(every > 0):
                def group(b, ready, first, final):
                    for h in range(2 * GC):
                        pe.wait_ge(hot_ready, ready + (h + 1))
                        nc.tensor.matmul(ps_w[b][:, :, :], hot_b[0:M, h, :], hot_c[0:M, h, :],
                                         start=(first and h == 0), stop=(final and h == 2 * GC - 1)).then_inc(hot_used, 1)

                with pe.Fori(0, NW // 2) as q:
                    for b in range(2):
                        pe.wait_ge(window_kept, q * 2 + (b + 1))
                        base = q * (2 * ER) + b * ER
                        group(b, base, True, False)
                        with pe.Fori(1, ER // (2 * GC) - 1) as g:
                            group(b, base + g * (2 * GC), False, False)
                        group(b, base + (ER - 2 * GC), False, True)
                        pe.wait_ge(hot_used, base + (ER + 2 * GC))
                        pe.sem_inc(window_done, 1)
            pe.wait_ge(window_kept, NW + 2)
            pe.wait_ge(zeroed, 1)
            for t in range(CT):
                for a in range(NT):
                    last = nc.tensor.matmul(ps_deg[t][:, :], ones_r[0:M, :], adj[0:M, a, t * CW:(t + 1) * CW],
                                            start=(a == 0), stop=(a == NT - 1))
                last.then_inc(deg_ready, 1)
            pe.wait_ge(inv_ready, CT)
            for a in range(NT):
                last = nc.tensor.transpose(ps_col[0:M, a:a + 1], inv_row[0:1, a * M:(a + 1) * M], ident[0:1, 0:1])
            last.then_inc(col_ready, 1)

        @block.scalar
        def _(act):
            with act.Fori(0, NW // 2) as q:
                for b in range(2):
                    act.wait_ge(window_done, q * 2 + (b + 1))
                    nc.scalar.copy(adj[0:M, :, ds(q * (2 * W) + b * W, W)], ps_w[b][0:M, :, :]).then_inc(window_kept, 1)


TURNS = ((0, 4), (4, 8), (8, NT))


def panel(w, j, width=P):
    return w[:, ds(j * width, width)].rearrange("(c p) n -> p c n", p=P)


def exact_product(pe, out, pairs):
    for n, (lh, ll, rh, rl) in enumerate(pairs):
        first, final = n == 0, n == len(pairs) - 1
        pe.matmul(out, lh, rh, start=first, stop=False)
        pe.matmul(out, lh, rl, start=False, stop=False)
        last = pe.matmul(out, ll, rh, start=False, stop=final)
    return last


def stage_sage0(nc, w_neigh, w_self, bias, xT_hi, xT_lo, adj, inv_row, ident, hT_hi_dram, hT_lo_dram):
    with ExitStack() as stack:
        m = Pool(nc, stack, "sage0")
        raw_n = m.sb("raw_n", [P, KC, P], F32)
        raw_s = m.sb("raw_s", [P, KC, P], F32)
        wn_hi = m.sb("wn_hi", [P, KC, P], F32R)
        wn_lo = m.sb("wn_lo", [P, KC, P], F32R)
        ws_hi = m.sb("ws_hi", [P, KC, P], F32R)
        ws_lo = m.sb("ws_lo", [P, KC, P], F32R)
        b_col = m.sb("b_col", [P, KC], F32)
        pT = m.sb("pT", [P, NP], F32)
        p_hi = m.sb("p_hi", [P, NT, P], F32R)
        p_lo = m.sb("p_lo", [P, NT, P], F32R)
        mean = m.sb("mean", [P, CT, CW], F32)
        pre = m.sb("pre", [P, CT, CW], F32)
        h_hi = m.sb("h_hi", [P, CT, CW], F32R)
        h_lo = m.sb("h_lo", [P, CT, CW], F32R)
        ps_n = [m.psum(f"ps_n{t}", [P, BANK]) for t in range(CT)]
        ps_s = [m.psum(f"ps_s{t}", [P, BANK]) for t in range(CT)]
        ps_t = [m.psum(f"ps_t{i}", [P, 4, P]) for i in range(2)]
        bias_in = m.sem("bias_in")
        raw_n_in = m.sem("raw_n_in")
        raw_s_in = m.sem("raw_s_in")
        wn_hi_ready = m.sem("wn_hi_ready")
        wn_ready = m.sem("wn_ready")
        ws_hi_ready = m.sem("ws_hi_ready")
        ws_ready = m.sem("ws_ready")
        n_done = m.sem("n_done")
        s_done = m.sem("s_done")
        pT_ready = m.sem("pT_ready")
        turned = m.sem("turned")
        p_hi_ready = m.sem("p_hi_ready")
        p_ready = m.sem("p_ready")
        agg_done = m.sem("agg_done")
        mean_ready = m.sem("mean_ready")
        pre_ready = m.sem("pre_ready")
        h_hi_ready = m.sem("h_hi_ready")
        h_ready = m.sem("h_ready")
        h_out = [m.sem(f"h_out{t}") for t in range(CT)]
        block = stack.enter_context(nc.Block())
        cols = lambda t: slice(t * CW, (t + 1) * CW)

        @block.sync
        def _(sp):
            with nc.allow_non_contiguous_dma(reason="a bias, one word a partition"):
                sp.dma_start(b_col[:, :], bias.rearrange("(c p) -> p c", p=P)).then_inc(bias_in, 16)
            sp.dma_start(raw_n[:, :, :], panel(w_neigh, 0)).then_inc(raw_n_in, 16)
            sp.dma_start(raw_s[:, :, :], panel(w_self, 0)).then_inc(raw_s_in, 16)

            def chunk(j, last=False):
                if not last:
                    sp.wait_ge(wn_ready, j + 1)
                    sp.dma_start(raw_n[:, :, :], panel(w_neigh, j + 1)).then_inc(raw_n_in, 16)
                    sp.wait_ge(ws_ready, j + 1)
                    sp.dma_start(raw_s[:, :, :], panel(w_self, j + 1)).then_inc(raw_s_in, 16)
                for t in range(CT):
                    sp.wait_ge(h_ready, j * CT + (t + 1))
                    sp.dma_start(hT_hi_dram[ds(j * P, P), cols(t)], h_hi[:, t, :].bitcast(F32)).then_inc(h_out[t], 16)
                    sp.dma_start(hT_lo_dram[ds(j * P, P), cols(t)], h_lo[:, t, :].bitcast(F32)).then_inc(h_out[t], 16)

            with sp.Fori(0, KC - 1) as j:
                chunk(j)
            chunk(KC - 1, last=True)
            for t in range(CT):
                sp.wait_ge(h_out[t], 32 * KC + 32)

        @block.scalar
        def _(act):
            def split_n(j):
                act.wait_ge(raw_n_in, j * 16 + 16)
                nc.scalar.copy(wn_hi[:, :, :], raw_n[:, :, :]).then_inc(wn_hi_ready, 1)

            def split_s(j):
                act.wait_ge(raw_s_in, j * 16 + 16)
                nc.scalar.copy(ws_hi[:, :, :], raw_s[:, :, :]).then_inc(ws_hi_ready, 1)

            def chunk(j, last=False):
                for t in range(CT):
                    act.wait_ge(n_done, j * CT + (t + 1))
                    nc.scalar.copy(pT[:, cols(t)], ps_n[t][:, 0:CW]).then_inc(pT_ready, 1)
                if not last:
                    split_n(j + 1)
                for g, (a, b) in enumerate(TURNS):
                    act.wait_ge(turned, j * 3 + (g + 1))
                    nc.scalar.copy(p_hi[0:M, a:b, :], ps_t[g % 2][0:M, 0:b - a, :]).then_inc(p_hi_ready, 1)
                if not last:
                    act.wait_ge(s_done, j * CT + CT)
                    split_s(j + 1)
                for t in range(CT):
                    act.wait_ge(pre_ready, j * CT + (CT + t + 1))
                    act.wait_ge(h_out[t], j * 32 + 32)
                    nc.scalar.activation(h_hi[:, t, :], pre[:, t, :], ACT.Relu).then_inc(h_hi_ready, 1)

            for t in range(CT):
                act.sem_inc(h_out[t], 32)
            split_n(0)
            split_s(0)
            with act.Fori(0, KC - 1) as j:
                chunk(j)
            chunk(KC - 1, last=True)

        @block.vector
        def _(dve):
            def split_n(j):
                dve.wait_ge(wn_hi_ready, j + 1)
                nc.vector.tensor_tensor(wn_lo[:, :, :], raw_n[:, :, :], wn_hi[:, :, :].bitcast(F32),
                                        ALU.subtract).then_inc(wn_ready, 1)

            def split_s(j):
                dve.wait_ge(ws_hi_ready, j + 1)
                nc.vector.tensor_tensor(ws_lo[:, :, :], raw_s[:, :, :], ws_hi[:, :, :].bitcast(F32),
                                        ALU.subtract).then_inc(ws_ready, 1)

            def chunk(j, last=False):
                if not last:
                    split_n(j + 1)
                for g, (a, b) in enumerate(TURNS):
                    dve.wait_ge(p_hi_ready, j * 3 + (g + 1))
                    nc.vector.tensor_tensor(p_lo[0:M, a:b, :], ps_t[g % 2][0:M, 0:b - a, :],
                                            p_hi[0:M, a:b, :].bitcast(F32), ALU.subtract).then_inc(p_ready, 1)
                if not last:
                    split_s(j + 1)
                for t in range(CT):
                    dve.wait_ge(agg_done, j * CT + (t + 1))
                    nc.vector.tensor_tensor(mean[:, t, :], ps_n[t][:, 0:CW], inv_row[:, cols(t)],
                                            ALU.mult).then_inc(mean_ready, 1)
                    dve.wait_ge(mean_ready, j * CT + (CT + t + 1))
                    nc.vector.scalar_tensor_tensor(pre[:, t, :], ps_s[t][:, 0:CW], b_col[:, ds(j, 1)],
                                                   mean[:, t, :], ALU.add, ALU.add).then_inc(pre_ready, 1)
                for t in range(CT):
                    dve.wait_ge(h_hi_ready, j * CT + (t + 1))
                    nc.vector.scalar_tensor_tensor(h_lo[:, t, :], pre[:, t, :], 0.0, h_hi[:, t, :].bitcast(F32),
                                                   ALU.max, ALU.subtract).then_inc(h_ready, 1)

            dve.sem_inc(mean_ready, CT)
            dve.sem_inc(pre_ready, CT)
            dve.sem_inc(p_ready, 1)
            dve.wait_ge(bias_in, 16)
            split_n(0)
            split_s(0)
            with dve.Fori(0, KC - 1) as j:
                chunk(j)
            chunk(KC - 1, last=True)

        @block.tensor
        def _(pe):
            def chunk(j):
                pe.wait_ge(wn_ready, j + 1)
                for t in range(CT):
                    pe.wait_ge(mean_ready, j * CT + (t + 1))
                    exact_product(pe, ps_n[t][:, 0:CW],
                                  [(wn_hi[:, k, :], wn_lo[:, k, :], xT_hi[:, k, cols(t)], xT_lo[:, k, cols(t)])
                                   for k in range(KC)]).then_inc(n_done, 1)
                pe.wait_ge(ws_ready, j + 1)
                for t in range(CT):
                    pe.wait_ge(pre_ready, j * CT + (t + 1))
                    exact_product(pe, ps_s[t][:, 0:CW],
                                  [(ws_hi[:, k, :], ws_lo[:, k, :], xT_hi[:, k, cols(t)], xT_lo[:, k, cols(t)])
                                   for k in range(KC)]).then_inc(s_done, 1)
                pe.wait_ge(pT_ready, j * CT + CT)
                for g, (a, b) in enumerate(TURNS):
                    pe.wait_ge(p_ready, j * 3 + (1, 1, 2)[g])
                    for n in range(a, b):
                        last = pe.transpose(ps_t[g % 2][0:M, n - a, :], pT[:, n * M:(n + 1) * M], ident[:, :])
                    last.then_inc(turned, 1)
                pe.wait_ge(p_ready, j * 3 + 4)
                for t in range(CT):
                    for a in range(NT):
                        pe.matmul(ps_n[t][:, 0:CW], p_hi[0:M, a, :], adj[0:M, a, cols(t)],
                                  start=(a == 0), stop=False)
                        last = pe.matmul(ps_n[t][:, 0:CW], p_lo[0:M, a, :], adj[0:M, a, cols(t)],
                                         start=False, stop=(a == NT - 1))
                    last.then_inc(agg_done, 1)

            with pe.Fori(0, KC) as j:
                chunk(j)


HEADS, HD, NF = 16, 64, 256
HP = HEADS // 2
VW = HD + 2
PAIR = 2 * M
STEPS = NT // 2
EPS_Z = 1e-6


def stage_attention(nc, w_qkv, proj, xT_hi, xT_lo, ident, oT_hi_dram, oT_lo_dram):
    with ExitStack() as stack:
        m = Pool(nc, stack, "att")
        raw = {n: m.sb(f"raw_{n}", [P, KC, P], F32) for n in "qkv"}
        w_hi = {n: m.sb(f"w{n}_hi", [P, KC, P], F32R) for n in "qkv"}
        w_lo = {n: m.sb(f"w{n}_lo", [P, KC, P], F32R) for n in "qkv"}
        t_hi = {n: m.sb(f"{n}T_hi", [P, NP], F32R) for n in "qk"}
        t_lo = {n: m.sb(f"{n}T_lo", [P, NP], F32R) for n in "qk"}
        vT = m.sb("vT", [P, NP], F32)
        v_hi = m.sb("v_hi", [P, NT, 2, VW], F32R)
        v_lo = m.sb("v_lo", [P, NT, 2, VW], F32R)
        raw_p = m.sb("raw_p", [P, NF], F32)
        pj_hi = m.sb("pj_hi", [P, 2 * NF], F32R)
        pj_lo = m.sb("pj_lo", [P, 2 * NF], F32R)
        neg_max = m.sb("neg_max", [P, 2, 2], F32)
        feat = m.sb("feat", [P, 2, 2 * NF], F32)
        k_hi = m.sb("k_hi", [P, 2, 2 * NF], F32R)
        k_lo = m.sb("k_lo", [P, 2, 2 * NF], F32R)
        qf_hi = m.sb("qf_hi", [P, 2, 4, PAIR], F32R)
        qf_lo = m.sb("qf_lo", [P, 2, 4, PAIR], F32R)
        kv_hi = m.sb("kv_hi", [P, 4, P], F32R)
        kv_lo = m.sb("kv_lo", [P, 4, P], F32R)
        den = m.sb("den", [P, PAIR], F32)
        att = m.sb("att", [P, PAIR], F32)
        att_hi = m.sb("att_hi", [P, PAIR], F32R)
        att_lo = m.sb("att_lo", [P, PAIR], F32R)
        ps_g = [m.psum(f"ps_g{i}", [P, BANK]) for i in range(2)]
        ps_z = [m.psum(f"ps_z{i}", [P, BANK]) for i in range(2)]
        ps_t = [m.psum(f"ps_t{i}", [P, BANK]) for i in range(2)]
        ps_kv = m.psum("ps_kv", [P, BANK])
        ps_o = m.psum("ps_o", [P, BANK])
        raw_in = {n: m.sem(f"raw_{n}_in") for n in "qkvp"}
        w_hi_ready = {n: m.sem(f"w{n}_hi_ready") for n in "qkv"}
        w_ready = {n: m.sem(f"w{n}_ready") for n in "qkv"}
        pj_hi_ready = m.sem("pj_hi_ready")
        pj_ready = m.sem("pj_ready")
        g_done = {n: m.sem(f"{n}_done") for n in "qkv"}
        t_hi_ready = {n: m.sem(f"{n}T_hi_ready") for n in "qk"}
        t_ready = {n: m.sem(f"{n}T_ready") for n in "qkv"}
        z_done = m.sem("z_done")
        max_ready = m.sem("max_ready")
        feat_ready = m.sem("feat_ready")
        k_hi_ready = m.sem("k_hi_ready")
        k_ready = m.sem("k_ready")
        kv_added = m.sem("kv_added")
        kv_hi_ready = m.sem("kv_hi_ready")
        kv_ready = m.sem("kv_ready")
        q_turned = m.sem("q_turned")
        qf_hi_ready = m.sem("qf_hi_ready")
        qf_ready = m.sem("qf_ready")
        v_turned = m.sem("v_turned")
        v_hi_ready = m.sem("v_hi_ready")
        v_ready = m.sem("v_ready")
        out_done = m.sem("out_done")
        den_ready = m.sem("den_ready")
        inv_ready = m.sem("inv_ready")
        att_ready = m.sem("att_ready")
        att_hi_ready = m.sem("att_hi_ready")
        att_split = m.sem("att_split")
        att_out = m.sem("att_out")
        blank = m.sem("blank")
        held = m.sem("held")
        block = stack.enter_context(nc.Block())
        cols = lambda t: slice(t * CW, (t + 1) * CW)
        tile = lambda t: slice(t * M, (t + 1) * M)
        half = lambda t: slice((t % 2) * M, (t % 2) * M + M)
        OFF = {"q": 0, "k": 1, "v": 2}
        BANKS = {"q": ((0, "v", 0, 3), (1, None, 0, 0), (0, "q", 0, 1)),
                 "k": ((1, "q", -1, 2), (0, "q", -1, 3), (1, "k", 0, 1)),
                 "v": ((0, "k", 0, 2), (1, "k", 0, 3), (0, "v", 0, 1))}

        @block.sync
        def _(sp):
            def load_w(n, hp):
                sp.dma_start(raw[n][:, :, :], panel(w_qkv[:, OFF[n] * D:(OFF[n] + 1) * D], hp)).then_inc(raw_in[n], 16)

            def load_p(hp):
                sp.dma_start(raw_p[:, :], proj[ds(hp * 2, 2), :, :].rearrange("h d f -> (h d) f")).then_inc(raw_in["p"], 16)

            def pair(hp, after_next, last=False):
                if not last:
                    sp.wait_ge(w_ready["q"], hp + 1)
                    load_w("q", hp + 1)
                    sp.wait_ge(pj_ready, hp * 2 + 2)
                    load_p(hp + 1)
                    for n in "kv":
                        sp.wait_ge(w_ready[n], hp + 2)
                        load_w(n, after_next)
                for s in range(STEPS):
                    sp.wait_ge(att_split, hp * STEPS + (s + 2))
                    sp.dma_start(oT_hi_dram[ds(hp * P, P), s * PAIR:(s + 1) * PAIR], att_hi[:, :].bitcast(F32)).then_inc(att_out, 16)
                    sp.dma_start(oT_lo_dram[ds(hp * P, P), s * PAIR:(s + 1) * PAIR], att_lo[:, :].bitcast(F32)).then_inc(att_out, 16)

            for n in "kvq":
                load_w(n, 0)
            load_p(0)
            for n in "kv":
                sp.wait_ge(w_ready[n], 1)
                load_w(n, 1)
            with sp.Fori(0, HP - 2) as hp:
                pair(hp, hp + 2)
            pair(HP - 2, HP - 1)
            pair(HP - 1, None, last=True)
            sp.wait_ge(att_out, 32 * HP * STEPS + 32)

        @block.gpsimd
        def _(pool):
            def split_w(n, hp):
                pool.wait_ge(raw_in[n], hp * 16 + 16)
                pool.sem_inc(held, 1)
                nc.gpsimd.tensor_copy(w_hi[n][:, :, :], raw[n][:, :, :]).then_inc(w_hi_ready[n], 1)

            def split_att(hp, s):
                pool.wait_ge(att_ready, hp * STEPS + (s + 2))
                pool.wait_ge(att_out, hp * (32 * STEPS) + 32 * (s + 1))
                pool.sem_inc(held, 1)
                nc.gpsimd.tensor_copy(att_hi[:, :], att[:, :]).then_inc(att_hi_ready, 1)
                pool.wait_ge(att_hi_ready, hp * STEPS + (s + 1))
                nc.gpsimd.tensor_tensor(att_lo[:, :], att[:, :], att_hi[:, :].bitcast(F32),
                                        ALU.subtract).then_inc(att_split, 1)

            def pair(hp, last=False):
                for t in range(NT):
                    pool.wait_ge(feat_ready, hp * (2 * NT) + (t + 3))
                    pool.wait_ge(kv_added, hp * NT + (t + 1))
                    pool.sem_inc(held, 1)
                    nc.gpsimd.tensor_copy(k_hi[0:M, t % 2, :], feat[0:M, t % 2, :]).then_inc(k_hi_ready, 1)
                for s in range(1, STEPS):
                    if not last and s == 1:
                        pool.wait_ge(g_done["q"], hp * CT + CT)
                        split_w("q", hp + 1)
                    if not last and s == 3:
                        pool.wait_ge(g_done["k"], hp * CT + 2 * CT)
                        split_w("k", hp + 2)
                    split_att(hp, s - 1)
                if not last:
                    pool.wait_ge(g_done["v"], hp * CT + 2 * CT)
                    split_w("v", hp + 2)
                split_att(hp, STEPS - 1)

            pool.sem_inc(att_split, 1)
            pool.sem_inc(att_out, 32)
            for n in "kvq":
                split_w(n, 0)
            for n in "kv":
                pool.wait_ge(g_done[n], CT)
                split_w(n, 1)
            with pool.Fori(0, HP - 1) as hp:
                pair(hp)
            pair(HP - 1, last=True)

        @block.scalar
        def _(act):
            def keep(n, hp, t):
                act.wait_ge(g_done[n], hp * CT + (t + 1))
                src = ps_g[BANKS[n][t][0]][:, 0:CW]
                if n == "v":
                    nc.scalar.copy(vT[:, cols(t)], src).then_inc(t_ready["v"], 1)
                else:
                    nc.scalar.copy(t_hi[n][:, cols(t)], src).then_inc(t_hi_ready[n], 1)

            def features(hp, t, i):
                act.wait_ge(max_ready, hp * (2 * NT) + (i + 1))
                if i < NT:
                    act.wait_ge(k_ready, hp * NT + (t + 1))
                    if t < 2:
                        act.wait_ge(q_turned, hp * NT + 2)
                else:
                    act.wait_ge(q_turned, hp * NT + (t + 1))
                    if t < 2:
                        act.wait_ge(k_ready, hp * NT + (NT + 2))
                for h in range(2):
                    last = nc.scalar.activation(feat[0:M, t % 2, h * NF:(h + 1) * NF],
                                                ps_z[t % 2][0:M, h * NF:(h + 1) * NF], ACT.Exp,
                                                bias=neg_max[0:M, t % 2, h:h + 1])
                last.then_inc(feat_ready, 1)

            def split_p(hp):
                act.wait_ge(raw_in["p"], hp * 16 + 16)
                for h in range(2):
                    r = slice(h * HD, (h + 1) * HD)
                    nc.scalar.copy(pj_hi[r, h * NF:(h + 1) * NF], raw_p[r, :]).then_inc(pj_hi_ready, 1)

            def keep_kv(hp):
                act.wait_ge(kv_added, hp * NT + (NT + 2))
                kv = ps_kv[:, 0:4 * VW].rearrange("p (c w) -> p c w", w=VW)
                for h in range(2):
                    here, there = slice(h * HD, (h + 1) * HD), slice((1 - h) * HD, (2 - h) * HD)
                    nc.scalar.copy(kv_hi[:, 2 * h:2 * h + 2, here], kv[:, 2 * h:2 * h + 2, 0:HD])
                    last = nc.scalar.copy(kv_hi[:, 2 * h:2 * h + 2, there],
                                          kv[:, 2 * h:2 * h + 2, HD:HD + 1].to_broadcast([P, 2, HD]))
                last.then_inc(kv_hi_ready, 1)

            def keep_turned(hp, t):
                act.wait_ge(q_turned, hp * NT + (t + 3))
                s = t // 2
                act.wait_ge(out_done, hp * STEPS + max(s, 1))
                nc.scalar.copy(qf_hi[:, s % 2, :, half(t)], ps_t[t % 2][:, 0:4 * M].rearrange("p (c n) -> p c n", n=M)
                               ).then_inc(qf_hi_ready, 1)

            def keep_v(hp):
                for g, (a, b) in enumerate(TURNS):
                    act.wait_ge(v_turned, hp * 3 + (g + 1))
                    nc.scalar.copy(v_hi[0:M, a:b, :, 0:HD],
                                   ps_t[g % 2][0:M, 0:(b - a) * P].rearrange("p (a h d) -> p a h d", h=2, d=HD)
                                   ).then_inc(v_hi_ready, 1)

            def denominators(hp, s):
                act.wait_ge(out_done, hp * STEPS + (s + 2))
                nc.scalar.activation(den[0:HD, :], ps_o[HD:P, 0:PAIR], ACT.Copy, bias=EPS_Z)
                nc.scalar.activation(den[HD:P, :], ps_o[0:HD, PAIR:2 * PAIR], ACT.Copy,
                                     bias=EPS_Z).then_inc(den_ready, 1)

            def pair(hp, last=False):
                for s in range(STEPS):
                    features(hp, 2 * s, 2 * s)
                    features(hp, 2 * s + 1, 2 * s + 1)
                    for t in {1: (0,), 3: (1,), 4: (2,)}.get(s, ()):
                        keep("q", hp, t)
                for s in range(STEPS):
                    features(hp, 2 * s, NT + 2 * s)
                    features(hp, 2 * s + 1, NT + 2 * s + 1)
                    if s == 0:
                        keep_kv(hp)
                    else:
                        keep_turned(hp, 2 * s - 2)
                        keep_turned(hp, 2 * s - 1)
                    if not last:
                        for n, t in {0: (("k", 0),), 1: (("k", 1),), 2: (("k", 2),), 3: (("v", 0), ("v", 1)),
                                     4: (("v", 2),)}[s]:
                            keep(n, hp + 1, t)
                    if s:
                        denominators(hp, s - 1)
                keep_turned(hp, NT - 2)
                keep_turned(hp, NT - 1)
                if not last:
                    act.wait_ge(z_done, hp * (2 * NT) + 2 * NT)
                    split_p(hp + 1)
                    keep_v(hp + 1)
                denominators(hp, STEPS - 1)

            act.wait_ge(blank, 4)
            split_p(0)
            for n in "kv":
                for t in range(CT):
                    keep(n, 0, t)
            keep_v(0)
            with act.Fori(0, HP - 1) as hp:
                pair(hp)
            pair(HP - 1, last=True)

        @block.vector
        def _(dve):
            def split_w(n, hp):
                dve.wait_ge(w_hi_ready[n], hp + 1)
                nc.vector.tensor_tensor(w_lo[n][:, :, :], raw[n][:, :, :], w_hi[n][:, :, :].bitcast(F32),
                                        ALU.subtract).then_inc(w_ready[n], 1)

            def keep(n, hp, t):
                dve.wait_ge(t_hi_ready[n], hp * CT + (t + 1))
                nc.vector.tensor_tensor(t_lo[n][:, cols(t)], ps_g[BANKS[n][t][0]][:, 0:CW],
                                        t_hi[n][:, cols(t)].bitcast(F32), ALU.subtract).then_inc(t_ready[n], 1)

            def maximum(hp, t, i):
                dve.wait_ge(z_done, hp * (2 * NT) + (i + 1))
                nc.vector.tensor_reduce(neg_max[0:M, t % 2, :], ps_z[t % 2][0:M, :].rearrange("p (h f) -> p h f", h=2),
                                        AX_X, ALU.max, negate=True).then_inc(max_ready, 1)

            def split_k(hp, t):
                dve.wait_ge(k_hi_ready, hp * NT + (t + 1))
                nc.vector.tensor_tensor(k_lo[0:M, t % 2, :], feat[0:M, t % 2, :], k_hi[0:M, t % 2, :].bitcast(F32),
                                        ALU.subtract).then_inc(k_ready, 1)

            def split_p(hp):
                dve.wait_ge(pj_hi_ready, hp * 2 + 2)
                for h in range(2):
                    r = slice(h * HD, (h + 1) * HD)
                    nc.vector.tensor_tensor(pj_lo[r, h * NF:(h + 1) * NF], raw_p[r, :],
                                            pj_hi[r, h * NF:(h + 1) * NF].bitcast(F32),
                                            ALU.subtract).then_inc(pj_ready, 1)

            def keep_kv(hp):
                dve.wait_ge(kv_hi_ready, hp + 1)
                kv = ps_kv[:, 0:4 * VW].rearrange("p (c w) -> p c w", w=VW)
                for h in range(2):
                    here, there = slice(h * HD, (h + 1) * HD), slice((1 - h) * HD, (2 - h) * HD)
                    nc.vector.tensor_tensor(kv_lo[:, 2 * h:2 * h + 2, here], kv[:, 2 * h:2 * h + 2, 0:HD],
                                            kv_hi[:, 2 * h:2 * h + 2, here].bitcast(F32), ALU.subtract)
                    last = nc.vector.tensor_tensor(kv_lo[:, 2 * h:2 * h + 2, there],
                                                   kv[:, 2 * h:2 * h + 2, HD:HD + 1].to_broadcast([P, 2, HD]),
                                                   kv_hi[:, 2 * h:2 * h + 2, there].bitcast(F32), ALU.subtract)
                last.then_inc(kv_ready, 1)

            def keep_turned(hp, t):
                dve.wait_ge(qf_hi_ready, hp * NT + (t + 1))
                s = t // 2
                nc.vector.tensor_tensor(qf_lo[:, s % 2, :, half(t)], ps_t[t % 2][:, 0:4 * M].rearrange("p (c n) -> p c n", n=M),
                                        qf_hi[:, s % 2, :, half(t)].bitcast(F32), ALU.subtract).then_inc(qf_ready, 1)

            def keep_v(hp):
                for g, (a, b) in enumerate(TURNS):
                    dve.wait_ge(v_hi_ready, hp * 3 + (g + 1))
                    nc.vector.tensor_tensor(v_lo[0:M, a:b, :, 0:HD],
                                            ps_t[g % 2][0:M, 0:(b - a) * P].rearrange("p (a h d) -> p a h d", h=2, d=HD),
                                            v_hi[0:M, a:b, :, 0:HD].bitcast(F32), ALU.subtract).then_inc(v_ready, 1)

            def divide(hp, s):
                dve.wait_ge(den_ready, hp * STEPS + (s + 1))
                nc.vector.reciprocal(den[:, :], den[:, :]).then_inc(inv_ready, 1)
                dve.wait_ge(inv_ready, hp * STEPS + (s + 1))
                dve.wait_ge(att_split, hp * STEPS + (s + 1))
                nc.vector.tensor_tensor(att[0:HD, :], ps_o[0:HD, 0:PAIR], den[0:HD, :], ALU.mult)
                nc.vector.tensor_tensor(att[HD:P, :], ps_o[HD:P, PAIR:2 * PAIR], den[HD:P, :],
                                        ALU.mult).then_inc(att_ready, 1)

            def pair(hp, last=False):
                for s in range(STEPS):
                    maximum(hp, 2 * s, 2 * s)
                    maximum(hp, 2 * s + 1, 2 * s + 1)
                    split_k(hp, 2 * s)
                    split_k(hp, 2 * s + 1)
                    for t in {1: (0,), 3: (1,), 4: (2,)}.get(s, ()):
                        keep("q", hp, t)
                for s in range(STEPS):
                    maximum(hp, 2 * s, NT + 2 * s)
                    maximum(hp, 2 * s + 1, NT + 2 * s + 1)
                    if s == 0:
                        keep_kv(hp)
                    else:
                        keep_turned(hp, 2 * s - 2)
                        keep_turned(hp, 2 * s - 1)
                    if not last:
                        if s < CT:
                            keep("k", hp + 1, s)
                        if s == 1:
                            split_w("q", hp + 1)
                        if s == 3:
                            split_w("k", hp + 2)
                    if s:
                        divide(hp, s - 1)
                keep_turned(hp, NT - 2)
                keep_turned(hp, NT - 1)
                if not last:
                    split_p(hp + 1)
                    keep_v(hp + 1)
                divide(hp, STEPS - 1)
                if not last:
                    split_w("v", hp + 2)

            for t, to in ((pj_hi, 0.0), (pj_lo, 0.0)):
                nc.vector.memset(t[:, :].bitcast(F32), to).then_inc(blank, 1)
            nc.vector.memset(v_hi[:, :, :, HD:HD + 1].bitcast(F32), 1.0)
            nc.vector.memset(v_hi[:, :, :, HD + 1:VW].bitcast(F32), 0.0).then_inc(blank, 1)
            nc.vector.memset(v_lo[:, :, :, HD:VW].bitcast(F32), 0.0).then_inc(blank, 1)
            dve.sem_inc(k_ready, 2)
            dve.sem_inc(kv_ready, 1)
            dve.sem_inc(att_ready, 1)
            for n in "kvq":
                split_w(n, 0)
            split_p(0)
            for t in range(CT):
                keep("k", 0, t)
            keep_v(0)
            for n in "kv":
                split_w(n, 1)
            with dve.Fori(0, HP - 1) as hp:
                pair(hp)
            pair(HP - 1, last=True)

        @block.tensor
        def _(pe):
            def gemm(n, hp, first, count, start_up=False):
                for u in range(first, first + count):
                    t, k = divmod(u, KC)
                    bank, whose, ahead, c = BANKS[n][t]
                    if u == 0:
                        pe.wait_ge(w_ready[n], hp + 1)
                    if k == 0 and whose and not (start_up and whose == "q"):
                        pe.wait_ge(t_ready[whose], hp * CT + (ahead * CT + c))
                    out = ps_g[bank][:, 0:CW]
                    pe.matmul(out, w_hi[n][:, k, :], xT_hi[:, k, cols(t)], start=(k == 0), stop=False)
                    pe.matmul(out, w_hi[n][:, k, :], xT_lo[:, k, cols(t)], start=False, stop=False)
                    last = pe.matmul(out, w_lo[n][:, k, :], xT_hi[:, k, cols(t)], start=False, stop=(k == KC - 1))
                    if k == KC - 1:
                        last.then_inc(g_done[n], 1)

            def project(n, hp, t, i):
                pe.wait_ge(feat_ready, hp * (2 * NT) + (i + 1))
                if t % 4 == 0 or t == NT - 1:
                    pe.wait_ge(t_ready[n], hp * CT + min(CT, ((t + 4) * M - 1) // CW + 1))
                exact_product(pe, ps_z[t % 2][0:M, :],
                              [(t_hi[n][:, tile(t)], t_lo[n][:, tile(t)], pj_hi[:, :], pj_lo[:, :])]
                              ).then_inc(z_done, 1)

            def add_kv(hp, t):
                pe.wait_ge(k_ready, hp * NT + (t + 3))
                for h in range(2):
                    for c in range(2):
                        f = 2 * h + c
                        at = slice(f * P, (f + 1) * P)
                        out = ps_kv[:, f * VW:(f + 1) * VW]
                        for n, (l, r) in enumerate(((k_hi, v_hi), (k_hi, v_lo), (k_lo, v_hi))):
                            last = pe.matmul(out, l[0:M, t % 2, at], r[0:M, t, h, :],
                                             start=(t == 0 and f == 0 and n == 0), stop=(t == NT - 1 and n == 2),
                                             skip_group_check=True)
                last.then_inc(kv_added, 1)

            def turn_q(hp, t):
                pe.wait_ge(feat_ready, hp * (2 * NT) + (NT + t + 3))
                if t >= 2:
                    pe.wait_ge(qf_ready, hp * NT + (t - 1))
                else:
                    pe.wait_ge(v_ready, hp * 3 + 3)
                for f in range(4):
                    last = pe.transpose(ps_t[t % 2][:, f * M:(f + 1) * M], feat[0:M, t % 2, f * P:(f + 1) * P],
                                        ident[0:M, 0:M])
                last.then_inc(q_turned, 1)

            def turn_v(hp, start_up=False):
                pe.wait_ge(t_ready["v"], hp * CT + CT)
                for g, (a, b) in enumerate(TURNS):
                    if g == 2:
                        pe.wait_ge(v_ready, hp * 3 + 1)
                    elif not start_up:
                        pe.wait_ge(qf_ready, hp * NT + (g - 1))
                    for n in range(a, b):
                        last = pe.transpose(ps_t[g % 2][0:M, (n - a) * P:(n - a + 1) * P], vT[:, tile(n)], ident[:, :])
                    last.then_inc(v_turned, 1)

            def multiply(hp, s):
                pe.wait_ge(qf_ready, hp * NT + (2 * s + 2))
                if s == 0:
                    pe.wait_ge(kv_ready, hp + 2)
                pe.wait_ge(att_ready, hp * STEPS + (s + 1))
                for h in range(2):
                    last = exact_product(pe, ps_o[:, h * PAIR:(h + 1) * PAIR],
                                         [(kv_hi[:, f, :], kv_lo[:, f, :], qf_hi[:, s % 2, f, :], qf_lo[:, s % 2, f, :])
                                          for f in (2 * h, 2 * h + 1)])
                last.then_inc(out_done, 1)

            def pair(hp, last=False):
                for s in range(STEPS):
                    if s == 0:
                        pe.wait_ge(pj_ready, hp * 2 + 2)
                    project("k", hp, 2 * s, 2 * s)
                    project("k", hp, 2 * s + 1, 2 * s + 1)
                    gemm("q", hp, 5 * s, min(5, CT * KC - 5 * s))
                    if s == 0:
                        pe.wait_ge(v_ready, hp * 3 + 3)
                        pe.wait_ge(kv_ready, hp + 1)
                    else:
                        add_kv(hp, 2 * s - 2)
                        add_kv(hp, 2 * s - 1)
                units = [("k", u) for u in range(CT * KC)] + [("v", u) for u in range(CT * KC)]

                def ahead(first):
                    if not last:
                        for n, u in units[first:first + 5]:
                            gemm(n, hp + 1, u, 1)

                for s in range(STEPS):
                    project("q", hp, 2 * s, NT + 2 * s)
                    project("q", hp, 2 * s + 1, NT + 2 * s + 1)
                    ahead(10 * s)
                    if s == 0:
                        add_kv(hp, NT - 2)
                        add_kv(hp, NT - 1)
                    else:
                        turn_q(hp, 2 * s - 2)
                        turn_q(hp, 2 * s - 1)
                    ahead(10 * s + 5)
                    if s:
                        multiply(hp, s - 1)
                turn_q(hp, NT - 2)
                turn_q(hp, NT - 1)
                if not last:
                    turn_v(hp + 1)
                multiply(hp, STEPS - 1)

            pe.sem_inc(feat_ready, 2)
            pe.sem_inc(kv_added, 2)
            pe.sem_inc(q_turned, 2)
            pe.sem_inc(out_done, 1)
            pe.wait_ge(blank, 4)
            gemm("k", 0, 0, CT * KC, start_up=True)
            gemm("v", 0, 0, CT * KC, start_up=True)
            turn_v(0, start_up=True)
            with pe.Fori(0, HP - 1) as hp:
                pair(hp)
            pair(HP - 1, last=True)


PW = 256
HID = 512
HC = HID // P
EPS_Q = 1e-5


def chained(engine, sem):
    count = [0]

    def link(ins):
        count[0] += 1
        ins.then_inc(sem, 1)
        engine.wait_ge(sem, count[0])

    return link


def stage_ternary(nc, w1, w2, ident_b, ones_r, w1T, w2T, unit):
    with ExitStack() as stack:
        m = Pool(nc, stack, "tern")
        raw = [m.sb("raw1", [P, HC * D], F32), m.sb("raw2", [P, HC * D], F32)]
        tern = [m.sb("tern1", [P, HC * D], BF16), m.sb("tern2", [P, HC * D], BF16)]
        total = m.sb("total", [P, 2], F32)
        scale = m.sb("scale", [P, 2], F32)
        ps_sum = m.bank("ps_sum")
        ps_t = [m.psum(f"ps_t{i}", [P, 2 * BANK], BF16) for i in range(4)]
        raw_in = [m.sem("raw1_in"), m.sem("raw2_in")]
        summed = m.sem("summed")
        total_ready = m.sem("total_ready")
        tern_ready = m.sem("tern_ready")
        turned = m.sem("turned")
        kept = m.sem("kept")
        chain = m.sem("chain")
        block = stack.enter_context(nc.Block())
        JOBS = [(0, c, c * D, w1T[:, :, c * P:(c + 1) * P]) for c in range(HC)]
        JOBS += [(1, c, c * HID, w2T[:, :, c * P:(c + 2) * P]) for c in range(0, KC, 2)]

        @block.sync
        def _(sp):
            sp.dma_start(raw[0][:, :].rearrange("p (c k) -> p c k", k=D), w1.rearrange("(c p) k -> p c k", p=P)).then_inc(raw_in[0], 16)
            sp.dma_start(raw[1][:, :].rearrange("p (c k) -> p c k", k=HID), w2.rearrange("(c p) k -> p c k", p=P)).then_inc(raw_in[1], 16)

        @block.vector
        def _(dve):
            link = chained(dve, chain)
            for i in range(2):
                dve.wait_ge(raw_in[i], 16)
                nc.vector.tensor_reduce(total[:, i:i + 1], raw[i][:, :], AX_X, ALU.add,
                                        apply_absolute_value=True).then_inc(total_ready, 1)
            dve.wait_ge(summed, 1)
            link(nc.vector.tensor_scalar(unit[:, :], ps_sum[:, 0:2], 1.0 / (HID * D), EPS_Q, ALU.mult, ALU.max))
            link(nc.vector.reciprocal(scale[:, :], unit[:, :]))
            for i in range(2):
                link(nc.vector.tensor_scalar(raw[i][:, :], raw[i][:, :], scale[:, i:i + 1], ROUND, ALU.mult, ALU.add))
                link(nc.vector.tensor_scalar(raw[i][:, :], raw[i][:, :], ROUND, 1.0, ALU.subtract, ALU.min))
                nc.vector.tensor_scalar(tern[i][:, :], raw[i][:, :], -1.0, None, ALU.max).then_inc(tern_ready, 1)

        @block.tensor
        def _(pe):
            pe.wait_ge(total_ready, 2)
            nc.tensor.matmul(ps_sum[:, 0:2], ones_r[:, :].bitcast(F32), total[:, :], start=True, stop=True).then_inc(summed, 1)
            for n, (i, c, at, _) in enumerate(JOBS):
                pe.wait_ge(tern_ready, i + 1)
                if n >= 4:
                    pe.wait_ge(kept, n - 3)
                for u in range(8):
                    col = u if i == 0 else (u % HC) * 2 + u // HC
                    last = nc.tensor.transpose(ps_t[n % 4][:, col * P:(col + 1) * P],
                                               tern[i][:, at + u * P:at + (u + 1) * P], ident_b[:, :])
                last.then_inc(turned, 1)

        @block.scalar
        def _(act):
            for n, (i, _, _, to) in enumerate(JOBS):
                act.wait_ge(turned, n + 1)
                nc.scalar.copy(to, ps_t[n % 4][:, :].rearrange("p (c n) -> p c n", c=(KC, HC)[i])).then_inc(kept, 1)


def stage_sage1(nc, w_neigh, w_self, hT_hi_dram, hT_lo_dram, adj, inv_col, mid_dram):
    with ExitStack() as stack:
        m = Pool(nc, stack, "sage1")
        hT_hi = m.sb("hT_hi", [P, KC, N], F32R)
        hT_lo = m.sb("hT_lo", [P, KC, N], F32R)
        raw = {n: m.sb(f"raw_{n}", [P, KC, PW], F32) for n in "ns"}
        w_hi = {n: m.sb(f"w{n}_hi", [P, KC, PW], F32R) for n in "ns"}
        w_lo = {n: m.sb(f"w{n}_lo", [P, KC, PW], F32R) for n in "ns"}
        p_hi = m.sb("p_hi", [P, NT, PW], F32R)
        p_lo = m.sb("p_lo", [P, NT, PW], F32R)
        mean = m.sb("mean", [P, 2, PW], F32)
        mid = m.sb("mid", [P, 2, PW], F32)
        ps_p = [m.bank(f"ps_p{i}") for i in range(2)]
        ps_a = [m.bank(f"ps_a{i}") for i in range(2)]
        ps_s = [m.bank(f"ps_s{i}") for i in range(2)]
        h_in = m.sem("h_in")
        raw_in = {n: m.sem(f"raw_{n}_in") for n in "ns"}
        w_hi_ready = {n: m.sem(f"w{n}_hi_ready") for n in "ns"}
        w_ready = {n: m.sem(f"w{n}_ready") for n in "ns"}
        p_done = m.sem("p_done")
        p_hi_ready = m.sem("p_hi_ready")
        p_ready = m.sem("p_ready")
        agg_done = m.sem("agg_done")
        self_done = m.sem("self_done")
        mean_ready = m.sem("mean_ready")
        mid_ready = m.sem("mid_ready")
        mid_out = [m.sem(f"mid_out{i}") for i in range(2)]
        block = stack.enter_context(nc.Block())
        NPAN = D // PW
        tile = lambda t: slice(t * M, (t + 1) * M)

        @block.sync
        def _(sp):
            def load_w(n, j):
                sp.dma_start(raw[n][:, :, :], panel(w_neigh if n == "n" else w_self, j, PW)).then_inc(raw_in[n], 16)

            load_w("n", 0)
            for k in range(KC):
                sp.dma_start(hT_hi[:, k, :].bitcast(F32), hT_hi_dram[k * P:(k + 1) * P, 0:N]).then_inc(h_in, 16)
                sp.dma_start(hT_lo[:, k, :].bitcast(F32), hT_lo_dram[k * P:(k + 1) * P, 0:N]).then_inc(h_in, 16)
            load_w("s", 0)

            def step(j, last=False):
                if not last:
                    for n in "ns":
                        sp.wait_ge(w_ready[n], j + 1)
                        load_w(n, j + 1)
                for t in range(NT):
                    sp.wait_ge(mid_ready, j * NT + (t + 3))
                    sp.dma_start(mid_dram[tile(t), ds(j * PW, PW)], mid[0:M, t % 2, :]).then_inc(mid_out[t % 2], 16)

            with sp.Fori(0, NPAN - 1) as j:
                step(j)
            step(NPAN - 1, last=True)
            for i in range(2):
                sp.wait_ge(mid_out[i], 16 * (NPAN * NT // 2 + 1))

        @block.scalar
        def _(act):
            def split_w(n, j):
                act.wait_ge(raw_in[n], j * 16 + 16)
                nc.scalar.copy(w_hi[n][:, :, :], raw[n][:, :, :]).then_inc(w_hi_ready[n], 1)

            def step(j, last=False):
                for t in range(NT):
                    act.wait_ge(p_done, j * NT + (t + 1))
                    nc.scalar.copy(p_hi[0:M, t, :], ps_p[t % 2][0:M, 0:PW]).then_inc(p_hi_ready, 1)
                if not last:
                    split_w("n", j + 1)
                for t in range(NT):
                    act.wait_ge(agg_done, j * NT + (t + 1))
                    act.wait_ge(mid_ready, j * NT + (t + 1))
                    nc.scalar.activation(mean[0:M, t % 2, :], ps_a[t % 2][0:M, 0:PW], ACT.Copy,
                                         scale=inv_col[0:M, t:t + 1]).then_inc(mean_ready, 1)
                if not last:
                    act.wait_ge(self_done, j * NT + NT)
                    split_w("s", j + 1)

            split_w("n", 0)
            split_w("s", 0)
            with act.Fori(0, NPAN - 1) as j:
                step(j)
            step(NPAN - 1, last=True)

        @block.vector
        def _(dve):
            def split_w(n, j):
                dve.wait_ge(w_hi_ready[n], j + 1)
                nc.vector.tensor_tensor(w_lo[n][:, :, :], raw[n][:, :, :], w_hi[n][:, :, :].bitcast(F32),
                                        ALU.subtract).then_inc(w_ready[n], 1)

            def step(j, last=False):
                for t in range(NT):
                    dve.wait_ge(p_hi_ready, j * NT + (t + 1))
                    nc.vector.tensor_tensor(p_lo[0:M, t, :], ps_p[t % 2][0:M, 0:PW], p_hi[0:M, t, :].bitcast(F32),
                                            ALU.subtract).then_inc(p_ready, 1)
                if not last:
                    split_w("n", j + 1)
                for t in range(NT):
                    dve.wait_ge(self_done, j * NT + (t + 1))
                    dve.wait_ge(mean_ready, j * NT + (t + 1))
                    dve.wait_ge(mid_out[t % 2], j * (16 * NT // 2) + 16 * (t // 2 + 1))
                    nc.vector.tensor_tensor(mid[0:M, t % 2, :], ps_s[t % 2][0:M, 0:PW], mean[0:M, t % 2, :],
                                            ALU.add).then_inc(mid_ready, 1)
                if not last:
                    split_w("s", j + 1)

            dve.sem_inc(p_ready, 2)
            dve.sem_inc(mid_ready, 2)
            for i in range(2):
                dve.sem_inc(mid_out[i], 16)
            split_w("n", 0)
            split_w("s", 0)
            with dve.Fori(0, NPAN - 1) as j:
                step(j)
            step(NPAN - 1, last=True)

        @block.tensor
        def _(pe):
            def dense(out, n, t):
                return exact_product(pe, out, [(hT_hi[:, k, tile(t)], hT_lo[:, k, tile(t)], w_hi[n][:, k, :],
                                                w_lo[n][:, k, :]) for k in range(KC)])

            pe.wait_ge(h_in, 32 * KC)
            with pe.Fori(0, NPAN) as j:
                pe.wait_ge(w_ready["n"], j + 1)
                for t in range(NT):
                    pe.wait_ge(p_ready, j * NT + (t + 1))
                    dense(ps_p[t % 2][0:M, 0:PW], "n", t).then_inc(p_done, 1)
                pe.wait_ge(w_ready["s"], j + 1)
                for t in range(NT):
                    pe.wait_ge(mid_ready, j * NT + (t + 1))
                    dense(ps_s[t % 2][0:M, 0:PW], "s", t).then_inc(self_done, 1)
                    if t == 0:
                        pe.wait_ge(p_ready, j * NT + (NT + 2))
                    for a in range(NT):
                        pe.matmul(ps_a[t % 2][0:M, 0:PW], adj[0:M, a, tile(t)], p_hi[0:M, a, :],
                                  start=(a == 0), stop=False)
                        last = pe.matmul(ps_a[t % 2][0:M, 0:PW], adj[0:M, a, tile(t)], p_lo[0:M, a, :],
                                         start=False, stop=(a == NT - 1))
                    last.then_inc(agg_done, 1)


PAIRS = NT // 2


def stage_mix(nc, w_out, b_graph, b_out, x, oT_hi_dram, oT_lo_dram, mid_dram, ident_b, x1_dram, qT, unit_x):
    with ExitStack() as stack:
        m = Pool(nc, stack, "mix")
        raw = m.sb("raw", [P, 2, KC, PW], F32)
        w_hi = m.sb("w_hi", [P, KC, D], F32R)
        w_lo = m.sb("w_lo", [P, KC, D], F32R)
        bias = m.sb("bias", [P, 2, D], F32)
        o_hi = m.sb("o_hi", [P, 2, KC, M], F32R)
        o_lo = m.sb("o_lo", [P, 2, KC, M], F32R)
        mid = m.sb("mid", [P, 2, D], F32)
        x_in = m.sb("x_in", [P, 2, D], F32)
        x1 = m.sb("x1", [P, 2, D], F32)
        y = m.sb("y", [P, D], F32)
        code = m.sb("code", [P, D], BF16)
        stats = m.sb("stats", [P, 2, 6], F32)
        mv = m.sb("mv", [P, 2], F32)
        rs = m.sb("rs", [P, 6], F32)
        big = m.sb("big", [P, 3], F32)
        ps_x = [m.bank(f"ps_x{i}") for i in range(4)]
        ps_t = m.psum("ps_t", [P, 2 * BANK], BF16)
        raw_in = [m.sem(f"raw_in{i}") for i in range(2)]
        bias_in = m.sem("bias_in")
        bias_ready = m.sem("bias_ready")
        w_hi_ready = m.sem("w_hi_ready")
        w_ready = m.sem("w_ready")
        o_in = [m.sem(f"o_in{b}") for b in range(2)]
        m_in = [m.sem(f"m_in{b}") for b in range(2)]
        sum_ready = m.sem("sum_ready")
        base_ready = m.sem("base_ready")
        x_done = m.sem("x_done")
        x1_ready = m.sem("x1_ready")
        x1_out = [m.sem(f"x1_out{b}") for b in range(2)]
        var_ready = m.sem("var_ready")
        root_ready = m.sem("root_ready")
        seen = m.sem("seen")
        code_ready = m.sem("code_ready")
        turned = m.sem("turned")
        kept = m.sem("kept")
        chain = m.sem("chain")
        block = stack.enter_context(nc.Block())
        NPAN = D // PW
        row = lambda v: v.rearrange("(a n) -> a n", a=1).to_broadcast([P, D])

        @block.sync
        def _(sp):
            sp.dma_start(raw[:, 0, :, :], panel(w_out, 0, PW)).then_inc(raw_in[0], 16)
            sp.dma_start(raw[:, 1, :, :], panel(w_out, 1, PW)).then_inc(raw_in[1], 16)

            def load_o(t, b):
                sp.dma_start(o_hi[:, b, :, :].bitcast(F32), oT_hi_dram[:, ds(t * M, M)].rearrange("(c p) n -> p c n", p=P)).then_inc(o_in[b], 16)
                sp.dma_start(o_lo[:, b, :, :].bitcast(F32), oT_lo_dram[:, ds(t * M, M)].rearrange("(c p) n -> p c n", p=P)).then_inc(o_in[b], 16)

            def load_m(t, b):
                sp.dma_start(mid[0:M, b, :], mid_dram[ds(t * M, M), :]).then_inc(m_in[b], 16)
                sp.dma_start(x_in[0:M, b, :], x[ds(t * M, M), :]).then_inc(m_in[b], 16)

            for b in range(2):
                load_o(b, b)
            for i, v in enumerate((b_graph, b_out)):
                sp.dma_start(bias[:, i, :], row(v)).then_inc(bias_in, 16)
            for b in range(2):
                load_m(b, b)
            for j in range(2, NPAN):
                sp.wait_ge(w_ready, j - 1)
                sp.dma_start(raw[:, j % 2, :, :], panel(w_out, j, PW)).then_inc(raw_in[j % 2], 16)

            def pair(i, last=False):
                for b in range(2):
                    sp.wait_ge(x1_ready, i * 4 + (2 * b + 6))
                    sp.dma_start(x1_dram[ds(i * (2 * M) + b * M, M), :], x1[0:M, b, :]).then_inc(x1_out[b], 16)
                    if not last:
                        load_o(i * 2 + (b + 2), b)
                        load_m(i * 2 + (b + 2), b)

            with sp.Fori(0, PAIRS - 1) as i:
                pair(i)
            pair(PAIRS - 1, last=True)
            for b in range(2):
                sp.wait_ge(x1_out[b], 16 * (PAIRS + 1))

        @block.gpsimd
        def _(pool):
            pool.wait_ge(bias_in, 32)
            nc.gpsimd.tensor_tensor(bias[:, 0, :], bias[:, 0, :], bias[:, 1, :], ALU.add).then_inc(bias_ready, 1)
            pool.wait_ge(bias_ready, 1)
            with pool.Fori(0, PAIRS) as i:
                for b in range(2):
                    pool.wait_ge(m_in[b], i * 32 + 32)
                    nc.gpsimd.tensor_tensor(mid[0:M, b, :], mid[0:M, b, :], x_in[0:M, b, :], ALU.add).then_inc(sum_ready, 1)
                    pool.wait_ge(sum_ready, i * 2 + (b + 1))
                    nc.gpsimd.tensor_tensor(mid[0:M, b, :], mid[0:M, b, :], bias[0:M, 0, :], ALU.add).then_inc(base_ready, 1)

        @block.scalar
        def _(act):
            for j in range(NPAN):
                act.wait_ge(raw_in[j % 2], 16 * (j // 2 + 1))
                nc.scalar.copy(w_hi[:, :, j * PW:(j + 1) * PW], raw[:, j % 2, :, :]).then_inc(w_hi_ready, 1)

            def root(t):
                act.wait_ge(var_ready, t + 1)
                nc.scalar.activation(rs[0:M, 1:2], rs[0:M, 0:1], ACT.Sqrt).then_inc(root_ready, 1)

            def keep(t):
                act.wait_ge(turned, t + 2)
                nc.scalar.copy(qT[:, :, ds(t * M, M)], ps_t[:, :].rearrange("p (c n) -> p c n", n=P)[:, :, 0:M]).then_inc(kept, 1)

            root(0)
            root(1)
            keep(0)
            with act.Fori(1, PAIRS) as i:
                for b in range(2):
                    root(i * 2 + b)
                    keep(i * 2 + (b - 1))
            keep(NT - 1)

        @block.vector
        def _(dve):
            for b in range(2):
                dve.sem_inc(x1_out[b], 16)
            for j in range(NPAN):
                dve.wait_ge(w_hi_ready, j + 1)
                nc.vector.tensor_tensor(w_lo[:, :, j * PW:(j + 1) * PW], raw[:, j % 2, :, :],
                                        w_hi[:, :, j * PW:(j + 1) * PW].bitcast(F32), ALU.subtract).then_inc(w_ready, 1)
            LINKS = 15
            with dve.Fori(0, PAIRS) as i:
                for b in range(2):
                    c0 = i * (2 * LINKS) + b * LINKS
                    at = [0]

                    def link(ins):
                        at[0] += 1
                        ins.then_inc(chain, 1)
                        dve.wait_ge(chain, c0 + at[0])

                    dve.wait_ge(base_ready, i * 2 + (b + 1))
                    dve.wait_ge(x1_out[b], i * 16 + 16)
                    for h in range(2):
                        dve.wait_ge(x_done, i * 4 + (2 * b + h + 1))
                        nc.vector.tensor_tensor(x1[0:M, b, h * BANK:(h + 1) * BANK], ps_x[2 * b + h][0:M, :],
                                                mid[0:M, b, h * BANK:(h + 1) * BANK], ALU.add).then_inc(x1_ready, 1)
                        dve.wait_ge(x1_ready, i * 4 + (2 * b + h + 5))
                        nc.vector.bn_stats(stats[0:M, h, :], x1[0:M, b, h * BANK:(h + 1) * BANK]).then_inc(chain, 1)
                        at[0] += 1
                    dve.wait_ge(chain, c0 + 2)
                    dve.sem_inc(seen, 1)
                    link(nc.vector.bn_aggr(mv[0:M, :], stats[0:M, :, :]))
                    nc.vector.tensor_scalar(rs[0:M, 0:1], mv[0:M, 1:2], EPS_LN, None, ALU.add).then_inc(var_ready, 1)
                    dve.wait_ge(root_ready, i * 2 + (b + 1))
                    link(nc.vector.reciprocal(rs[0:M, 2:3], rs[0:M, 1:2]))
                    link(nc.vector.tensor_tensor(rs[0:M, 3:4], rs[0:M, 2:3], rs[0:M, 2:3], ALU.mult))
                    link(nc.vector.tensor_tensor(rs[0:M, 4:5], rs[0:M, 3:4], rs[0:M, 0:1], ALU.mult))
                    link(nc.vector.tensor_scalar(rs[0:M, 4:5], rs[0:M, 4:5], -0.5, 1.5, ALU.mult, ALU.add))
                    link(nc.vector.tensor_tensor(rs[0:M, 5:6], rs[0:M, 4:5], rs[0:M, 2:3], ALU.mult))
                    link(nc.vector.tensor_scalar(y[0:M, :], x1[0:M, b, :], mv[0:M, 0:1], rs[0:M, 5:6],
                                                 ALU.subtract, ALU.mult))
                    link(nc.vector.tensor_reduce(big[0:M, 0:1], y[0:M, :], AX_X, ALU.max, apply_absolute_value=True))
                    link(nc.vector.tensor_scalar(big[0:M, 1:2], big[0:M, 0:1], EPS_Q, None, ALU.max))
                    link(nc.vector.reciprocal(big[0:M, 2:3], big[0:M, 1:2]))
                    link(nc.vector.tensor_scalar(big[0:M, 2:3], big[0:M, 2:3], 127.0, None, ALU.mult))
                    nc.vector.tensor_scalar(unit_x[0:M, ds(i * 2 + b, 1)], big[0:M, 1:2], 1.0 / 127.0, None, ALU.mult)
                    link(nc.vector.tensor_scalar(y[0:M, :], y[0:M, :], big[0:M, 2:3], ROUND, ALU.mult, ALU.add))
                    link(nc.vector.tensor_scalar(y[0:M, :], y[0:M, :], ROUND, 127.0, ALU.subtract, ALU.min))
                    dve.wait_ge(turned, i * 2 + (b + 1))
                    nc.vector.tensor_scalar(code[0:M, :], y[0:M, :], -128.0, None, ALU.max).then_inc(code_ready, 1)
                    assert at[0] == LINKS

        @block.tensor
        def _(pe):
            def products(i, b):
                pe.wait_ge(o_in[b], i * 32 + 32)
                for h in range(2):
                    pe.wait_ge(x1_ready, i * 4 + (2 * b + h + 1))
                    exact_product(pe, ps_x[2 * b + h][0:M, :],
                                  [(o_hi[:, b, k, :], o_lo[:, b, k, :], w_hi[:, k, h * BANK:(h + 1) * BANK],
                                    w_lo[:, k, h * BANK:(h + 1) * BANK]) for k in range(KC)]).then_inc(x_done, 1)

            def turn(t):
                pe.wait_ge(code_ready, t + 1)
                pe.wait_ge(kept, t + 1)
                for k in range(KC):
                    last = pe.transpose(ps_t[:, k * P:k * P + M], code[0:M, k * P:(k + 1) * P], ident_b[0:M, 0:M])
                last.then_inc(turned, 1)

            pe.sem_inc(x1_ready, 4)
            pe.sem_inc(turned, 1)
            pe.sem_inc(kept, 1)
            pe.wait_ge(w_ready, NPAN)
            products(0, 0)
            products(0, 1)
            turn(0)
            with pe.Fori(1, PAIRS) as i:
                for b in range(2):
                    products(i, b)
                    turn(i * 2 + (b - 1))
            turn(NT - 1)


def stage_ffn(nc, conv_w, conv_b, x1_dram, out, ident, ident_b, w1T, w2T, unit_w, qT, unit_x):
    with ExitStack() as stack:
        m = Pool(nc, stack, "ffn")
        cw = m.sb("cw", [P, HC, 3], F32)
        cb = m.sb("cb", [P, HC], F32)
        x1 = m.sb("x1", [P, NT, D], F32)
        step_x = m.sb("step_x", [P, NT], F32)
        step_row = m.sb("step_row", [P, N], F32)
        h = m.sb("h", [P, HC, N + 2], F32)
        mixed = m.sb("mixed", [P, 2, N], F32)
        s = m.sb("s", [P, HC, N], F32)
        big = m.sb("big", [P, 2, 4], F32)
        y = m.sb("y", [P, 2, HID], F32)
        code = m.sb("code", [P, 2, HID], BF16)
        codeT = m.sb("codeT", [P, 2, HC, M], BF16)
        res = m.sb("res", [P, 2, D], F32)
        ps_h = [m.bank(f"ps_h{i}") for i in range(CT)]
        ps_s = [m.bank(f"ps_s{i}") for i in range(2)]
        ps_c = m.psum("ps_c", [P, 2 * BANK], BF16)
        ps_o = [m.bank(f"ps_o{i}") for i in range(2)]
        w_in = m.sem("w_in")
        x1_in = m.sem("x1_in")
        step_ready = m.sem("step_ready")
        spread = m.sem("spread")
        row_ready = m.sem("row_ready")
        edge_ready = m.sem("edge_ready")
        h_done = m.sem("h_done")
        h_ready = m.sem("h_ready")
        mid_ready = m.sem("mid_ready")
        conv_ready = m.sem("conv_ready")
        s_ready = m.sem("s_ready")
        s_turned = m.sem("s_turned")
        scale_ready = m.sem("scale_ready")
        y_ready = m.sem("y_ready")
        code_ready = m.sem("code_ready")
        c_turned = m.sem("c_turned")
        c_kept = m.sem("c_kept")
        o_done = m.sem("o_done")
        res_ready = m.sem("res_ready")
        res_out = [m.sem(f"res_out{b}") for b in range(2)]
        chain = m.sem("chain")
        block = stack.enter_context(nc.Block())
        WIDTH = (CW, CW, N - 2 * CW)
        cols = lambda t, off=0: slice(t * CW + off, t * CW + off + WIDTH[t])

        @block.sync
        def _(sp):
            with nc.allow_non_contiguous_dma(reason="a few words a partition"):
                sp.dma_start(cw[:, :, :], conv_w.rearrange("(c p) a w -> p c (a w)", p=P)).then_inc(w_in, 16)
                sp.dma_start(cb[:, :], conv_b.rearrange("(c p) -> p c", p=P)).then_inc(w_in, 16)
            sp.dma_start(x1[0:M, :, :], x1_dram.rearrange("(t p) d -> p t d", p=M)).then_inc(x1_in, 16)
            for t in range(NT):
                sp.wait_ge(res_ready, 2 * t + 4)
                sp.dma_start(out[t * M:(t + 1) * M, :], res[0:M, t % 2, :]).then_inc(res_out[t % 2], 16)
            for b in range(2):
                sp.wait_ge(res_out[b], 16 * (PAIRS + 1))

        @block.tensor
        def _(pe):
            pe.wait_ge(step_ready, 1)
            for t in range(NT):
                g = t // 4
                last = pe.matmul(ps_h[g][:, (t % 4) * M:(t % 4 + 1) * M], step_x[0:M, t:t + 1].to_broadcast([M, P]),
                                 ident[0:M, 0:M], start=True, stop=True)
                if t % 4 == 3 or t == NT - 1:
                    last.then_inc(spread, 1)
            for c in range(HC):
                for t in range(CT):
                    if c == 0:
                        pe.wait_ge(row_ready, t + 1)
                    else:
                        pe.wait_ge(h_ready, (c - 1) * CT + t + 1)
                    for k in range(KC):
                        last = pe.matmul(ps_h[t][:, 0:WIDTH[t]], w1T[:, k, c * P:(c + 1) * P], qT[:, k, cols(t)],
                                         start=(k == 0), stop=(k == KC - 1))
                    last.then_inc(h_done, 1)

            def turn_s(t):
                pe.wait_ge(y_ready, t + 1)
                for c in range(HC):
                    last = pe.transpose(ps_s[t % 2][0:M, c * P:(c + 1) * P], s[:, c, t * M:(t + 1) * M], ident[:, :])
                last.then_inc(s_turned, 1)

            def finish(t):
                pe.wait_ge(code_ready, t + 1)
                pe.wait_ge(c_kept, t + 1)
                for c in range(HC):
                    last = pe.transpose(ps_c[:, c * P:c * P + M], code[0:M, t % 2, c * P:(c + 1) * P],
                                        ident_b[0:M, 0:M])
                last.then_inc(c_turned, 1)
                pe.wait_ge(c_kept, t + 2)
                for half in range(2):
                    pe.wait_ge(res_ready, t * 2 + half + 1)
                    for c in range(HC):
                        last = pe.matmul(ps_o[half][0:M, :], codeT[:, t % 2, c, :], w2T[:, c, half * BANK:(half + 1) * BANK],
                                         start=(c == 0), stop=(c == HC - 1))
                    last.then_inc(o_done, 1)

            pe.wait_ge(s_ready, HC)
            turn_s(0)
            for t in range(NT):
                if t + 1 < NT:
                    turn_s(t + 1)
                finish(t)

        @block.scalar
        def _(act):
            act.sem_inc(c_kept, 1)
            act.sem_inc(y_ready, 2)

            def silu(c):
                act.wait_ge(conv_ready, c + 1)
                nc.scalar.activation(s[:, c, :], mixed[:, c % 2, :], ACT.Silu).then_inc(s_ready, 1)

            for g, (a, b) in enumerate(TURNS):
                act.wait_ge(spread, g + 1)
                nc.scalar.copy(step_row[:, a * M:b * M], ps_h[g][:, 0:(b - a) * M]).then_inc(row_ready, 1)
            act.wait_ge(w_in, 32)
            for c in range(HC):
                act.wait_ge(h_ready, (c + 1) * CT)
                if c >= 2:
                    act.wait_ge(s_ready, c - 1)
                nc.scalar.activation(mixed[:, c % 2, :], h[:, c, 1:N + 1], ACT.Identity, bias=cb[:, c:c + 1],
                                     scale=cw[:, c, 1:2]).then_inc(mid_ready, 1)
                if c >= 1:
                    silu(c - 1)
            silu(HC - 1)

            for t in range(NT + 1):
                if t < NT:
                    act.wait_ge(scale_ready, t + 1)
                    nc.scalar.activation(y[0:M, t % 2, :], ps_s[t % 2][0:M, :], ACT.Copy, bias=ROUND,
                                         scale=big[0:M, t % 2, 2:3]).then_inc(y_ready, 1)
                if t:
                    act.wait_ge(c_turned, t)
                    nc.scalar.copy(codeT[:, (t - 1) % 2, :, :],
                                   ps_c[:, 0:HC * P].rearrange("p (c n) -> p c n", n=P)[:, :, 0:M]).then_inc(c_kept, 1)

        @block.vector
        def _(dve):
            link = chained(dve, chain)
            link(nc.vector.tensor_scalar(step_x[0:M, :], unit_x[0:M, :], unit_w[0:M, 0:1], None, ALU.mult))
            dve.sem_inc(step_ready, 1)
            nc.vector.memset(h[:, :, 0:1], 0.0)
            link(nc.vector.memset(h[:, :, N + 1:N + 2], 0.0))
            dve.sem_inc(res_ready, 2)
            for b in range(2):
                dve.sem_inc(res_out[b], 16)
            dve.wait_ge(w_in, 32)
            dve.wait_ge(row_ready, CT)

            def scale_h(c):
                for t in range(CT):
                    dve.wait_ge(h_done, c * CT + t + 1)
                    nc.vector.tensor_tensor(h[:, c, cols(t, 1)], ps_h[t][:, 0:WIDTH[t]], step_row[:, cols(t)],
                                            ALU.mult).then_inc(h_ready, 1)

            def convolve(c):
                dve.wait_ge(mid_ready, c + 1)
                link(nc.vector.scalar_tensor_tensor(mixed[:, c % 2, :], h[:, c, 0:N], cw[:, c, 0:1], mixed[:, c % 2, :],
                                                    ALU.mult, ALU.add))
                nc.vector.scalar_tensor_tensor(mixed[:, c % 2, :], h[:, c, 2:N + 2], cw[:, c, 2:3], mixed[:, c % 2, :],
                                               ALU.mult, ALU.add).then_inc(conv_ready, 1)

            scale_h(0)
            for c in range(HC):
                if c + 1 < HC:
                    scale_h(c + 1)
                convolve(c)

            def scale(t):
                b = t % 2
                dve.wait_ge(s_turned, t + 1)
                link(nc.vector.tensor_reduce(big[0:M, b, 0:1], ps_s[b][0:M, :], AX_X, ALU.max,
                                             apply_absolute_value=True))
                link(nc.vector.tensor_scalar(big[0:M, b, 1:2], big[0:M, b, 0:1], EPS_Q, None, ALU.max))
                link(nc.vector.reciprocal(big[0:M, b, 2:3], big[0:M, b, 1:2]))
                nc.vector.tensor_scalar(big[0:M, b, 2:3], big[0:M, b, 2:3], 127.0, None, ALU.mult).then_inc(scale_ready, 1)
                link(nc.vector.tensor_scalar(big[0:M, b, 3:4], big[0:M, b, 1:2], unit_w[0:M, 1:2], 1.0 / 127.0,
                                             ALU.mult, ALU.mult))

            def codes(t):
                b = t % 2
                dve.wait_ge(y_ready, t + 3)
                link(nc.vector.tensor_scalar(y[0:M, b, :], y[0:M, b, :], ROUND, 127.0, ALU.subtract, ALU.min))
                nc.vector.tensor_scalar(code[0:M, b, :], y[0:M, b, :], -128.0, None, ALU.max).then_inc(code_ready, 1)

            def result(t):
                b = t % 2
                dve.wait_ge(res_out[b], 16 * (t // 2 + 1))
                for half in range(2):
                    dve.wait_ge(o_done, t * 2 + half + 1)
                    nc.vector.scalar_tensor_tensor(res[0:M, b, half * BANK:(half + 1) * BANK], ps_o[half][0:M, :],
                                                   big[0:M, b, 3:4], x1[0:M, t, half * BANK:(half + 1) * BANK],
                                                   ALU.mult, ALU.add).then_inc(res_ready, 1)

            scale(0)
            dve.wait_ge(x1_in, 16)
            for t in range(NT):
                codes(t)
                if t:
                    result(t - 1)
                if t + 1 < NT:
                    scale(t + 1)
            result(NT - 1)


def stage_move(nc, pairs, tag):
    with ExitStack() as stack:
        m = Pool(nc, stack, tag)
        moved = m.sem("moved")
        block = stack.enter_context(nc.Block())

        @block.sync
        def _(sp):
            for to, what in pairs:
                sp.dma_start(to, what).then_inc(moved, 16)
            sp.wait_ge(moved, 16 * len(pairs))


def program(nc, x, src, dst, W_self0, W_neigh0, b0, W_self1, W_neigh1, b1, w_qkv, w_out, b_out, proj,
            ffn_w1, ffn_conv_w, ffn_conv_b, ffn_w2, out):
    def dram(name, shape, dt=F32):
        return nc.dram_tensor(name, shape, dt, kind="Internal").ap()

    src_pad, dst_pad = dram("src_pad", (E + ECAP,), I32), dram("dst_pad", (E + ECAP,), I32)
    hT_hi, hT_lo = dram("hT_hi", (D, NP)), dram("hT_lo", (D, NP))
    oT_hi, oT_lo = dram("oT_hi", (D, N)), dram("oT_lo", (D, N))
    mid, x1 = dram("mid", (N, D)), dram("x1", (N, D))
    w1T_dram, w2T_dram = dram("w1T", (P, KC, HID), BF16), dram("w2T", (P, HC, D), BF16)
    with ExitStack() as stack:
        m = Pool(nc, stack, "all")
        ident = m.sb("ident", [P, P], F32)
        ident_b = m.sb("ident_b", [P, P], BF16)
        ones_r = m.sb("ones_r", [P, P], F32R)
        unit_w = m.sb("unit_w", [P, 2], F32)
        with ExitStack() as graph:
            with ExitStack() as nodes:
                m = Pool(nc, nodes, "xn")
                xT_hi = m.sb("xT_hi", [P, KC, NP], F32R)
                xT_lo = m.sb("xT_lo", [P, KC, NP], F32R)
                stage_norm(nc, x, ident, ident_b, ones_r, xT_hi, xT_lo)
                with ExitStack() as ternary:
                    m = Pool(nc, ternary, "tern_out")
                    w1T = m.sb("w1T", [P, KC, HID], BF16)
                    w2T = m.sb("w2T", [P, HC, D], BF16)
                    stage_ternary(nc, ffn_w1, ffn_w2, ident_b, ones_r, w1T, w2T, unit_w)
                    stage_move(nc, [(w1T_dram, w1T[:, :, :]), (w2T_dram, w2T[:, :, :])], "put")
                stage_attention(nc, w_qkv, proj, xT_hi, xT_lo, ident, oT_hi, oT_lo)
                m = Pool(nc, graph, "graph_out")
                adj = m.sb("adj", [P, NT, NP], F32R, side="right")
                inv_row = m.sb("inv_row", [P, NP], F32, side="right")
                inv_col = m.sb("inv_col", [P, NT], F32, side="right")
                stage_graph(nc, src, dst, src_pad, dst_pad, ident, ones_r, adj, inv_row, inv_col)
                stage_sage0(nc, W_neigh0, W_self0, b0, xT_hi, xT_lo, adj, inv_row, ident, hT_hi, hT_lo)
            stage_sage1(nc, W_neigh1, W_self1, hT_hi, hT_lo, adj, inv_col, mid)
        m = Pool(nc, stack, "codes")
        qT = m.sb("qT", [P, KC, N], BF16)
        unit_x = m.sb("unit_x", [P, NT], F32)
        w1T = m.sb("w1T", [P, KC, HID], BF16)
        w2T = m.sb("w2T", [P, HC, D], BF16)
        stage_mix(nc, w_out, b1, b_out, x, oT_hi, oT_lo, mid, ident_b, x1, qT, unit_x)
        stage_move(nc, [(w1T[:, :, :], w1T_dram), (w2T[:, :, :], w2T_dram)], "get")
        stage_ffn(nc, ffn_conv_w, ffn_conv_b, x1, out, ident, ident_b, w1T, w2T, unit_w, qT, unit_x)


INPUTS = ["x", "src", "dst", "L0_gnn_W_self0", "L0_gnn_W_neigh0", "L0_gnn_b0", "L0_gnn_W_self1", "L0_gnn_W_neigh1",
          "L0_gnn_b1", "L0_mix_w_qkv", "L0_mix_w_out", "L0_mix_b_out", "L0_mix_proj", "L0_ffn_w1", "L0_ffn_conv_w",
          "L0_ffn_conv_b", "L0_ffn_w2"]


def kernel(**inputs):
    import numpy as np
    import concourse.bacc as bacc
    from concourse.bass_utils import run_bass_kernel_spmd

    nc = bacc.Bacc("TRN2", target_bir_lowering=False, num_devices=1)
    arrays = {f"in_{name}": np.ascontiguousarray(inputs[name]) for name in INPUTS}
    args = [nc.dram_tensor(name, a.shape, mybir.dt.from_np(a.dtype), kind="ExternalInput").ap()
            for name, a in arrays.items()]
    out = nc.dram_tensor("out", (N, D), F32, kind="ExternalOutput").ap()
    program(nc, *args, out)
    run = run_bass_kernel_spmd(nc, [arrays], core_ids=[0])
    return run.results[0]["out"]
```

```python
from contextlib import ExitStack

import concourse.bass as bass
from concourse import mybir

F32 = mybir.dt.float32
F32R = mybir.dt.float32r
BF16 = mybir.dt.bfloat16
I32 = mybir.dt.int32
ALU = mybir.AluOpType
ACT = mybir.ActivationFunctionType
AX_X = mybir.AxisListType.X
ds = bass.ds

N, D, E = 1250, 1024, 20000
P = 128
M = 125
NT = N // M
KC = D // P
CT = 3
CW = 418
NP = CT * CW
BANK = 512
EPS_LN = 1e-5

TURNS = ((0, 4), (4, 8), (8, NT))
W = 25
NW = N // W
HALF_W = NW // 2 + 1
WC = NT * W
EC = 4
ECAP = EC * P
ER = E // M
GC = 8
ROUND = 12582912.0
PW = 256
HID = 512
HC = HID // P
EPS_Q = 1e-5
PAIRS = NT // 2


def chained(engine, sem):
    count = [0]

    def link(ins):
        count[0] += 1
        ins.then_inc(sem, 1)
        engine.wait_ge(sem, count[0])

    return link


class Pool:

    def __init__(self, nc, stack, tag):
        self.nc, self.stack, self.tag, self.sems = nc, stack, tag, []
        stack.callback(self.close)

    def close(self):
        if self.sems:
            self.nc.clear_and_free_semaphores(self.sems)
            self.nc.all_engine_barrier()

    def sb(self, name, shape, dt, side="left"):
        return self.stack.enter_context(self.nc.sbuf_tensor(f"{self.tag}_{name}", shape, dt, side=side))

    def psum(self, name, shape, dt=F32):
        return self.stack.enter_context(self.nc.psum_tensor(f"{self.tag}_{name}", shape, dt))

    def bank(self, name):
        return self.psum(name, [P, BANK])

    def sem(self, name):
        self.sems.append(self.nc.alloc_semaphore(name=f"{self.tag}_{name}"))
        return self.sems[-1]


def stage_prepare(nc, x, src, dst, edges_pad, w1, w2, ident, ident_b, ones_r, xT_hi, xT_lo, work, w1T_dram, w2T_dram,
                  unit):
    with ExitStack() as stack:
        m = Pool(nc, stack, "prep")
        x_all = m.sb("x_all", [P, NT, D], F32)
        stats = m.sb("stats", [P, NT, 2, 6], F32)
        mv = m.sb("mv", [P, NT, 2], F32)
        rs = m.sb("rs", [P, 7, NT], F32)
        dst_i = m.sb("dst_i", [P, ER], I32)
        next_i = m.sb("next_i", [P, 1], I32)
        next_f = m.sb("next_f", [P, 1], F32)
        pad_i = m.sb("pad_i", [1, ECAP], I32)
        below = m.sb("below", [P, HALF_W, ER], BF16)
        back = m.sb("back", [P, ER], F32)
        part = m.sb("part", [P, NW + 4], F32)
        start_f = m.sb("start_f", [P, NW + 4], F32)
        start_i = m.sb("start_i", [P, NW + 4], I32)
        load_f = m.sb("load_f", [P, NW], F32)
        flag_f = m.sb("flag_f", [P, 2], F32)
        raw = [m.sb("raw1", [P, HC * D], F32), m.sb("raw2", [P, HC * D], F32)]
        tern = [m.sb("tern1", [P, HC * D], BF16), m.sb("tern2", [P, HC * D], BF16)]
        w1T = m.sb("w1T", [P, KC, HID], BF16)
        w2T = m.sb("w2T", [P, HC, D], BF16)
        total = m.sb("total", [P, 2], F32)
        scale = m.sb("scale", [P, 2], F32)
        tp_banks = [m.bank(f"tp{i}") for i in range(4)]
        tp = [b[:, 0:4 * M].rearrange("p (c n) -> p c n", n=M) for b in tp_banks]
        ps_sum = m.bank("ps_sum")
        ps_total = m.bank("ps_total")
        ps_t = [m.psum(f"ps_t{i}", [P, 2 * BANK], BF16) for i in range(2)]
        const_ready = m.sem("const_ready")
        x_loaded = [m.sem(f"x_loaded{b}") for b in range(2)]
        stats_ready = m.sem("stats_ready")
        stats_seen = m.sem("stats_seen")
        var_ready = m.sem("var_ready")
        root_ready = m.sem("root_ready")
        rstd_ready = m.sem("rstd_ready")
        xn_ready = m.sem("xn_ready")
        turned = m.sem("turned")
        turned_hi = m.sem("turned_hi")
        turned_lo = m.sem("turned_lo")
        edges_in = m.sem("edges_in")
        next_in = m.sem("next_in")
        pad_set = m.sem("pad_set")
        padded = m.sem("padded")
        src_in = m.sem("src_in")
        counted = m.sem("counted")
        summed = m.sem("summed")
        flag_set = m.sem("flag_set")
        raw_in = [m.sem("raw1_in"), m.sem("raw2_in")]
        total_ready = m.sem("total_ready")
        total_summed = m.sem("total_summed")
        scale_ready = m.sem("scale_ready")
        rounded = m.sem("rounded")
        tern_ready = m.sem("tern_ready")
        w_turned = m.sem("w_turned")
        w_kept = m.sem("w_kept")
        w_out = m.sem("w_out")
        chain = m.sem("chain")
        block = stack.enter_context(nc.Block())
        JOBS = [(0, c, c * D, w1T[:, :, c * P:(c + 1) * P]) for c in range(HC)]
        JOBS += [(1, c, c * HID, w2T[:, :, c * P:(c + 2) * P]) for c in range(0, KC, 2)]
        HALF = NT // 2
        rows = lambda t: t.rearrange("(p c) -> p c", c=ER)

        @block.sync
        def _(sp):
            sp.dma_start(dst_i[0:M, :], rows(dst)).then_inc(edges_in, 16)
            with nc.allow_non_contiguous_dma(reason="one word of each row"):
                sp.dma_start(next_i[0:M - 1, :], rows(dst)[1:M, 0:1]).then_inc(next_in, 16)
            for b in range(2):
                sp.dma_start(x_all[0:M, b * HALF:(b + 1) * HALF, :],
                             x[b * HALF * M:(b + 1) * HALF * M, :].rearrange("(t p) d -> p t d", p=M)
                             ).then_inc(x_loaded[b], 16)
            sp.dma_start(work.src_i[0:M, :], rows(src)).then_inc(src_in, 16)
            sp.dma_start(rows(edges_pad[0, 0:E]), rows(dst)).then_inc(padded, 16)
            sp.dma_start(rows(edges_pad[1, 0:E]), rows(src)).then_inc(padded, 16)
            sp.wait_ge(pad_set, 1)
            for i in range(2):
                sp.dma_start(edges_pad[i:i + 1, E:E + ECAP], pad_i[:, :]).then_inc(padded, 16)
            sp.dma_start(raw[0][:, :].rearrange("p (c k) -> p c k", k=D),
                         w1.rearrange("(c p) k -> p c k", p=P)).then_inc(raw_in[0], 16)
            sp.dma_start(raw[1][:, :].rearrange("p (c k) -> p c k", k=HID),
                         w2.rearrange("(c p) k -> p c k", p=P)).then_inc(raw_in[1], 16)
            sp.wait_ge(padded, 64)
            sp.wait_ge(flag_set, 1)
            every = sp.value_load(work.flag_i[0:1, 0:1], min_val=0, max_val=1)
            with sp.If(every < 1):
                with sp.Fori(0, NW) as j:
                    first = sp.value_load(start_i[0:1, ds(j, 1)], min_val=0, max_val=E)
                    sp.dma_start(work.edges[:, :, ds(j, 1), :].rearrange("p i a c -> p i (a c)"),
                                 edges_pad[:, ds(first, ECAP)].rearrange("i (p c) -> p i c", c=EC)
                                 ).then_inc(work.edges_in, 16)
            sp.wait_ge(w_kept, len(JOBS) + 2)
            sp.dma_start(w1T_dram, w1T[:, :, :]).then_inc(w_out, 16)
            sp.dma_start(w2T_dram, w2T[:, :, :]).then_inc(w_out, 16)
            sp.wait_ge(w_out, 32)
            sp.wait_ge(src_in, 16)

        @block.gpsimd
        def _(pool):
            pool.iota(work.limit[:, :], [[W, NW + 1]], base=0, channel_multiplier=0,
                      allow_small_or_imprecise_dtypes=True).then_inc(const_ready, 1)
            pool.iota(pad_i[:, :], [[0, ECAP]], base=-1, channel_multiplier=0).then_inc(pad_set, 1)
            pool.memset(ident[:, :], 0.0).then_inc(const_ready, 1)
            pool.wait_ge(const_ready, 2)
            pool.affine_select(out=ident[:, :], in_=ident[:, :], compare_op=ALU.not_equal, fill=1.0,
                               base=0, pattern=[[-1, P]], channel_multiplier=1).then_inc(const_ready, 1)
            pool.wait_ge(const_ready, 3)
            pool.tensor_copy(ident_b[:, :], ident[:, :]).then_inc(const_ready, 1)

        @block.vector
        def _(dve):
            link = chained(dve, chain)
            nc.vector.memset(ones_r[:, :].bitcast(F32), 1.0)
            nc.vector.memset(xT_hi[:, :, N:NP].bitcast(F32), 0.0)
            nc.vector.memset(xT_lo[:, :, N:NP].bitcast(F32), 0.0)

            link(nc.vector.memset(part[:, :], 0.0))
            dve.wait_ge(const_ready, 1)
            dve.wait_ge(edges_in, 16)
            dve.wait_ge(next_in, 16)
            link(nc.vector.tensor_copy(work.dst_f[0:M, :], dst_i[0:M, :]))
            link(nc.vector.tensor_copy(next_f[0:M - 1, :], next_i[0:M - 1, :]))
            for a, b in ((0, HALF_W), (HALF_W, NW + 1)):
                link(nc.vector.tensor_tensor(below[0:M, 0:b - a, :],
                                             work.dst_f[0:M, :].unsqueeze(1).to_broadcast([M, b - a, ER]),
                                             work.limit[0:M, a:b].unsqueeze(2).to_broadcast([M, b - a, ER]), ALU.is_lt))
                link(nc.vector.tensor_reduce(part[0:M, a:b], below[0:M, 0:b - a, :], AX_X, ALU.add))
            link(nc.vector.tensor_tensor(back[0:M, 0:ER - 1], work.dst_f[0:M, 0:ER - 1], work.dst_f[0:M, 1:ER],
                                         ALU.is_gt))
            link(nc.vector.tensor_reduce(part[0:M, NW + 1:NW + 2], back[0:M, 0:ER - 1], AX_X, ALU.add))
            nc.vector.tensor_tensor(part[0:M - 1, NW + 2:NW + 3], work.dst_f[0:M - 1, ER - 1:ER],
                                    next_f[0:M - 1, :], ALU.is_gt).then_inc(counted, 1)

            def tile_stats(t):
                for h in range(2):
                    nc.vector.bn_stats(stats[0:M, ds(t, 1), h, :].rearrange("p t s -> p (t s)"),
                                       x_all[0:M, ds(t, 1), h * 512:(h + 1) * 512].rearrange("p t d -> p (t d)")
                                       ).then_inc(stats_ready, 1)

            dve.wait_ge(x_loaded[0], 16)
            dve.sem_inc(stats_seen, 1)
            with dve.Fori(0, HALF) as t:
                tile_stats(t)

            dve.wait_ge(summed, 1)
            link(nc.vector.tensor_copy(start_f[:, :], ps_sum[:, 0:NW + 4]))
            link(nc.vector.tensor_copy(start_i[:, :], start_f[:, :]))
            link(nc.vector.tensor_tensor(load_f[:, :], start_f[:, 1:NW + 1], start_f[:, 0:NW], ALU.subtract))
            link(nc.vector.tensor_reduce(flag_f[:, 0:1], load_f[:, :], AX_X, ALU.max))
            link(nc.vector.tensor_scalar(flag_f[:, 0:1], flag_f[:, 0:1], float(ECAP), None, ALU.is_gt))
            link(nc.vector.tensor_tensor(flag_f[:, 0:1], flag_f[:, 0:1], start_f[:, NW + 1:NW + 2], ALU.add))
            link(nc.vector.tensor_tensor(flag_f[:, 0:1], flag_f[:, 0:1], start_f[:, NW + 2:NW + 3], ALU.add))
            nc.vector.tensor_scalar(work.flag_i[:, :], flag_f[:, 0:1], 1.0, None, ALU.min).then_inc(flag_set, 1)

            dve.wait_ge(x_loaded[1], 16)
            dve.sem_inc(stats_seen, 1)
            with dve.Fori(HALF, NT) as t:
                tile_stats(t)
            dve.wait_ge(stats_ready, 2 * NT)
            dve.sem_inc(stats_seen, 1)
            for t in range(NT):
                last = nc.vector.bn_aggr(mv[0:M, t, :], stats[0:M, t, :, :])
            link(last)
            r = lambda i: rs[0:M, i, :]
            mean, var = mv[0:M, :, 0], mv[0:M, :, 1]
            nc.vector.tensor_scalar(r(0), var, EPS_LN, None, ALU.add).then_inc(var_ready, 1)
            dve.wait_ge(root_ready, 1)
            link(nc.vector.reciprocal(r(2), r(1)))
            link(nc.vector.tensor_tensor(r(3), r(2), r(2), ALU.mult))
            link(nc.vector.tensor_tensor(r(4), r(3), r(0), ALU.mult))
            link(nc.vector.tensor_scalar(r(4), r(4), -0.5, 1.5, ALU.mult, ALU.add))
            link(nc.vector.tensor_tensor(r(5), r(4), r(2), ALU.mult))
            nc.vector.scalar_tensor_tensor(r(6), mean, -1.0, r(5), ALU.mult, ALU.mult).then_inc(rstd_ready, 1)

            dve.wait_ge(total_summed, 1)
            link(nc.vector.tensor_scalar(unit[:, :], ps_total[:, 0:2], 1.0 / (HID * D), EPS_Q, ALU.mult, ALU.max))
            nc.vector.reciprocal(scale[:, :], unit[:, :]).then_inc(scale_ready, 1)

            with dve.Fori(0, HALF) as i:
                for b in range(2):
                    for h in range(2):
                        dve.wait_ge(turned_hi, i * 4 + (2 * b + h + 1))
                        nc.vector.tensor_tensor(xT_lo[:, 4 * h:4 * h + 4, ds(i * (2 * M) + b * M, M)],
                                                tp[2 * b + h][:, :, :],
                                                xT_hi[:, 4 * h:4 * h + 4, ds(i * (2 * M) + b * M, M)].bitcast(F32),
                                                ALU.subtract).then_inc(turned_lo, 1)
            for i in range(2):
                dve.wait_ge(rounded, i + 1)
                link(nc.vector.tensor_scalar(raw[i][:, :], raw[i][:, :], ROUND, 1.0, ALU.subtract, ALU.min))
                nc.vector.tensor_scalar(tern[i][:, :], raw[i][:, :], -1.0, None, ALU.max).then_inc(tern_ready, 1)

        @block.scalar
        def _(act):
            act.wait_ge(var_ready, 1)
            nc.scalar.activation(rs[0:M, 1, :], rs[0:M, 0, :], ACT.Sqrt).then_inc(root_ready, 1)
            for i in range(2):
                act.wait_ge(raw_in[i], 16)
                nc.scalar.activation(tern[i][:, :], raw[i][:, :], ACT.Abs,
                                     accum_out=total[:, i:i + 1]).then_inc(total_ready, 1)
            act.wait_ge(rstd_ready, 1)

            def normalise(t):
                at = x_all[0:M, t, :]
                nc.scalar.activation(at, at, ACT.Identity, bias=rs[0:M, 6, t:t + 1],
                                     scale=rs[0:M, 5, t:t + 1]).then_inc(xn_ready, 1)

            for t in range(NT):
                normalise(t)
            with act.Fori(0, HALF) as i:
                for b in range(2):
                    for h in range(2):
                        act.wait_ge(turned, i * 4 + (2 * b + h + 1))
                        nc.scalar.copy(xT_hi[:, 4 * h:4 * h + 4, ds(i * (2 * M) + b * M, M)],
                                       tp[2 * b + h][:, :, :]).then_inc(turned_hi, 1)
            act.wait_ge(scale_ready, 1)
            act.wait_ge(total_ready, 2)
            for i in range(2):
                nc.scalar.activation(raw[i][:, :], raw[i][:, :], ACT.Copy, bias=ROUND,
                                     scale=scale[:, i:i + 1]).then_inc(rounded, 1)
            for n, (i, _, _, to) in enumerate(JOBS):
                act.wait_ge(w_turned, n + 1)
                nc.scalar.copy(to, ps_t[n % 2][:, :].rearrange("p (c n) -> p c n", c=(KC, HC)[i])).then_inc(w_kept, 1)

        @block.tensor
        def _(pe):
            pe.wait_ge(counted, 1)
            nc.tensor.matmul(ps_sum[:, 0:NW + 4], ones_r[0:M, :].bitcast(F32), part[0:M, :],
                             start=True, stop=True).then_inc(summed, 1)
            pe.wait_ge(total_ready, 2)
            nc.tensor.matmul(ps_total[:, 0:2], ones_r[:, :].bitcast(F32), total[:, :],
                             start=True, stop=True).then_inc(total_summed, 1)
            pe.wait_ge(const_ready, 4)
            pe.sem_inc(turned_lo, 4)
            for t in range(NT):
                pe.wait_ge(xn_ready, t + 1)
                for h in range(2):
                    pe.wait_ge(turned_lo, 2 * t + h + 1)
                    for c in range(4):
                        k = 4 * h + c
                        last = nc.tensor.transpose(tp[2 * (t % 2) + h][:, c, :], x_all[0:M, t, k * P:(k + 1) * P],
                                                   ident[0:M, 0:M])
                    last.then_inc(turned, 1)
            pe.sem_inc(w_kept, 2)
            for n, (i, c, at, _) in enumerate(JOBS):
                pe.wait_ge(tern_ready, i + 1)
                pe.wait_ge(w_kept, n + 1)
                for u in range(8):
                    col = u if i == 0 else (u % HC) * 2 + u // HC
                    last = nc.tensor.transpose(ps_t[n % 2][:, col * P:(col + 1) * P],
                                               tern[i][:, at + u * P:at + (u + 1) * P], ident_b[:, :])
                last.then_inc(w_turned, 1)


class EdgeWork:

    def __init__(self, m):
        self.src_i = m.sb("src_i", [P, ER], I32)
        self.dst_f = m.sb("dst_f", [P, ER], F32)
        self.limit = m.sb("limit", [P, NW + 1], F32)
        self.flag_i = m.sb("flag_i", [P, 1], I32)
        self.edges = m.sb("edges", [P, 2, NW, EC], I32)
        self.edges_in = m.sem("edges_in")




def stage_graph(nc, work, ident, ones_r, adj_dram, inv_row, inv_col):
    with ExitStack() as stack:
        m = Pool(nc, stack, "graph")
        adj = m.sb("adj", [P, NT, NP], F32R)
        iota_b = m.sb("iota_b", [P, P], BF16)
        iota_c = m.sb("iota_c", [P, WC], BF16)
        s_f = m.sb("s_f", [P, NW, EC], F32)
        d_f = m.sb("d_f", [P, NW, EC], F32)
        a_f = m.sb("a_f", [P, NW, EC], F32)
        b_f = m.sb("b_f", [P, NW, EC], F32)
        in_f = m.sb("in_f", [P, NW, EC], F32)
        col_f = m.sb("col_f", [P, NW, EC], F32)
        hot_b = m.sb("hot_b", [P, 2 * GC, P], BF16)
        hot_c = m.sb("hot_c", [P, 2 * GC, WC], BF16)
        ps_w = [m.bank(f"ps_w{i}")[:, 0:WC].rearrange("p (a d) -> p a d", d=W) for i in range(2)]
        ps_deg = [m.bank(f"ps_deg{t}")[:, 0:CW] for t in range(CT)]
        ps_col = m.bank("ps_col")[:, 0:NT]
        consts = m.sem("consts")
        stored = m.sem("stored")
        chain = [m.sem(f"chain_{n}") for n in ("short", "general", "degree")]
        columns_set = m.sem("columns_set")
        hot_ready = m.sem("hot_ready")
        hot_used = m.sem("hot_used")
        window_done = m.sem("window_done")
        window_kept = m.sem("window_kept")
        zeroed = m.sem("zeroed")
        deg_ready = m.sem("deg_ready")
        inv_ready = m.sem("inv_ready")
        col_ready = m.sem("col_ready")
        block = stack.enter_context(nc.Block())

        @block.sync
        def _(sp):
            for i in range(2):
                sp.wait_ge(window_kept, NW // 2 * (i + 1) + 2)
                if i:
                    sp.wait_ge(zeroed, 1)
                cols = slice(i * N // 2, (N // 2, NP)[i])
                sp.dma_start(adj_dram[:, :, cols], adj[0:M, :, cols].bitcast(F32)).then_inc(stored, 16)
            sp.wait_ge(stored, 32)

        @block.gpsimd
        def _(pool):
            pool.iota(iota_b[:, :], [[1, P]], base=0, channel_multiplier=0,
                      allow_small_or_imprecise_dtypes=True).then_inc(consts, 1)
            pool.iota(iota_c[:, :], [[1, WC]], base=0, channel_multiplier=0,
                      allow_small_or_imprecise_dtypes=True).then_inc(consts, 1)

        @block.vector
        def _(dve):
            at = [0, 0]

            def link(ins):
                at[1] += 1
                ins.then_inc(chain[at[0]], 1)
                dve.wait_ge(chain[at[0]], at[1])

            nc.vector.memset(adj[:, :, N:NP].bitcast(F32), 0.0).then_inc(zeroed, 1)
            dve.wait_ge(consts, 2)

            def split_source(a, b, s):
                link(nc.vector.tensor_scalar(a, s, 1.0 / M, 0.5 / M - 0.5, ALU.mult, ALU.add))
                link(nc.vector.tensor_scalar(a, a, ROUND, ROUND, ALU.add, ALU.subtract))
                link(nc.vector.scalar_tensor_tensor(b, a, -float(M), s, ALU.mult, ALU.add))

            every = dve.value_load(work.flag_i[0:1, 0:1], min_val=0, max_val=1)
            dve.sem_inc(hot_used, 2 * GC)
            at[:] = 0, 0
            with dve.If(every < 1):
                dve.wait_ge(work.edges_in, 16 * NW)
                link(nc.vector.tensor_copy(s_f[:, :, :], work.edges[:, 1, :, :]))
                link(nc.vector.tensor_copy(d_f[:, :, :], work.edges[:, 0, :, :]))
                split_source(a_f[:, :, :], b_f[:, :, :], s_f[:, :, :])
                link(nc.vector.tensor_tensor(d_f[:, :, :], d_f[:, :, :],
                                             work.limit[:, 0:NW].unsqueeze(2).to_broadcast([P, NW, EC]), ALU.subtract))
                link(nc.vector.tensor_scalar(in_f[:, :, :], d_f[:, :, :], 0.0, None, ALU.is_ge))
                link(nc.vector.scalar_tensor_tensor(in_f[:, :, :], d_f[:, :, :], W - 1.0, in_f[:, :, :],
                                                    ALU.is_le, ALU.mult))
                link(nc.vector.scalar_tensor_tensor(col_f[:, :, :], a_f[:, :, :], float(W), d_f[:, :, :],
                                                    ALU.mult, ALU.add))
                link(nc.vector.scalar_tensor_tensor(col_f[:, :, :], col_f[:, :, :], 1.0, in_f[:, :, :],
                                                    ALU.add, ALU.mult))
                link(nc.vector.tensor_scalar(col_f[:, :, :], col_f[:, :, :], -1.0, None, ALU.add))
                with dve.Fori(0, NW // 4) as q:
                    for w in range(4):
                        for c in range(EC):
                            h = w * EC + c
                            dve.wait_ge(hot_used, q * (2 * GC) + (h + 1))
                            nc.vector.tensor_scalar(hot_b[:, h, :], iota_b[:, :],
                                                    b_f[:, ds(q * 4 + w, 1), c:c + 1].rearrange("p a c -> p (a c)"),
                                                    None, ALU.is_equal)
                            nc.vector.tensor_scalar(hot_c[:, h, :], iota_c[:, :],
                                                    col_f[:, ds(q * 4 + w, 1), c:c + 1].rearrange("p a c -> p (a c)"),
                                                    None, ALU.is_equal).then_inc(hot_ready, 1)
                for w in range(NW - NW // 4 * 4):
                    for c in range(EC):
                        h = w * EC + c
                        dve.wait_ge(hot_used, NW // 4 * 2 * GC + h + 1)
                        nc.vector.tensor_scalar(hot_b[:, h, :], iota_b[:, :], b_f[:, NW // 4 * 4 + w, c:c + 1],
                                                None, ALU.is_equal)
                        nc.vector.tensor_scalar(hot_c[:, h, :], iota_c[:, :], col_f[:, NW // 4 * 4 + w, c:c + 1],
                                                None, ALU.is_equal).then_inc(hot_ready, 1)
            at[:] = 1, 0
            with dve.If(every > 0):
                flat = lambda t: t[0:M, :, :].rearrange("p a c -> p (a c)")[:, 0:ER]
                link(nc.vector.tensor_copy(flat(s_f), work.src_i[0:M, :]))
                split_source(flat(a_f), flat(b_f), flat(s_f))
                with dve.Fori(0, NW) as j:
                    c0 = j * 5 + at[1]
                    nc.vector.tensor_scalar(flat(d_f), work.dst_f[0:M, :], work.limit[0:M, ds(j, 1)], None,
                                            ALU.subtract).then_inc(chain[1], 1)
                    dve.wait_ge(chain[1], c0 + 1)
                    nc.vector.tensor_scalar(flat(in_f), flat(d_f), 0.0, None, ALU.is_ge).then_inc(chain[1], 1)
                    dve.wait_ge(chain[1], c0 + 2)
                    nc.vector.scalar_tensor_tensor(flat(in_f), flat(d_f), W - 1.0, flat(in_f),
                                                   ALU.is_le, ALU.mult).then_inc(chain[1], 1)
                    nc.vector.scalar_tensor_tensor(flat(col_f), flat(a_f), float(W), flat(d_f),
                                                   ALU.mult, ALU.add).then_inc(chain[1], 1)
                    dve.wait_ge(chain[1], c0 + 4)
                    nc.vector.scalar_tensor_tensor(flat(col_f), flat(col_f), 1.0, flat(in_f),
                                                   ALU.add, ALU.mult).then_inc(chain[1], 1)
                    dve.wait_ge(chain[1], c0 + 5)
                    dve.sem_inc(columns_set, 1)
                    with dve.Fori(0, ER // (2 * GC)) as g:
                        for h in range(2 * GC):
                            dve.wait_ge(hot_used, j * ER + g * (2 * GC) + (h + 1))
                            nc.vector.tensor_scalar(hot_b[0:M, h, :], iota_b[0:M, :],
                                                    flat(b_f)[:, ds(g * (2 * GC) + h, 1)], None, ALU.is_equal)
                            nc.vector.tensor_scalar(hot_c[0:M, h, :], iota_c[0:M, :], 1.0,
                                                    flat(col_f)[:, ds(g * (2 * GC) + h, 1)],
                                                    ALU.add, ALU.is_equal).then_inc(hot_ready, 1)
            at[:] = 2, 0
            for t in range(CT):
                dve.wait_ge(deg_ready, t + 1)
                link(nc.vector.tensor_scalar(inv_row[:, t * CW:(t + 1) * CW], ps_deg[t][:, :], 1.0, None, ALU.max))
                nc.vector.reciprocal(inv_row[:, t * CW:(t + 1) * CW],
                                     inv_row[:, t * CW:(t + 1) * CW]).then_inc(inv_ready, 1)
            dve.wait_ge(col_ready, 1)
            nc.vector.tensor_copy(inv_col[0:M, :], ps_col[0:M, :]).then_inc(inv_ready, 1)

        @block.tensor
        def _(pe):
            pe.sem_inc(window_kept, 2)
            every = pe.value_load(work.flag_i[0:1, 0:1], min_val=0, max_val=1)
            with pe.If(every < 1):
                def window(w, kept, ready):
                    pe.wait_ge(window_kept, kept)
                    for c in range(EC):
                        h = w * EC + c
                        pe.wait_ge(hot_ready, ready + (h + 1))
                        last = nc.tensor.matmul(ps_w[w % 2][:, :, :], hot_b[:, h, :], hot_c[:, h, :],
                                                start=(c == 0), stop=(c == EC - 1)).then_inc(hot_used, 1)
                    pe.wait_ge(hot_used, ready + (2 * GC + w * EC + EC))
                    pe.sem_inc(window_done, 1)

                with pe.Fori(0, NW // 4) as q:
                    for w in range(4):
                        window(w, q * 4 + (w + 1), q * (2 * GC))
                for w in range(NW - NW // 4 * 4):
                    window(w, NW // 4 * 4 + w + 1, NW // 4 * 2 * GC)
            with pe.If(every > 0):
                def group(b, ready, first, final):
                    for h in range(2 * GC):
                        pe.wait_ge(hot_ready, ready + (h + 1))
                        nc.tensor.matmul(ps_w[b][:, :, :], hot_b[0:M, h, :], hot_c[0:M, h, :],
                                         start=(first and h == 0), stop=(final and h == 2 * GC - 1)).then_inc(hot_used, 1)

                with pe.Fori(0, NW // 2) as q:
                    for b in range(2):
                        pe.wait_ge(window_kept, q * 2 + (b + 1))
                        base = q * (2 * ER) + b * ER
                        group(b, base, True, False)
                        with pe.Fori(1, ER // (2 * GC) - 1) as g:
                            group(b, base + g * (2 * GC), False, False)
                        group(b, base + (ER - 2 * GC), False, True)
                        pe.wait_ge(hot_used, base + (ER + 2 * GC))
                        pe.sem_inc(window_done, 1)
            pe.wait_ge(window_kept, NW + 2)
            pe.wait_ge(zeroed, 1)
            for t in range(CT):
                for a in range(NT):
                    last = nc.tensor.matmul(ps_deg[t][:, :], ones_r[0:M, :], adj[0:M, a, t * CW:(t + 1) * CW],
                                            start=(a == 0), stop=(a == NT - 1))
                last.then_inc(deg_ready, 1)
            pe.wait_ge(inv_ready, CT)
            for a in range(NT):
                last = nc.tensor.transpose(ps_col[0:M, a:a + 1], inv_row[0:1, a * M:(a + 1) * M], ident[0:1, 0:1])
            last.then_inc(col_ready, 1)

        @block.scalar
        def _(act):
            with act.Fori(0, NW // 2) as q:
                for b in range(2):
                    act.wait_ge(window_done, q * 2 + (b + 1))
                    nc.scalar.copy(adj[0:M, :, ds(q * (2 * W) + b * W, W)], ps_w[b][0:M, :, :]).then_inc(window_kept, 1)


def panel(w, j, width=P):
    return w[:, ds(j * width, width)].rearrange("(c p) n -> p c n", p=P)


def exact_product(pe, out, pairs):
    for n, (lh, ll, rh, rl) in enumerate(pairs):
        first, final = n == 0, n == len(pairs) - 1
        pe.matmul(out, lh, rh, start=first, stop=False)
        pe.matmul(out, lh, rl, start=False, stop=False)
        last = pe.matmul(out, ll, rh, start=False, stop=final)
    return last


def stage_sage0(nc, w_neigh, w_self, bias, xT_hi, xT_lo, adj_dram, adj, inv_row, ident, hT_hi_dram, hT_lo_dram):
    with ExitStack() as stack:
        m = Pool(nc, stack, "sage0")
        raw_n = m.sb("raw_n", [P, KC, P], F32)
        raw_s = m.sb("raw_s", [P, KC, P], F32)
        wn_hi = m.sb("wn_hi", [P, KC, P], F32R)
        wn_lo = m.sb("wn_lo", [P, KC, P], F32R)
        ws_hi = m.sb("ws_hi", [P, KC, P], F32R)
        ws_lo = m.sb("ws_lo", [P, KC, P], F32R)
        b_col = m.sb("b_col", [P, KC], F32)
        pT = m.sb("pT", [P, NP], F32)
        p_hi = m.sb("p_hi", [P, NT, P], F32R)
        p_lo = m.sb("p_lo", [P, NT, P], F32R)
        mean = m.sb("mean", [P, CT, CW], F32)
        pre = m.sb("pre", [P, CT, CW], F32)
        h_hi = m.sb("h_hi", [P, CT, CW], F32R)
        h_lo = m.sb("h_lo", [P, CT, CW], F32R)
        ps_n = [m.psum(f"ps_n{t}", [P, BANK]) for t in range(CT)]
        ps_s = [m.psum(f"ps_s{t}", [P, BANK]) for t in range(CT)]
        ps_t = [m.psum(f"ps_t{i}", [P, 4, P]) for i in range(2)]
        bias_in = m.sem("bias_in")
        adj_in = m.sem("adj_in")
        raw_n_in = m.sem("raw_n_in")
        raw_s_in = m.sem("raw_s_in")
        wn_hi_ready = m.sem("wn_hi_ready")
        wn_ready = m.sem("wn_ready")
        ws_hi_ready = m.sem("ws_hi_ready")
        ws_ready = m.sem("ws_ready")
        n_done = m.sem("n_done")
        s_done = m.sem("s_done")
        pT_ready = m.sem("pT_ready")
        turned = m.sem("turned")
        p_hi_ready = m.sem("p_hi_ready")
        p_ready = m.sem("p_ready")
        agg_done = m.sem("agg_done")
        mean_ready = m.sem("mean_ready")
        pre_ready = m.sem("pre_ready")
        h_hi_ready = m.sem("h_hi_ready")
        h_ready = m.sem("h_ready")
        h_out = [m.sem(f"h_out{t}") for t in range(CT)]
        block = stack.enter_context(nc.Block())
        cols = lambda t: slice(t * CW, (t + 1) * CW)

        @block.sync
        def _(sp):
            with nc.allow_non_contiguous_dma(reason="a bias, one word a partition"):
                sp.dma_start(b_col[:, :], bias.rearrange("(c p) -> p c", p=P)).then_inc(bias_in, 16)
            sp.dma_start(raw_n[:, :, :], panel(w_neigh, 0)).then_inc(raw_n_in, 16)
            sp.dma_start(raw_s[:, :, :], panel(w_self, 0)).then_inc(raw_s_in, 16)
            sp.dma_start(adj[0:M, :, :].bitcast(F32), adj_dram).then_inc(adj_in, 16)

            def chunk(j, last=False):
                if not last:
                    sp.wait_ge(wn_ready, j + 1)
                    sp.dma_start(raw_n[:, :, :], panel(w_neigh, j + 1)).then_inc(raw_n_in, 16)
                    sp.wait_ge(ws_ready, j + 1)
                    sp.dma_start(raw_s[:, :, :], panel(w_self, j + 1)).then_inc(raw_s_in, 16)
                for t in range(CT):
                    sp.wait_ge(h_ready, j * CT + (t + 1))
                    sp.dma_start(hT_hi_dram[ds(j * P, P), cols(t)], h_hi[:, t, :].bitcast(F32)).then_inc(h_out[t], 16)
                    sp.dma_start(hT_lo_dram[ds(j * P, P), cols(t)], h_lo[:, t, :].bitcast(F32)).then_inc(h_out[t], 16)

            with sp.Fori(0, KC - 1) as j:
                chunk(j)
            chunk(KC - 1, last=True)
            for t in range(CT):
                sp.wait_ge(h_out[t], 32 * KC + 32)

        @block.scalar
        def _(act):
            def split_n(j):
                act.wait_ge(raw_n_in, j * 16 + 16)
                nc.scalar.copy(wn_hi[:, :, :], raw_n[:, :, :]).then_inc(wn_hi_ready, 1)

            def split_s(j):
                act.wait_ge(raw_s_in, j * 16 + 16)
                nc.scalar.copy(ws_hi[:, :, :], raw_s[:, :, :]).then_inc(ws_hi_ready, 1)

            def chunk(j, last=False):
                for t in range(CT):
                    act.wait_ge(n_done, j * CT + (t + 1))
                    nc.scalar.copy(pT[:, cols(t)], ps_n[t][:, 0:CW]).then_inc(pT_ready, 1)
                if not last:
                    split_n(j + 1)
                for g, (a, b) in enumerate(TURNS):
                    act.wait_ge(turned, j * 3 + (g + 1))
                    nc.scalar.copy(p_hi[0:M, a:b, :], ps_t[g % 2][0:M, 0:b - a, :]).then_inc(p_hi_ready, 1)
                if not last:
                    act.wait_ge(s_done, j * CT + CT)
                    split_s(j + 1)
                for t in range(CT):
                    act.wait_ge(pre_ready, j * CT + (CT + t + 1))
                    act.wait_ge(h_out[t], j * 32 + 32)
                    nc.scalar.activation(h_hi[:, t, :], pre[:, t, :], ACT.Relu).then_inc(h_hi_ready, 1)

            for t in range(CT):
                act.sem_inc(h_out[t], 32)
            split_n(0)
            split_s(0)
            with act.Fori(0, KC - 1) as j:
                chunk(j)
            chunk(KC - 1, last=True)

        @block.vector
        def _(dve):
            def split_n(j):
                dve.wait_ge(wn_hi_ready, j + 1)
                nc.vector.tensor_tensor(wn_lo[:, :, :], raw_n[:, :, :], wn_hi[:, :, :].bitcast(F32),
                                        ALU.subtract).then_inc(wn_ready, 1)

            def split_s(j):
                dve.wait_ge(ws_hi_ready, j + 1)
                nc.vector.tensor_tensor(ws_lo[:, :, :], raw_s[:, :, :], ws_hi[:, :, :].bitcast(F32),
                                        ALU.subtract).then_inc(ws_ready, 1)

            def chunk(j, last=False):
                if not last:
                    split_n(j + 1)
                for g, (a, b) in enumerate(TURNS):
                    dve.wait_ge(p_hi_ready, j * 3 + (g + 1))
                    nc.vector.tensor_tensor(p_lo[0:M, a:b, :], ps_t[g % 2][0:M, 0:b - a, :],
                                            p_hi[0:M, a:b, :].bitcast(F32), ALU.subtract).then_inc(p_ready, 1)
                if not last:
                    split_s(j + 1)
                for t in range(CT):
                    dve.wait_ge(agg_done, j * CT + (t + 1))
                    nc.vector.tensor_tensor(mean[:, t, :], ps_n[t][:, 0:CW], inv_row[:, cols(t)],
                                            ALU.mult).then_inc(mean_ready, 1)
                    dve.wait_ge(mean_ready, j * CT + (CT + t + 1))
                    nc.vector.scalar_tensor_tensor(pre[:, t, :], ps_s[t][:, 0:CW], b_col[:, ds(j, 1)],
                                                   mean[:, t, :], ALU.add, ALU.add).then_inc(pre_ready, 1)
                for t in range(CT):
                    dve.wait_ge(h_hi_ready, j * CT + (t + 1))
                    nc.vector.scalar_tensor_tensor(h_lo[:, t, :], pre[:, t, :], 0.0, h_hi[:, t, :].bitcast(F32),
                                                   ALU.max, ALU.subtract).then_inc(h_ready, 1)

            dve.sem_inc(mean_ready, CT)
            dve.sem_inc(pre_ready, CT)
            dve.sem_inc(p_ready, 1)
            dve.wait_ge(bias_in, 16)
            split_n(0)
            split_s(0)
            with dve.Fori(0, KC - 1) as j:
                chunk(j)
            chunk(KC - 1, last=True)

        @block.tensor
        def _(pe):
            def chunk(j):
                pe.wait_ge(wn_ready, j + 1)
                for t in range(CT):
                    pe.wait_ge(mean_ready, j * CT + (t + 1))
                    exact_product(pe, ps_n[t][:, 0:CW],
                                  [(wn_hi[:, k, :], wn_lo[:, k, :], xT_hi[:, k, cols(t)], xT_lo[:, k, cols(t)])
                                   for k in range(KC)]).then_inc(n_done, 1)
                pe.wait_ge(ws_ready, j + 1)

                def self_product(t):
                    pe.wait_ge(pre_ready, j * CT + (t + 1))
                    exact_product(pe, ps_s[t][:, 0:CW],
                                  [(ws_hi[:, k, :], ws_lo[:, k, :], xT_hi[:, k, cols(t)], xT_lo[:, k, cols(t)])
                                   for k in range(KC)]).then_inc(s_done, 1)

                def turn(g):
                    pe.wait_ge(p_ready, j * 3 + (1, 1, 2)[g])
                    a, b = TURNS[g]
                    for n in range(a, b):
                        last = pe.transpose(ps_t[g % 2][0:M, n - a, :], pT[:, n * M:(n + 1) * M], ident[:, :])
                    last.then_inc(turned, 1)

                self_product(0)
                pe.wait_ge(pT_ready, j * CT + CT)
                turn(0)
                turn(1)
                self_product(1)
                turn(2)
                self_product(2)
                pe.wait_ge(p_ready, j * 3 + 4)
                pe.wait_ge(adj_in, 16)
                for t in range(CT):
                    for a in range(NT):
                        pe.matmul(ps_n[t][:, 0:CW], p_hi[0:M, a, :], adj[0:M, a, cols(t)],
                                  start=(a == 0), stop=False)
                        last = pe.matmul(ps_n[t][:, 0:CW], p_lo[0:M, a, :], adj[0:M, a, cols(t)],
                                         start=False, stop=(a == NT - 1))
                    last.then_inc(agg_done, 1)

            with pe.Fori(0, KC) as j:
                chunk(j)


HEADS, HD, NF = 16, 64, 256
HP = HEADS // 2
VW = HD + 2
PAIR = 2 * M
STEPS = NT // 2
EPS_Z = 1e-6


def stage_attention(nc, w_qkv, proj, xT_hi, xT_lo, ident, oT_hi_dram, oT_lo_dram):
    with ExitStack() as stack:
        m = Pool(nc, stack, "att")
        raw = {n: m.sb(f"raw_{n}", [P, KC, P], F32) for n in "qkv"}
        w_hi = {n: m.sb(f"w{n}_hi", [P, KC, P], F32R) for n in "qkv"}
        w_lo = {n: m.sb(f"w{n}_lo", [P, KC, P], F32R) for n in "qkv"}
        t_hi = {n: m.sb(f"{n}T_hi", [P, NP], F32R) for n in "qk"}
        t_lo = {n: m.sb(f"{n}T_lo", [P, NP], F32R) for n in "qk"}
        vT = m.sb("vT", [P, NP], F32)
        v_hi = m.sb("v_hi", [P, NT, 2, VW], F32R)
        v_lo = m.sb("v_lo", [P, NT, 2, VW], F32R)
        raw_p = m.sb("raw_p", [P, NF], F32)
        pj_hi = m.sb("pj_hi", [P, 2 * NF], F32R)
        pj_lo = m.sb("pj_lo", [P, 2 * NF], F32R)
        neg_max = m.sb("neg_max", [P, 2, 2], F32)
        feat = m.sb("feat", [P, 2, 2 * NF], F32)
        k_hi = m.sb("k_hi", [P, 2, 2 * NF], F32R)
        k_lo = m.sb("k_lo", [P, 2, 2 * NF], F32R)
        qf_hi = m.sb("qf_hi", [P, 2, 4, PAIR], F32R)
        qf_lo = m.sb("qf_lo", [P, 2, 4, PAIR], F32R)
        kvT = m.sb("kvT", [VW, 2 * NF], F32)
        kv_hi = m.sb("kv_hi", [P, 4, P], F32R)
        kv_lo = m.sb("kv_lo", [P, 4, P], F32R)
        den = m.sb("den", [P, PAIR], F32)
        att = m.sb("att", [P, PAIR], F32)
        att_hi = m.sb("att_hi", [P, PAIR], F32R)
        att_lo = m.sb("att_lo", [P, PAIR], F32R)
        ps_g = [m.psum(f"ps_g{i}", [P, BANK]) for i in range(2)]
        ps_z = [m.psum(f"ps_z{i}", [P, BANK]) for i in range(2)]
        ps_t = [m.psum(f"ps_t{i}", [P, BANK]) for i in range(2)]
        ps_kv = m.psum("ps_kv", [P, BANK])
        ps_o = m.psum("ps_o", [P, BANK])
        raw_in = {n: m.sem(f"raw_{n}_in") for n in "qkvp"}
        w_hi_ready = {n: m.sem(f"w{n}_hi_ready") for n in "qkv"}
        w_ready = {n: m.sem(f"w{n}_ready") for n in "qkv"}
        pj_hi_ready = m.sem("pj_hi_ready")
        pj_ready = m.sem("pj_ready")
        g_done = {n: m.sem(f"{n}_done") for n in "qkv"}
        t_hi_ready = {n: m.sem(f"{n}T_hi_ready") for n in "qk"}
        t_ready = {n: m.sem(f"{n}T_ready") for n in "qkv"}
        z_done = m.sem("z_done")
        max_ready = m.sem("max_ready")
        feat_ready = m.sem("feat_ready")
        k_ready = m.sem("k_ready")
        kv_added = m.sem("kv_added")
        kvT_ready = m.sem("kvT_ready")
        kv_turned = m.sem("kv_turned")
        kv_hi_ready = m.sem("kv_hi_ready")
        kv_ready = m.sem("kv_ready")
        q_turned = m.sem("q_turned")
        qf_hi_ready = m.sem("qf_hi_ready")
        qf_ready = m.sem("qf_ready")
        v_turned = m.sem("v_turned")
        v_hi_ready = m.sem("v_hi_ready")
        v_ready = m.sem("v_ready")
        out_done = m.sem("out_done")
        den_ready = m.sem("den_ready")
        inv_ready = m.sem("inv_ready")
        att_ready = m.sem("att_ready")
        att_hi_ready = m.sem("att_hi_ready")
        att_split = m.sem("att_split")
        att_out = m.sem("att_out")
        blank = m.sem("blank")
        held = m.sem("held")
        block = stack.enter_context(nc.Block())
        cols = lambda t: slice(t * CW, (t + 1) * CW)
        tile = lambda t: slice(t * M, (t + 1) * M)
        half = lambda t: slice((t % 2) * M, (t % 2) * M + M)
        OFF = {"q": 0, "k": 1, "v": 2}
        BANKS = {"q": ((1, "k", 0, 3), (0, "k", 0, 2), (1, "q", 0, 1)),
                 "v": ((0, "q", -1, 2), (1, "q", -1, 3), (0, "v", 0, 1)),
                 "k": ((1, "v", 0, 2), (0, "v", 0, 3), (1, "k", 0, 1))}

        @block.sync
        def _(sp):
            def load_w(n, hp):
                sp.dma_start(raw[n][:, :, :], panel(w_qkv[:, OFF[n] * D:(OFF[n] + 1) * D], hp)).then_inc(raw_in[n], 16)

            def load_p(hp):
                sp.dma_start(raw_p[:, :], proj[ds(hp * 2, 2), :, :].rearrange("h d f -> (h d) f")).then_inc(raw_in["p"], 16)

            def store(hp, s):
                sp.wait_ge(att_split, hp * STEPS + (s + 2))
                sp.dma_start(oT_hi_dram[ds(hp * P, P), s * PAIR:(s + 1) * PAIR], att_hi[:, :].bitcast(F32)).then_inc(att_out, 16)
                sp.dma_start(oT_lo_dram[ds(hp * P, P), s * PAIR:(s + 1) * PAIR], att_lo[:, :].bitcast(F32)).then_inc(att_out, 16)

            def pair(hp, after_next, first=False, last=False):
                if not first:
                    for s in (STEPS - 2, STEPS - 1):
                        store(hp - 1, s)
                if not last:
                    sp.wait_ge(w_ready["q"], hp + 1)
                    load_w("q", hp + 1)
                    sp.wait_ge(pj_ready, hp * 2 + 2)
                    load_p(hp + 1)
                    for n in "vk":
                        sp.wait_ge(w_ready[n], hp + 2)
                        load_w(n, after_next)
                for s in range(STEPS - 2):
                    store(hp, s)

            for n in "vkq":
                load_w(n, 0)
            load_p(0)
            for n in "vk":
                sp.wait_ge(w_ready[n], 1)
                load_w(n, 1)
            pair(0, 2, first=True)
            with sp.Fori(1, HP - 2) as hp:
                pair(hp, hp + 2)
            pair(HP - 2, HP - 1)
            pair(HP - 1, None, last=True)
            for s in (STEPS - 2, STEPS - 1):
                store(HP - 1, s)
            sp.wait_ge(att_out, 32 * HP * STEPS + 32)

        @block.gpsimd
        def _(pool):
            def split_w(n, hp):
                pool.wait_ge(raw_in[n], hp * 16 + 16)
                pool.sem_inc(held, 1)
                nc.gpsimd.tensor_copy(w_hi[n][:, :, :], raw[n][:, :, :]).then_inc(w_hi_ready[n], 1)

            def split_att(hp, s):
                pool.wait_ge(att_ready, hp * STEPS + (s + 2))
                pool.wait_ge(att_out, hp * (32 * STEPS) + 32 * (s + 1))
                pool.sem_inc(held, 1)
                nc.gpsimd.tensor_copy(att_hi[:, :], att[:, :]).then_inc(att_hi_ready, 1)
                pool.wait_ge(att_hi_ready, hp * STEPS + (s + 1))
                nc.gpsimd.tensor_tensor(att_lo[:, :], att[:, :], att_hi[:, :].bitcast(F32),
                                        ALU.subtract).then_inc(att_split, 1)

            def pair(hp, first=False, last=False):
                if not first:
                    for s in (STEPS - 2, STEPS - 1):
                        split_att(hp - 1, s)
                for s in range(1, STEPS):
                    if not last and s == 1:
                        pool.wait_ge(g_done["q"], hp * CT + CT)
                        split_w("q", hp + 1)
                    if not last and s == 3:
                        pool.wait_ge(g_done["v"], hp * CT + 2 * CT)
                        split_w("v", hp + 2)
                    if s >= 2:
                        split_att(hp, s - 2)
                if not last:
                    pool.wait_ge(g_done["k"], hp * CT + 2 * CT)
                    split_w("k", hp + 2)

            pool.sem_inc(att_split, 1)
            pool.sem_inc(att_out, 32)
            for n in "vkq":
                split_w(n, 0)
            for n in "vk":
                pool.wait_ge(g_done[n], CT)
                split_w(n, 1)
            pair(0, first=True)
            with pool.Fori(1, HP - 1) as hp:
                pair(hp)
            pair(HP - 1, last=True)
            for s in (STEPS - 2, STEPS - 1):
                split_att(HP - 1, s)

        @block.scalar
        def _(act):
            def keep(n, hp, t):
                act.wait_ge(g_done[n], hp * CT + (t + 1))
                src = ps_g[BANKS[n][t][0]][:, 0:CW]
                if n == "v":
                    nc.scalar.copy(vT[:, cols(t)], src).then_inc(t_ready["v"], 1)
                else:
                    nc.scalar.copy(t_hi[n][:, cols(t)], src).then_inc(t_hi_ready[n], 1)

            def features(hp, t, i):
                act.wait_ge(max_ready, hp * (2 * NT) + (i + 1))
                if i < NT:
                    act.wait_ge(k_ready, hp * NT + (t + 1))
                    act.wait_ge(kv_added, hp * NT + (t + 1))
                    if t < 2:
                        act.wait_ge(q_turned, hp * NT + 2)
                else:
                    act.wait_ge(q_turned, hp * NT + (t + 1))
                    if t < 2:
                        act.wait_ge(k_ready, hp * NT + (NT + 2))
                for to in (k_hi, feat) if i < NT else (feat,):
                    for h in range(2):
                        last = nc.scalar.activation(to[0:M, t % 2, h * NF:(h + 1) * NF],
                                                    ps_z[t % 2][0:M, h * NF:(h + 1) * NF], ACT.Exp,
                                                    bias=neg_max[0:M, t % 2, h:h + 1])
                last.then_inc(feat_ready, 1)

            def split_p(hp):
                act.wait_ge(raw_in["p"], hp * 16 + 16)
                for h in range(2):
                    r = slice(h * HD, (h + 1) * HD)
                    nc.scalar.copy(pj_hi[r, h * NF:(h + 1) * NF], raw_p[r, :]).then_inc(pj_hi_ready, 1)

            def keep_kvT(hp):
                act.wait_ge(kv_added, hp * NT + (NT + 2))
                nc.scalar.copy(kvT[:, :], ps_kv[0:VW, :]).then_inc(kvT_ready, 1)

            def keep_kv(hp):
                act.wait_ge(kv_turned, hp + 1)
                kv = ps_o[:, 0:4 * VW].rearrange("p (c w) -> p c w", w=VW)
                for h in range(2):
                    here, there = slice(h * HD, (h + 1) * HD), slice((1 - h) * HD, (2 - h) * HD)
                    nc.scalar.copy(kv_hi[:, 2 * h:2 * h + 2, here], kv[:, 2 * h:2 * h + 2, 0:HD])
                    last = nc.scalar.copy(kv_hi[:, 2 * h:2 * h + 2, there],
                                          kv[:, 2 * h:2 * h + 2, HD:HD + 1].to_broadcast([P, 2, HD]))
                last.then_inc(kv_hi_ready, 1)

            def keep_turned(hp, t):
                act.wait_ge(q_turned, hp * NT + (t + 3))
                s = t // 2
                act.wait_ge(out_done, hp * STEPS + max(s, 1))
                nc.scalar.copy(qf_hi[:, s % 2, :, half(t)], ps_t[t % 2][:, 0:4 * M].rearrange("p (c n) -> p c n", n=M)
                               ).then_inc(qf_hi_ready, 1)

            def keep_v(hp, g):
                a, b = TURNS[g]
                act.wait_ge(v_turned, hp * 3 + (g + 1))
                nc.scalar.copy(v_hi[0:M, a:b, :, 0:HD],
                               ps_kv[0:M, 0:(b - a) * P].rearrange("p (a h d) -> p a h d", h=2, d=HD)
                               ).then_inc(v_hi_ready, 1)

            def denominators(hp, s):
                act.wait_ge(out_done, hp * STEPS + (s + 2))
                nc.scalar.activation(den[0:HD, :], ps_o[HD:P, 0:PAIR], ACT.Copy, bias=EPS_Z)
                nc.scalar.activation(den[HD:P, :], ps_o[0:HD, PAIR:2 * PAIR], ACT.Copy,
                                     bias=EPS_Z).then_inc(den_ready, 1)

            def pair(hp, first=False, last=False):
                for s in range(STEPS):
                    features(hp, 2 * s, 2 * s)
                    features(hp, 2 * s + 1, 2 * s + 1)
                    for t in {1: (0,), 3: (1,), 4: (2,)}.get(s, ()):
                        keep("q", hp, t)
                    if s == 0 and not first:
                        denominators(hp - 1, STEPS - 1)
                for s in range(STEPS):
                    features(hp, 2 * s, NT + 2 * s)
                    features(hp, 2 * s + 1, NT + 2 * s + 1)
                    if s == 0:
                        keep_kvT(hp)
                    else:
                        if s == STEPS - 1 and not last:
                            act.wait_ge(z_done, hp * (2 * NT) + 2 * NT)
                            split_p(hp + 1)
                        keep_turned(hp, 2 * s - 2)
                        keep_turned(hp, 2 * s - 1)
                    if not last:
                        if s >= 3:
                            keep_v(hp + 1, s - 3)
                        for n, t in {0: (("v", 0),), 1: (("v", 1),), 2: (("v", 2),), 3: (("k", 0), ("k", 1)),
                                     4: (("k", 2),)}[s]:
                            keep(n, hp + 1, t)
                    if s == 0:
                        keep_kv(hp)
                    else:
                        denominators(hp, s - 1)
                if not last:
                    keep_v(hp + 1, 2)
                keep_turned(hp, NT - 2)
                keep_turned(hp, NT - 1)

            act.wait_ge(blank, 4)
            split_p(0)
            for n in "vk":
                for t in range(CT):
                    keep(n, 0, t)
            for g in range(3):
                keep_v(0, g)
            pair(0, first=True)
            with act.Fori(1, HP - 1) as hp:
                pair(hp)
            pair(HP - 1, last=True)
            denominators(HP - 1, STEPS - 1)

        @block.vector
        def _(dve):
            def split_w(n, hp):
                dve.wait_ge(w_hi_ready[n], hp + 1)
                nc.vector.tensor_tensor(w_lo[n][:, :, :], raw[n][:, :, :], w_hi[n][:, :, :].bitcast(F32),
                                        ALU.subtract).then_inc(w_ready[n], 1)

            def keep(n, hp, t):
                dve.wait_ge(t_hi_ready[n], hp * CT + (t + 1))
                nc.vector.tensor_tensor(t_lo[n][:, cols(t)], ps_g[BANKS[n][t][0]][:, 0:CW],
                                        t_hi[n][:, cols(t)].bitcast(F32), ALU.subtract).then_inc(t_ready[n], 1)

            def maximum(hp, t, i):
                dve.wait_ge(z_done, hp * (2 * NT) + (i + 1))
                nc.vector.tensor_reduce(neg_max[0:M, t % 2, :], ps_z[t % 2][0:M, :].rearrange("p (h f) -> p h f", h=2),
                                        AX_X, ALU.max, negate=True).then_inc(max_ready, 1)

            def split_k(hp, t):
                dve.wait_ge(feat_ready, hp * (2 * NT) + (t + 3))
                nc.vector.tensor_tensor(k_lo[0:M, t % 2, :], feat[0:M, t % 2, :], k_hi[0:M, t % 2, :].bitcast(F32),
                                        ALU.subtract).then_inc(k_ready, 1)

            def split_p(hp):
                dve.wait_ge(pj_hi_ready, hp * 2 + 2)
                for h in range(2):
                    r = slice(h * HD, (h + 1) * HD)
                    nc.vector.tensor_tensor(pj_lo[r, h * NF:(h + 1) * NF], raw_p[r, :],
                                            pj_hi[r, h * NF:(h + 1) * NF].bitcast(F32),
                                            ALU.subtract).then_inc(pj_ready, 1)

            def keep_kv(hp):
                dve.wait_ge(kv_hi_ready, hp + 1)
                kv = ps_o[:, 0:4 * VW].rearrange("p (c w) -> p c w", w=VW)
                for h in range(2):
                    here, there = slice(h * HD, (h + 1) * HD), slice((1 - h) * HD, (2 - h) * HD)
                    nc.vector.tensor_tensor(kv_lo[:, 2 * h:2 * h + 2, here], kv[:, 2 * h:2 * h + 2, 0:HD],
                                            kv_hi[:, 2 * h:2 * h + 2, here].bitcast(F32), ALU.subtract)
                    last = nc.vector.tensor_tensor(kv_lo[:, 2 * h:2 * h + 2, there],
                                                   kv[:, 2 * h:2 * h + 2, HD:HD + 1].to_broadcast([P, 2, HD]),
                                                   kv_hi[:, 2 * h:2 * h + 2, there].bitcast(F32), ALU.subtract)
                last.then_inc(kv_ready, 1)

            def keep_turned(hp, t):
                dve.wait_ge(qf_hi_ready, hp * NT + (t + 1))
                s = t // 2
                nc.vector.tensor_tensor(qf_lo[:, s % 2, :, half(t)], ps_t[t % 2][:, 0:4 * M].rearrange("p (c n) -> p c n", n=M),
                                        qf_hi[:, s % 2, :, half(t)].bitcast(F32), ALU.subtract).then_inc(qf_ready, 1)

            def keep_v(hp, g):
                a, b = TURNS[g]
                dve.wait_ge(v_hi_ready, hp * 3 + (g + 1))
                nc.vector.tensor_tensor(v_lo[0:M, a:b, :, 0:HD],
                                        ps_kv[0:M, 0:(b - a) * P].rearrange("p (a h d) -> p a h d", h=2, d=HD),
                                        v_hi[0:M, a:b, :, 0:HD].bitcast(F32), ALU.subtract).then_inc(v_ready, 1)

            def divide(hp, s):
                dve.wait_ge(den_ready, hp * STEPS + (s + 1))
                nc.vector.reciprocal(den[:, :], den[:, :]).then_inc(inv_ready, 1)
                dve.wait_ge(inv_ready, hp * STEPS + (s + 1))
                dve.wait_ge(att_split, hp * STEPS + (s + 1))
                nc.vector.tensor_tensor(att[0:HD, :], ps_o[0:HD, 0:PAIR], den[0:HD, :], ALU.mult)
                nc.vector.tensor_tensor(att[HD:P, :], ps_o[HD:P, PAIR:2 * PAIR], den[HD:P, :],
                                        ALU.mult).then_inc(att_ready, 1)

            def pair(hp, first=False, last=False):
                for s in range(STEPS):
                    maximum(hp, 2 * s, 2 * s)
                    maximum(hp, 2 * s + 1, 2 * s + 1)
                    if s < 2 and not first:
                        divide(hp - 1, STEPS - 2 + s)
                    split_k(hp, 2 * s)
                    split_k(hp, 2 * s + 1)
                    for t in {1: (0,), 3: (1,), 4: (2,)}.get(s, ()):
                        keep("q", hp, t)
                    if s == 1 and not first and not last:
                        split_w("k", hp + 1)
                for s in range(STEPS):
                    maximum(hp, 2 * s, NT + 2 * s)
                    maximum(hp, 2 * s + 1, NT + 2 * s + 1)
                    if s >= 2:
                        divide(hp, s - 2)
                    if s == 0:
                        keep_kv(hp)
                    else:
                        keep_turned(hp, 2 * s - 2)
                        keep_turned(hp, 2 * s - 1)
                    if not last:
                        if s == 1:
                            split_w("q", hp + 1)
                        if s >= 3:
                            keep_v(hp + 1, s - 3)
                        if s == STEPS - 1:
                            split_p(hp + 1)
                        if s == 3:
                            keep("k", hp + 1, 0)
                            split_w("v", hp + 2)
                            keep("k", hp + 1, 1)
                        if s == 4:
                            keep("k", hp + 1, 2)
                if not last:
                    keep_v(hp + 1, 2)
                keep_turned(hp, NT - 2)
                keep_turned(hp, NT - 1)

            for t, to in ((pj_hi, 0.0), (pj_lo, 0.0)):
                nc.vector.memset(t[:, :].bitcast(F32), to).then_inc(blank, 1)
            nc.vector.memset(v_hi[:, :, :, HD:HD + 1].bitcast(F32), 1.0)
            nc.vector.memset(v_hi[:, :, :, HD + 1:VW].bitcast(F32), 0.0).then_inc(blank, 1)
            nc.vector.memset(v_lo[:, :, :, HD:VW].bitcast(F32), 0.0).then_inc(blank, 1)
            dve.sem_inc(k_ready, 2)
            dve.sem_inc(att_ready, 1)
            for n in "vkq":
                split_w(n, 0)
            split_p(0)
            for t in range(CT):
                keep("k", 0, t)
            for g in range(3):
                keep_v(0, g)
            for n in "vk":
                split_w(n, 1)
            pair(0, first=True)
            with dve.Fori(1, HP - 1) as hp:
                pair(hp)
            pair(HP - 1, last=True)
            for s in (STEPS - 2, STEPS - 1):
                divide(HP - 1, s)

        @block.tensor
        def _(pe):
            def gemm(n, hp, first, count, start_up=False):
                for u in range(first, first + count):
                    t, k = divmod(u, KC)
                    bank, whose, ahead, c = BANKS[n][t]
                    if u == 0:
                        pe.wait_ge(w_ready[n], hp + 1)
                    if k == 0 and whose and not (start_up and whose == "q"):
                        pe.wait_ge(t_ready[whose], hp * CT + (ahead * CT + c))
                    out = ps_g[bank][:, 0:CW]
                    pe.matmul(out, w_hi[n][:, k, :], xT_hi[:, k, cols(t)], start=(k == 0), stop=False)
                    pe.matmul(out, w_hi[n][:, k, :], xT_lo[:, k, cols(t)], start=False, stop=False)
                    last = pe.matmul(out, w_lo[n][:, k, :], xT_hi[:, k, cols(t)], start=False, stop=(k == KC - 1))
                    if k == KC - 1:
                        last.then_inc(g_done[n], 1)

            def project(n, hp, t, i):
                pe.wait_ge(feat_ready, hp * (2 * NT) + (i + 1))
                if t % 4 == 0 or t == NT - 1:
                    pe.wait_ge(t_ready[n], hp * CT + min(CT, ((t + 4) * M - 1) // CW + 1))
                exact_product(pe, ps_z[t % 2][0:M, :],
                              [(t_hi[n][:, tile(t)], t_lo[n][:, tile(t)], pj_hi[:, :], pj_lo[:, :])]
                              ).then_inc(z_done, 1)

            def add_kv(hp, t):
                pe.wait_ge(k_ready, hp * NT + (t + 3))
                for h in range(2):
                    at = slice(h * NF, (h + 1) * NF)
                    for n, (l, r) in enumerate(((v_hi, k_hi), (v_lo, k_hi), (v_hi, k_lo))):
                        last = pe.matmul(ps_kv[0:VW, at], l[0:M, t, h, :], r[0:M, t % 2, at],
                                         start=(t == 0 and h == 0 and n == 0), stop=(t == NT - 1 and n == 2),
                                         skip_group_check=True)
                last.then_inc(kv_added, 1)

            def turn_kv(hp):
                pe.wait_ge(kvT_ready, hp + 1)
                pe.wait_ge(att_ready, hp * STEPS + 1)
                for f in range(4):
                    last = pe.transpose(ps_o[:, f * VW:(f + 1) * VW], kvT[:, f * P:(f + 1) * P], ident[0:VW, 0:VW])
                last.then_inc(kv_turned, 1)

            def turn_q(hp, t):
                pe.wait_ge(feat_ready, hp * (2 * NT) + (NT + t + 3))
                if t >= 2:
                    pe.wait_ge(qf_ready, hp * NT + (t - 1))
                for f in range(4):
                    last = pe.transpose(ps_t[t % 2][:, f * M:(f + 1) * M], feat[0:M, t % 2, f * P:(f + 1) * P],
                                        ident[0:M, 0:M])
                last.then_inc(q_turned, 1)

            def turn_v(hp, g):
                if g == 0:
                    pe.wait_ge(t_ready["v"], hp * CT + CT)
                else:
                    pe.wait_ge(v_ready, hp * 3 + g)
                a, b = TURNS[g]
                for n in range(a, b):
                    last = pe.transpose(ps_kv[0:M, (n - a) * P:(n - a + 1) * P], vT[:, tile(n)], ident[:, :])
                last.then_inc(v_turned, 1)

            def multiply(hp, s):
                pe.wait_ge(qf_ready, hp * NT + (2 * s + 2))
                if s == 0:
                    pe.wait_ge(kv_ready, hp + 1)
                pe.wait_ge(att_ready, hp * STEPS + (s + 1))
                for h in range(2):
                    last = exact_product(pe, ps_o[:, h * PAIR:(h + 1) * PAIR],
                                         [(kv_hi[:, f, :], kv_lo[:, f, :], qf_hi[:, s % 2, f, :], qf_lo[:, s % 2, f, :])
                                          for f in (2 * h, 2 * h + 1)])
                last.then_inc(out_done, 1)

            def pair(hp, first=False, last=False):
                for s in range(STEPS):
                    if s == 0:
                        pe.wait_ge(pj_ready, hp * 2 + 2)
                    project("k", hp, 2 * s, 2 * s)
                    project("k", hp, 2 * s + 1, 2 * s + 1)
                    if s == 1:
                        pe.wait_ge(v_ready, hp * 3 + 3)
                    if s:
                        add_kv(hp, 2 * s - 2)
                        add_kv(hp, 2 * s - 1)
                    gemm("q", hp, 5 * s, min(5, CT * KC - 5 * s))
                    if s == 0 and not first:
                        multiply(hp - 1, STEPS - 1)
                units = [("v", u) for u in range(CT * KC)] + [("k", u) for u in range(CT * KC)]
                for s in range(STEPS):
                    project("q", hp, 2 * s, NT + 2 * s)
                    project("q", hp, 2 * s + 1, NT + 2 * s + 1)
                    if s == 0:
                        add_kv(hp, NT - 2)
                        add_kv(hp, NT - 1)
                    else:
                        turn_q(hp, 2 * s - 2)
                        turn_q(hp, 2 * s - 1)
                    if not last:
                        if s >= 3:
                            turn_v(hp + 1, s - 3)
                        for n, u in units[10 * s:10 * s + 10]:
                            gemm(n, hp + 1, u, 1)
                    if s == 0:
                        turn_kv(hp)
                    else:
                        multiply(hp, s - 1)
                if not last:
                    turn_v(hp + 1, 2)
                turn_q(hp, NT - 2)
                turn_q(hp, NT - 1)

            pe.sem_inc(feat_ready, 2)
            pe.sem_inc(kv_added, 2)
            pe.sem_inc(q_turned, 2)
            pe.sem_inc(out_done, 1)
            pe.wait_ge(blank, 4)
            gemm("v", 0, 0, CT * KC, start_up=True)
            gemm("k", 0, 0, CT * KC, start_up=True)
            for g in range(3):
                turn_v(0, g)
            pair(0, first=True)
            with pe.Fori(1, HP - 1) as hp:
                pair(hp)
            pair(HP - 1, last=True)
            multiply(HP - 1, STEPS - 1)


def stage_sage1(nc, w_neigh, w_self, hT_hi_dram, hT_lo_dram, adj, inv_col, mid_dram):
    with ExitStack() as stack:
        m = Pool(nc, stack, "sage1")
        hT_hi = m.sb("hT_hi", [P, KC, N], F32R)
        hT_lo = m.sb("hT_lo", [P, KC, N], F32R)
        raw = {n: m.sb(f"raw_{n}", [P, KC, PW], F32) for n in "ns"}
        w_hi = {n: m.sb(f"w{n}_hi", [P, KC, PW], F32R) for n in "ns"}
        w_lo = {n: m.sb(f"w{n}_lo", [P, KC, PW], F32R) for n in "ns"}
        p_hi = m.sb("p_hi", [P, NT, PW], F32R)
        p_lo = m.sb("p_lo", [P, NT, PW], F32R)
        mean = m.sb("mean", [P, 2, PW], F32)
        mid = m.sb("mid", [P, 2, PW], F32)
        ps_p = [m.bank(f"ps_p{i}") for i in range(2)]
        ps_a = [m.bank(f"ps_a{i}") for i in range(2)]
        ps_s = [m.bank(f"ps_s{i}") for i in range(2)]
        h_in = [m.sem(f"h_in{i}") for i in range(PAIRS)]
        raw_in = {n: m.sem(f"raw_{n}_in") for n in "ns"}
        w_hi_ready = {n: m.sem(f"w{n}_hi_ready") for n in "ns"}
        w_ready = {n: m.sem(f"w{n}_ready") for n in "ns"}
        p_done = m.sem("p_done")
        p_hi_ready = m.sem("p_hi_ready")
        p_ready = m.sem("p_ready")
        agg_done = m.sem("agg_done")
        self_done = m.sem("self_done")
        mean_ready = m.sem("mean_ready")
        mid_ready = m.sem("mid_ready")
        mid_out = [m.sem(f"mid_out{i}") for i in range(2)]
        block = stack.enter_context(nc.Block())
        NPAN = D // PW
        tile = lambda t: slice(t * M, (t + 1) * M)

        @block.sync
        def _(sp):
            def load_w(n, j):
                sp.dma_start(raw[n][:, :, :], panel(w_neigh if n == "n" else w_self, j, PW)).then_inc(raw_in[n], 16)

            load_w("n", 0)
            for i in range(PAIRS):
                at = slice(2 * i * M, 2 * (i + 1) * M)
                for part, dram in ((hT_hi, hT_hi_dram), (hT_lo, hT_lo_dram)):
                    sp.dma_start(part[:, :, at].bitcast(F32), dram[:, at].rearrange("(c p) n -> p c n", p=P)
                                 ).then_inc(h_in[i], 16)
                if i == 1:
                    load_w("s", 0)

            def step(j, last=False):
                if not last:
                    for n in "ns":
                        sp.wait_ge(w_ready[n], j + 1)
                        load_w(n, j + 1)
                for t in range(NT):
                    sp.wait_ge(mid_ready, j * NT + (t + 3))
                    sp.dma_start(mid_dram[tile(t), ds(j * PW, PW)], mid[0:M, t % 2, :]).then_inc(mid_out[t % 2], 16)

            with sp.Fori(0, NPAN - 1) as j:
                step(j)
            step(NPAN - 1, last=True)
            for i in range(2):
                sp.wait_ge(mid_out[i], 16 * (NPAN * NT // 2 + 1))

        @block.scalar
        def _(act):
            def split_w(n, j):
                act.wait_ge(raw_in[n], j * 16 + 16)
                nc.scalar.copy(w_hi[n][:, :, :], raw[n][:, :, :]).then_inc(w_hi_ready[n], 1)

            def step(j, last=False):
                for t in range(NT):
                    act.wait_ge(p_done, j * NT + (t + 1))
                    nc.scalar.copy(p_hi[0:M, t, :], ps_p[t % 2][0:M, 0:PW]).then_inc(p_hi_ready, 1)
                    if t == NT // 2:
                        split_w("s", j)
                if not last:
                    split_w("n", j + 1)
                for t in range(NT):
                    act.wait_ge(agg_done, j * NT + (t + 1))
                    act.wait_ge(mid_ready, j * NT + (t + 1))
                    nc.scalar.activation(mean[0:M, t % 2, :], ps_a[t % 2][0:M, 0:PW], ACT.Copy,
                                         scale=inv_col[0:M, t:t + 1]).then_inc(mean_ready, 1)

            split_w("n", 0)
            with act.Fori(0, NPAN - 1) as j:
                step(j)
            step(NPAN - 1, last=True)

        @block.vector
        def _(dve):
            def split_w(n, j):
                dve.wait_ge(w_hi_ready[n], j + 1)
                nc.vector.tensor_tensor(w_lo[n][:, :, :], raw[n][:, :, :], w_hi[n][:, :, :].bitcast(F32),
                                        ALU.subtract).then_inc(w_ready[n], 1)

            def step(j, last=False):
                for t in range(NT):
                    dve.wait_ge(p_hi_ready, j * NT + (t + 1))
                    nc.vector.tensor_tensor(p_lo[0:M, t, :], ps_p[t % 2][0:M, 0:PW], p_hi[0:M, t, :].bitcast(F32),
                                            ALU.subtract).then_inc(p_ready, 1)
                    if t == NT // 2:
                        split_w("s", j)
                if not last:
                    split_w("n", j + 1)
                for t in range(NT):
                    dve.wait_ge(self_done, j * NT + (t + 1))
                    dve.wait_ge(mean_ready, j * NT + (t + 1))
                    dve.wait_ge(mid_out[t % 2], j * (16 * NT // 2) + 16 * (t // 2 + 1))
                    nc.vector.tensor_tensor(mid[0:M, t % 2, :], ps_s[t % 2][0:M, 0:PW], mean[0:M, t % 2, :],
                                            ALU.add).then_inc(mid_ready, 1)

            dve.sem_inc(p_ready, 2)
            dve.sem_inc(mid_ready, 2)
            for i in range(2):
                dve.sem_inc(mid_out[i], 16)
            split_w("n", 0)
            with dve.Fori(0, NPAN - 1) as j:
                step(j)
            step(NPAN - 1, last=True)

        @block.tensor
        def _(pe):
            def dense(out, n, t):
                return exact_product(pe, out, [(hT_hi[:, k, tile(t)], hT_lo[:, k, tile(t)], w_hi[n][:, k, :],
                                                w_lo[n][:, k, :]) for k in range(KC)])

            with pe.Fori(0, NPAN) as j:
                pe.wait_ge(w_ready["n"], j + 1)
                for t in range(NT):
                    if t % 2 == 0:
                        pe.wait_ge(h_in[t // 2], 32)
                    pe.wait_ge(p_ready, j * NT + (t + 1))
                    dense(ps_p[t % 2][0:M, 0:PW], "n", t).then_inc(p_done, 1)
                pe.wait_ge(w_ready["s"], j + 1)
                for t in range(NT):
                    pe.wait_ge(mid_ready, j * NT + (t + 1))
                    dense(ps_s[t % 2][0:M, 0:PW], "s", t).then_inc(self_done, 1)
                    if t == 0:
                        pe.wait_ge(p_ready, j * NT + (NT + 2))
                    for a in range(NT):
                        pe.matmul(ps_a[t % 2][0:M, 0:PW], adj[0:M, a, tile(t)], p_hi[0:M, a, :],
                                  start=(a == 0), stop=False)
                        last = pe.matmul(ps_a[t % 2][0:M, 0:PW], adj[0:M, a, tile(t)], p_lo[0:M, a, :],
                                         start=False, stop=(a == NT - 1))
                    last.then_inc(agg_done, 1)


def stage_mix(nc, w_out, b_graph, b_out, x, oT_hi_dram, oT_lo_dram, mid_dram, ident_b, x1_dram, qT, unit_x,
              w1T, w1T_dram, w2T, w2T_dram):
    with ExitStack() as stack:
        m = Pool(nc, stack, "mix")
        raw = m.sb("raw", [P, D // PW, KC, PW], F32)
        w_hi = m.sb("w_hi", [P, KC, D], F32R)
        w_lo = m.sb("w_lo", [P, KC, D], F32R)
        bias = m.sb("bias", [P, 2, D], F32)
        o_hi = m.sb("o_hi", [P, 2, KC, M], F32R)
        o_lo = m.sb("o_lo", [P, 2, KC, M], F32R)
        mid = m.sb("mid", [P, 2, D], F32)
        x_in = m.sb("x_in", [P, 2, D], F32)
        x1 = m.sb("x1", [P, 2, D], F32)
        y = m.sb("y", [P, D], F32)
        code = m.sb("code", [P, D], BF16)
        stats = m.sb("stats", [P, 2, 6], F32)
        mv = m.sb("mv", [P, 2], F32)
        rs = m.sb("rs", [P, 6], F32)
        big = m.sb("big", [P, 3], F32)
        ps_x = [m.bank(f"ps_x{i}") for i in range(4)]
        ps_t = m.psum("ps_t", [P, 2 * BANK], BF16)
        ffn_in = m.sem("ffn_in")
        raw_in = [m.sem(f"raw_in{i}") for i in range(D // PW)]
        bias_in = m.sem("bias_in")
        bias_ready = m.sem("bias_ready")
        w_hi_ready = m.sem("w_hi_ready")
        w_ready = m.sem("w_ready")
        o_in = [m.sem(f"o_in{b}") for b in range(2)]
        m_in = [m.sem(f"m_in{b}") for b in range(2)]
        sum_ready = m.sem("sum_ready")
        base_ready = m.sem("base_ready")
        x_done = m.sem("x_done")
        x1_ready = m.sem("x1_ready")
        x1_out = [m.sem(f"x1_out{b}") for b in range(2)]
        var_ready = m.sem("var_ready")
        root_ready = m.sem("root_ready")
        seen = m.sem("seen")
        code_ready = m.sem("code_ready")
        turned = m.sem("turned")
        kept = m.sem("kept")
        chain = m.sem("chain")
        block = stack.enter_context(nc.Block())
        NPAN = D // PW
        row = lambda v: v.rearrange("(a n) -> a n", a=1).to_broadcast([P, D])

        @block.sync
        def _(sp):
            def load_w(j):
                sp.dma_start(raw[:, j, :, :], panel(w_out, j, PW)).then_inc(raw_in[j], 16)

            def load_o(t, b):
                sp.dma_start(o_hi[:, b, :, :].bitcast(F32), oT_hi_dram[:, ds(t * M, M)].rearrange("(c p) n -> p c n", p=P)).then_inc(o_in[b], 16)
                sp.dma_start(o_lo[:, b, :, :].bitcast(F32), oT_lo_dram[:, ds(t * M, M)].rearrange("(c p) n -> p c n", p=P)).then_inc(o_in[b], 16)

            def load_m(t, b):
                sp.dma_start(mid[0:M, b, :], mid_dram[ds(t * M, M), :]).then_inc(m_in[b], 16)
                sp.dma_start(x_in[0:M, b, :], x[ds(t * M, M), :]).then_inc(m_in[b], 16)

            load_w(0)
            load_w(1)
            load_o(0, 0)
            load_w(2)
            load_w(3)
            load_o(1, 1)
            for i, v in enumerate((b_graph, b_out)):
                sp.dma_start(bias[:, i, :], row(v)).then_inc(bias_in, 16)
            for b in range(2):
                load_m(b, b)
            for to, what in ((w1T, w1T_dram), (w2T, w2T_dram)):
                sp.dma_start(to[:, :, :], what).then_inc(ffn_in, 16)

            def pair(i, last=False):
                for b in range(2):
                    sp.wait_ge(x1_ready, i * 4 + (2 * b + 6))
                    sp.dma_start(x1_dram[ds(i * (2 * M) + b * M, M), :], x1[0:M, b, :]).then_inc(x1_out[b], 16)
                    if not last:
                        load_o(i * 2 + (b + 2), b)
                        load_m(i * 2 + (b + 2), b)

            with sp.Fori(0, PAIRS - 1) as i:
                pair(i)
            pair(PAIRS - 1, last=True)
            sp.wait_ge(ffn_in, 32)
            for b in range(2):
                sp.wait_ge(x1_out[b], 16 * (PAIRS + 1))

        @block.gpsimd
        def _(pool):
            pool.wait_ge(bias_in, 32)
            nc.gpsimd.tensor_tensor(bias[:, 0, :], bias[:, 0, :], bias[:, 1, :], ALU.add).then_inc(bias_ready, 1)
            pool.wait_ge(bias_ready, 1)
            with pool.Fori(0, PAIRS) as i:
                for b in range(2):
                    pool.wait_ge(m_in[b], i * 32 + 32)
                    nc.gpsimd.tensor_tensor(mid[0:M, b, :], mid[0:M, b, :], x_in[0:M, b, :], ALU.add).then_inc(sum_ready, 1)
                    pool.wait_ge(sum_ready, i * 2 + (b + 1))
                    nc.gpsimd.tensor_tensor(mid[0:M, b, :], mid[0:M, b, :], bias[0:M, 0, :], ALU.add).then_inc(base_ready, 1)

        @block.scalar
        def _(act):
            for j in range(NPAN):
                act.wait_ge(raw_in[j], 16)
                nc.scalar.copy(w_hi[:, :, j * PW:(j + 1) * PW], raw[:, j, :, :]).then_inc(w_hi_ready, 1)

            def root(t):
                act.wait_ge(var_ready, t + 1)
                nc.scalar.activation(rs[0:M, 1:2], rs[0:M, 0:1], ACT.Sqrt).then_inc(root_ready, 1)

            def keep(t):
                act.wait_ge(turned, t + 2)
                nc.scalar.copy(qT[:, :, ds(t * M, M)], ps_t[:, :].rearrange("p (c n) -> p c n", n=P)[:, :, 0:M]).then_inc(kept, 1)

            root(0)
            root(1)
            keep(0)
            with act.Fori(1, PAIRS) as i:
                for b in range(2):
                    root(i * 2 + b)
                    keep(i * 2 + (b - 1))
            keep(NT - 1)

        @block.vector
        def _(dve):
            for b in range(2):
                dve.sem_inc(x1_out[b], 16)
            for j in range(NPAN):
                dve.wait_ge(w_hi_ready, j + 1)
                nc.vector.tensor_tensor(w_lo[:, :, j * PW:(j + 1) * PW], raw[:, j, :, :],
                                        w_hi[:, :, j * PW:(j + 1) * PW].bitcast(F32), ALU.subtract).then_inc(w_ready, 1)
            LINKS = 15
            with dve.Fori(0, PAIRS) as i:
                for b in range(2):
                    c0 = i * (2 * LINKS) + b * LINKS
                    at = [0]

                    def link(ins):
                        at[0] += 1
                        ins.then_inc(chain, 1)
                        dve.wait_ge(chain, c0 + at[0])

                    dve.wait_ge(base_ready, i * 2 + (b + 1))
                    dve.wait_ge(x1_out[b], i * 16 + 16)
                    for h in range(2):
                        dve.wait_ge(x_done, i * 4 + (2 * b + h + 1))
                        nc.vector.tensor_tensor(x1[0:M, b, h * BANK:(h + 1) * BANK], ps_x[2 * b + h][0:M, :],
                                                mid[0:M, b, h * BANK:(h + 1) * BANK], ALU.add).then_inc(x1_ready, 1)
                        dve.wait_ge(x1_ready, i * 4 + (2 * b + h + 5))
                        nc.vector.bn_stats(stats[0:M, h, :], x1[0:M, b, h * BANK:(h + 1) * BANK]).then_inc(chain, 1)
                        at[0] += 1
                    dve.wait_ge(chain, c0 + 2)
                    dve.sem_inc(seen, 1)
                    link(nc.vector.bn_aggr(mv[0:M, :], stats[0:M, :, :]))
                    nc.vector.tensor_scalar(rs[0:M, 0:1], mv[0:M, 1:2], EPS_LN, None, ALU.add).then_inc(var_ready, 1)
                    dve.wait_ge(root_ready, i * 2 + (b + 1))
                    link(nc.vector.reciprocal(rs[0:M, 2:3], rs[0:M, 1:2]))
                    link(nc.vector.tensor_tensor(rs[0:M, 3:4], rs[0:M, 2:3], rs[0:M, 2:3], ALU.mult))
                    link(nc.vector.tensor_tensor(rs[0:M, 4:5], rs[0:M, 3:4], rs[0:M, 0:1], ALU.mult))
                    link(nc.vector.tensor_scalar(rs[0:M, 4:5], rs[0:M, 4:5], -0.5, 1.5, ALU.mult, ALU.add))
                    link(nc.vector.tensor_tensor(rs[0:M, 5:6], rs[0:M, 4:5], rs[0:M, 2:3], ALU.mult))
                    link(nc.vector.tensor_scalar(y[0:M, :], x1[0:M, b, :], mv[0:M, 0:1], rs[0:M, 5:6],
                                                 ALU.subtract, ALU.mult))
                    link(nc.vector.tensor_reduce(big[0:M, 0:1], y[0:M, :], AX_X, ALU.max, apply_absolute_value=True))
                    link(nc.vector.tensor_scalar(big[0:M, 1:2], big[0:M, 0:1], EPS_Q, None, ALU.max))
                    link(nc.vector.reciprocal(big[0:M, 2:3], big[0:M, 1:2]))
                    link(nc.vector.tensor_scalar(big[0:M, 2:3], big[0:M, 2:3], 127.0, None, ALU.mult))
                    nc.vector.tensor_scalar(unit_x[0:M, ds(i * 2 + b, 1)], big[0:M, 1:2], 1.0 / 127.0, None, ALU.mult)
                    link(nc.vector.tensor_scalar(y[0:M, :], y[0:M, :], big[0:M, 2:3], ROUND, ALU.mult, ALU.add))
                    link(nc.vector.tensor_scalar(y[0:M, :], y[0:M, :], ROUND, 127.0, ALU.subtract, ALU.min))
                    dve.wait_ge(turned, i * 2 + (b + 1))
                    nc.vector.tensor_scalar(code[0:M, :], y[0:M, :], -128.0, None, ALU.max).then_inc(code_ready, 1)
                    assert at[0] == LINKS

        @block.tensor
        def _(pe):
            def products(i, b):
                pe.wait_ge(o_in[b], i * 32 + 32)
                for h in range(2):
                    pe.wait_ge(w_ready, NPAN // 2 * (h + 1))
                    pe.wait_ge(x1_ready, i * 4 + (2 * b + h + 1))
                    exact_product(pe, ps_x[2 * b + h][0:M, :],
                                  [(o_hi[:, b, k, :], o_lo[:, b, k, :], w_hi[:, k, h * BANK:(h + 1) * BANK],
                                    w_lo[:, k, h * BANK:(h + 1) * BANK]) for k in range(KC)]).then_inc(x_done, 1)

            def turn(t):
                pe.wait_ge(code_ready, t + 1)
                pe.wait_ge(kept, t + 1)
                for k in range(KC):
                    last = pe.transpose(ps_t[:, k * P:k * P + M], code[0:M, k * P:(k + 1) * P], ident_b[0:M, 0:M])
                last.then_inc(turned, 1)

            pe.sem_inc(x1_ready, 4)
            pe.sem_inc(turned, 1)
            pe.sem_inc(kept, 1)
            products(0, 0)
            products(0, 1)
            turn(0)
            with pe.Fori(1, PAIRS) as i:
                for b in range(2):
                    products(i, b)
                    turn(i * 2 + (b - 1))
            turn(NT - 1)


def stage_ffn(nc, conv_w, conv_b, x1_dram, out, ident, ident_b, w1T, w2T, unit_w, qT, unit_x):
    with ExitStack() as stack:
        m = Pool(nc, stack, "ffn")
        cw = m.sb("cw", [P, HC, 3], F32)
        cb = m.sb("cb", [P, HC], F32)
        x1 = m.sb("x1", [P, NT, D], F32)
        step_x = m.sb("step_x", [P, NT], F32)
        step_row = m.sb("step_row", [P, N], F32)
        h = m.sb("h", [P, HC, N + 2], F32)
        mixed = m.sb("mixed", [P, 2, N], F32)
        s = m.sb("s", [P, HC, N], F32)
        big = m.sb("big", [P, 4, 4], F32)
        y = m.sb("y", [P, 2, HID], F32)
        code = m.sb("code", [P, 2, HID], BF16)
        codeT = m.sb("codeT", [P, 2, HC, M], BF16)
        res = m.sb("res", [P, 2, D], F32)
        ps_h = [m.bank(f"ps_h{i}") for i in range(CT)]
        ps_s = [m.bank(f"ps_s{i}") for i in range(2)]
        ps_c = m.psum("ps_c", [P, 2 * BANK], BF16)
        ps_o = [m.bank(f"ps_o{i}") for i in range(2)]
        w_in = m.sem("w_in")
        x1_in = m.sem("x1_in")
        step_ready = m.sem("step_ready")
        spread = m.sem("spread")
        row_ready = m.sem("row_ready")
        edge_ready = m.sem("edge_ready")
        h_done = m.sem("h_done")
        h_ready = m.sem("h_ready")
        mid_ready = m.sem("mid_ready")
        conv_ready = m.sem("conv_ready")
        s_ready = m.sem("s_ready")
        s_turned = m.sem("s_turned")
        scale_ready = m.sem("scale_ready")
        y_ready = m.sem("y_ready")
        code_ready = m.sem("code_ready")
        c_turned = m.sem("c_turned")
        c_kept = m.sem("c_kept")
        o_done = m.sem("o_done")
        res_ready = m.sem("res_ready")
        res_out = [m.sem(f"res_out{b}") for b in range(2)]
        chain = m.sem("chain")
        block = stack.enter_context(nc.Block())
        WIDTH = (CW, CW, N - 2 * CW)
        cols = lambda t, off=0: slice(t * CW + off, t * CW + off + WIDTH[t])

        @block.sync
        def _(sp):
            with nc.allow_non_contiguous_dma(reason="a few words a partition"):
                sp.dma_start(cw[:, :, :], conv_w.rearrange("(c p) a w -> p c (a w)", p=P)).then_inc(w_in, 16)
                sp.dma_start(cb[:, :], conv_b.rearrange("(c p) -> p c", p=P)).then_inc(w_in, 16)
            sp.dma_start(x1[0:M, :, :], x1_dram.rearrange("(t p) d -> p t d", p=M)).then_inc(x1_in, 16)
            for t in range(NT):
                sp.wait_ge(res_ready, 2 * t + 4)
                sp.dma_start(out[t * M:(t + 1) * M, :], res[0:M, t % 2, :]).then_inc(res_out[t % 2], 16)
            for b in range(2):
                sp.wait_ge(res_out[b], 16 * (PAIRS + 1))

        @block.tensor
        def _(pe):
            pe.wait_ge(step_ready, 1)
            for t in range(NT):
                g = t // 4
                last = pe.matmul(ps_h[g][:, (t % 4) * M:(t % 4 + 1) * M], step_x[0:M, t:t + 1].to_broadcast([M, P]),
                                 ident[0:M, 0:M], start=True, stop=True)
                if t % 4 == 3 or t == NT - 1:
                    last.then_inc(spread, 1)
            for c in range(HC):
                for t in range(CT):
                    if c == 0:
                        pe.wait_ge(row_ready, t + 1)
                    else:
                        pe.wait_ge(h_ready, (c - 1) * CT + t + 1)
                    for k in range(KC):
                        last = pe.matmul(ps_h[t][:, 0:WIDTH[t]], w1T[:, k, c * P:(c + 1) * P], qT[:, k, cols(t)],
                                         start=(k == 0), stop=(k == KC - 1))
                    last.then_inc(h_done, 1)

            def turn_s(t):
                pe.wait_ge(y_ready, t + 1)
                for c in range(HC):
                    last = pe.transpose(ps_s[t % 2][0:M, c * P:(c + 1) * P], s[:, c, t * M:(t + 1) * M], ident[:, :])
                last.then_inc(s_turned, 1)

            def turn_code(t):
                pe.wait_ge(code_ready, t + 1)
                pe.wait_ge(c_kept, t + 1)
                for c in range(HC):
                    last = pe.transpose(ps_c[:, c * P:c * P + M], code[0:M, t % 2, c * P:(c + 1) * P],
                                        ident_b[0:M, 0:M])
                last.then_inc(c_turned, 1)

            def products(t):
                pe.wait_ge(c_kept, t + 2)
                for half in range(2):
                    pe.wait_ge(res_ready, t * 2 + half + 1)
                    for c in range(HC):
                        last = pe.matmul(ps_o[half][0:M, :], codeT[:, t % 2, c, :], w2T[:, c, half * BANK:(half + 1) * BANK],
                                         start=(c == 0), stop=(c == HC - 1))
                    last.then_inc(o_done, 1)

            pe.wait_ge(s_ready, HC)
            turn_s(0)
            turn_s(1)
            for t in range(NT):
                turn_code(t)
                if t + 2 < NT:
                    turn_s(t + 2)
                products(t)

        @block.scalar
        def _(act):
            act.sem_inc(c_kept, 1)
            act.sem_inc(y_ready, 2)

            def silu(c):
                act.wait_ge(conv_ready, c + 1)
                nc.scalar.activation(s[:, c, :], mixed[:, c % 2, :], ACT.Silu).then_inc(s_ready, 1)

            for g, (a, b) in enumerate(TURNS):
                act.wait_ge(spread, g + 1)
                nc.scalar.copy(step_row[:, a * M:b * M], ps_h[g][:, 0:(b - a) * M]).then_inc(row_ready, 1)
            act.wait_ge(w_in, 32)
            for c in range(HC):
                act.wait_ge(h_ready, (c + 1) * CT)
                if c >= 2:
                    act.wait_ge(s_ready, c - 1)
                nc.scalar.activation(mixed[:, c % 2, :], h[:, c, 1:N + 1], ACT.Identity, bias=cb[:, c:c + 1],
                                     scale=cw[:, c, 1:2]).then_inc(mid_ready, 1)
                if c >= 1:
                    silu(c - 1)
            silu(HC - 1)

            def steps(t):
                act.wait_ge(scale_ready, t + 1)
                nc.scalar.activation(y[0:M, t % 2, :], ps_s[t % 2][0:M, :], ACT.Copy, bias=ROUND,
                                     scale=big[0:M, t % 4, 2:3]).then_inc(y_ready, 1)

            steps(0)
            for t in range(NT):
                act.wait_ge(c_turned, t + 1)
                nc.scalar.copy(codeT[:, t % 2, :, :],
                               ps_c[:, 0:HC * P].rearrange("p (c n) -> p c n", n=P)[:, :, 0:M]).then_inc(c_kept, 1)
                if t + 1 < NT:
                    steps(t + 1)

        @block.vector
        def _(dve):
            link = chained(dve, chain)
            link(nc.vector.tensor_scalar(step_x[0:M, :], unit_x[0:M, :], unit_w[0:M, 0:1], None, ALU.mult))
            dve.sem_inc(step_ready, 1)
            nc.vector.memset(h[:, :, 0:1], 0.0)
            link(nc.vector.memset(h[:, :, N + 1:N + 2], 0.0))
            dve.sem_inc(res_ready, 2)
            for b in range(2):
                dve.sem_inc(res_out[b], 16)
            dve.wait_ge(w_in, 32)
            dve.wait_ge(row_ready, CT)

            def scale_h(c):
                for t in range(CT):
                    dve.wait_ge(h_done, c * CT + t + 1)
                    nc.vector.tensor_tensor(h[:, c, cols(t, 1)], ps_h[t][:, 0:WIDTH[t]], step_row[:, cols(t)],
                                            ALU.mult).then_inc(h_ready, 1)

            def convolve(c):
                dve.wait_ge(mid_ready, c + 1)
                link(nc.vector.scalar_tensor_tensor(mixed[:, c % 2, :], h[:, c, 0:N], cw[:, c, 0:1], mixed[:, c % 2, :],
                                                    ALU.mult, ALU.add))
                nc.vector.scalar_tensor_tensor(mixed[:, c % 2, :], h[:, c, 2:N + 2], cw[:, c, 2:3], mixed[:, c % 2, :],
                                               ALU.mult, ALU.add).then_inc(conv_ready, 1)

            scale_h(0)
            for c in range(HC):
                if c + 1 < HC:
                    scale_h(c + 1)
                convolve(c)

            def scale(t):
                b = t % 4
                dve.wait_ge(s_turned, t + 1)
                link(nc.vector.tensor_reduce(big[0:M, b, 0:1], ps_s[t % 2][0:M, :], AX_X, ALU.max,
                                             apply_absolute_value=True))
                link(nc.vector.tensor_scalar(big[0:M, b, 1:2], big[0:M, b, 0:1], EPS_Q, None, ALU.max))
                link(nc.vector.reciprocal(big[0:M, b, 2:3], big[0:M, b, 1:2]))
                nc.vector.tensor_scalar(big[0:M, b, 2:3], big[0:M, b, 2:3], 127.0, None, ALU.mult).then_inc(scale_ready, 1)
                link(nc.vector.tensor_scalar(big[0:M, b, 3:4], big[0:M, b, 1:2], unit_w[0:M, 1:2], 1.0 / 127.0,
                                             ALU.mult, ALU.mult))

            def codes(t):
                b = t % 2
                dve.wait_ge(y_ready, t + 3)
                link(nc.vector.tensor_scalar(y[0:M, b, :], y[0:M, b, :], ROUND, 127.0, ALU.subtract, ALU.min))
                nc.vector.tensor_scalar(code[0:M, b, :], y[0:M, b, :], -128.0, None, ALU.max).then_inc(code_ready, 1)

            def result(t):
                b = t % 2
                dve.wait_ge(res_out[b], 16 * (t // 2 + 1))
                for half in range(2):
                    dve.wait_ge(o_done, t * 2 + half + 1)
                    nc.vector.scalar_tensor_tensor(res[0:M, b, half * BANK:(half + 1) * BANK], ps_o[half][0:M, :],
                                                   big[0:M, t % 4, 3:4], x1[0:M, t, half * BANK:(half + 1) * BANK],
                                                   ALU.mult, ALU.add).then_inc(res_ready, 1)

            scale(0)
            codes(0)
            dve.wait_ge(x1_in, 16)
            for t in range(NT):
                if t + 1 < NT:
                    scale(t + 1)
                if t:
                    result(t - 1)
                if t + 1 < NT:
                    codes(t + 1)
            result(NT - 1)




def program(nc, x, src, dst, W_self0, W_neigh0, b0, W_self1, W_neigh1, b1, w_qkv, w_out, b_out, proj,
            ffn_w1, ffn_conv_w, ffn_conv_b, ffn_w2, out):
    def dram(name, shape, dt=F32):
        return nc.dram_tensor(name, shape, dt, kind="Internal").ap()

    edges_pad = dram("edges_pad", (2, E + ECAP), I32)
    adj_dram = dram("adj_dram", (M, NT, NP))
    hT_hi, hT_lo = dram("hT_hi", (D, NP)), dram("hT_lo", (D, NP))
    oT_hi, oT_lo = dram("oT_hi", (D, N)), dram("oT_lo", (D, N))
    mid, x1 = dram("mid", (N, D)), dram("x1", (N, D))
    w1T_dram, w2T_dram = dram("w1T", (P, KC, HID), BF16), dram("w2T", (P, HC, D), BF16)
    with ExitStack() as stack:
        m = Pool(nc, stack, "all")
        ident = m.sb("ident", [P, P], F32)
        ident_b = m.sb("ident_b", [P, P], BF16)
        ones_r = m.sb("ones_r", [P, P], F32R)
        unit_w = m.sb("unit_w", [P, 2], F32)
        with ExitStack() as graph:
            m = Pool(nc, graph, "graph_out")
            inv_row = m.sb("inv_row", [P, NP], F32, side="right")
            inv_col = m.sb("inv_col", [P, NT], F32, side="right")
            with ExitStack() as nodes:
                m = Pool(nc, nodes, "xn")
                xT_hi = m.sb("xT_hi", [P, KC, NP], F32R)
                xT_lo = m.sb("xT_lo", [P, KC, NP], F32R)
                with ExitStack() as edges:
                    work = EdgeWork(Pool(nc, edges, "edges"))
                    stage_prepare(nc, x, src, dst, edges_pad, ffn_w1, ffn_w2, ident, ident_b, ones_r, xT_hi, xT_lo,
                                  work, w1T_dram, w2T_dram, unit_w)
                    stage_graph(nc, work, ident, ones_r, adj_dram, inv_row, inv_col)
                stage_attention(nc, w_qkv, proj, xT_hi, xT_lo, ident, oT_hi, oT_lo)
                adj = Pool(nc, graph, "adj").sb("adj", [P, NT, NP], F32R, side="right")
                stage_sage0(nc, W_neigh0, W_self0, b0, xT_hi, xT_lo, adj_dram, adj, inv_row, ident, hT_hi, hT_lo)
            stage_sage1(nc, W_neigh1, W_self1, hT_hi, hT_lo, adj, inv_col, mid)
        m = Pool(nc, stack, "codes")
        qT = m.sb("qT", [P, KC, N], BF16)
        unit_x = m.sb("unit_x", [P, NT], F32)
        w1T = m.sb("w1T", [P, KC, HID], BF16)
        w2T = m.sb("w2T", [P, HC, D], BF16)
        stage_mix(nc, w_out, b1, b_out, x, oT_hi, oT_lo, mid, ident_b, x1, qT, unit_x,
                  w1T, w1T_dram, w2T, w2T_dram)
        stage_ffn(nc, ffn_conv_w, ffn_conv_b, x1, out, ident, ident_b, w1T, w2T, unit_w, qT, unit_x)


INPUTS = ["x", "src", "dst", "L0_gnn_W_self0", "L0_gnn_W_neigh0", "L0_gnn_b0", "L0_gnn_W_self1", "L0_gnn_W_neigh1",
          "L0_gnn_b1", "L0_mix_w_qkv", "L0_mix_w_out", "L0_mix_b_out", "L0_mix_proj", "L0_ffn_w1", "L0_ffn_conv_w",
          "L0_ffn_conv_b", "L0_ffn_w2"]


def kernel(**inputs):
    import numpy as np
    import concourse.bacc as bacc
    from concourse.bass_utils import run_bass_kernel_spmd

    nc = bacc.Bacc("TRN2", target_bir_lowering=False, num_devices=1)
    arrays = {f"in_{name}": np.ascontiguousarray(inputs[name]) for name in INPUTS}
    args = [nc.dram_tensor(name, a.shape, mybir.dt.from_np(a.dtype), kind="ExternalInput").ap()
            for name, a in arrays.items()]
    out = nc.dram_tensor("out", (N, D), F32, kind="ExternalOutput").ap()
    program(nc, *args, out)
    run = run_bass_kernel_spmd(nc, [arrays], core_ids=[0])
    return run.results[0]["out"]
```

```python
from contextlib import ExitStack

import concourse.bass as bass
from concourse import mybir

F32 = mybir.dt.float32
F32R = mybir.dt.float32r
BF16 = mybir.dt.bfloat16
I32 = mybir.dt.int32
ALU = mybir.AluOpType
ACT = mybir.ActivationFunctionType
AX_X = mybir.AxisListType.X
ds = bass.ds

N, D, E = 1250, 1024, 20000
P = 128
M = 125
NT = N // M
M_EVEN = 112
KC = D // P
CT = 3
CW = 418
NP = CT * CW
BANK = 512
EPS_LN = 1e-5

TURNS = ((0, 4), (4, 8), (8, NT))
W = 25
NW = N // W
HALF_W = NW // 2 + 1
LAST_W = 42
GROUPS = ((0, 16), (16, 36), (36, NW))
WC = NT * W
EC = 4
ECAP = EC * P
ER = E // M
GC = 8
ROUND = 12582912.0
PW = 256
HID = 512
HC = HID // P
EPS_Q = 1e-5
PAIRS = NT // 2


def chained(engine, sem):
    count = [0]

    def link(ins):
        count[0] += 1
        ins.then_inc(sem, 1)
        engine.wait_ge(sem, count[0])

    return link


class Pool:

    def __init__(self, nc, stack, tag):
        self.nc, self.stack, self.tag, self.sems = nc, stack, tag, []
        stack.callback(self.close)

    def close(self):
        if self.sems:
            self.nc.clear_and_free_semaphores(self.sems)
            self.nc.all_engine_barrier()

    def sb(self, name, shape, dt, side="left"):
        return self.stack.enter_context(self.nc.sbuf_tensor(f"{self.tag}_{name}", shape, dt, side=side))

    def psum(self, name, shape, dt=F32):
        return self.stack.enter_context(self.nc.psum_tensor(f"{self.tag}_{name}", shape, dt))

    def bank(self, name):
        return self.psum(name, [P, BANK])

    def sem(self, name):
        self.sems.append(self.nc.alloc_semaphore(name=f"{self.tag}_{name}"))
        return self.sems[-1]


def spread_dma(engine, to, what, sem):
    engine.dma_start(to[0:M_EVEN], what[0:M_EVEN]).then_inc(sem, 16)
    engine.dma_start(to[M_EVEN:M], what[M_EVEN:M]).then_inc(sem, 16)


def stage_prepare(nc, x, src, dst, edges_pad, w1, w2, ident, ident_b, ones_r, xT_hi, xT_lo, w1T_dram, w2T_dram,
                  unit, adj_dram):
    with ExitStack() as stack:
        m = Pool(nc, stack, "prep")
        adj = m.sb("adj", [P, NT, NP], F32R)
        x_all = adj[:, :, 0:D].bitcast(F32)
        stats = m.sb("stats", [P, NT, 2, 6], F32)
        mv = m.sb("mv", [P, NT, 2], F32)
        rs = m.sb("rs", [P, 6, NT], F32)
        dst_i = m.sb("dst_i", [P, ER], I32)
        src_i = m.sb("src_i", [P, ER], I32)
        dst_f = m.sb("dst_f", [P, ER], F32)
        next_i = m.sb("next_i", [P, 1], I32)
        next_f = m.sb("next_f", [P, 1], F32)
        pad_i = m.sb("pad_i", [1, ECAP], I32)
        below = m.sb("below", [P, HALF_W, ER], BF16)
        back = m.sb("back", [P, ER], F32)
        limit = m.sb("limit", [P, NW + 1], F32)
        part = m.sb("part", [P, NW + 4], F32)
        start_f = m.sb("start_f", [P, NW + 4], F32)
        start_i = m.sb("start_i", [P, NW + 4], I32)
        load_f = m.sb("load_f", [P, NW], F32)
        flag_f = m.sb("flag_f", [P, 2], F32)
        flag_i = m.sb("flag_i", [P, 1], I32)
        iota_b = m.sb("iota_b", [P, P], BF16)
        iota_c = m.sb("iota_c", [P, WC], BF16)
        edges = m.sb("edges", [P, 2, NW, EC], I32)
        s_f = m.sb("s_f", [P, NW, EC], F32)
        d_f = m.sb("d_f", [P, NW, EC], F32)
        a_f = m.sb("a_f", [P, NW, EC], F32)
        b_f = m.sb("b_f", [P, NW, EC], F32)
        neg_b = m.sb("neg_b", [P, NW, EC], F32)
        in_f = m.sb("in_f", [P, NW, EC], F32)
        col_f = m.sb("col_f", [P, NW, EC], F32)
        dist = m.sb("dist", [P, 4, EC // 2, P], BF16)
        one = m.sb("one", [P, 1], F32)
        hot_b = m.sb("hot_b", [P, 2 * GC, P], BF16)
        hot_c = m.sb("hot_c", [P, 2 * GC, WC], BF16)
        raw = m.sb("raw", [P, HC * D], F32)
        tern = m.sb("tern", [P, HC * D], BF16)
        w1T = m.sb("w1T", [P, KC, HID], BF16)
        w2T = m.sb("w2T", [P, HC, D], BF16)
        total = m.sb("total", [P, 2], F32)
        scale = m.sb("scale", [P, 2], F32)
        bank = [m.bank(f"bank{i}") for i in range(4)]
        tp = [b[:, 0:4 * M].rearrange("p (c n) -> p c n", n=M) for b in bank]
        ps_w = [b[:, 0:WC].rearrange("p (a d) -> p a d", d=W) for b in bank[0:2]]
        ps_sum = m.bank("ps_sum")
        ps_total = m.bank("ps_total")
        ps_t = [m.psum(f"ps_t{i}", [P, 2 * BANK], BF16) for i in range(2)]
        const_ready = m.sem("const_ready")
        iota_ready = m.sem("iota_ready")
        x_loaded = [m.sem(f"x_loaded{b}") for b in range(2)]
        stats_ready = m.sem("stats_ready")
        held = m.sem("held")
        var_ready = m.sem("var_ready")
        root_ready = m.sem("root_ready")
        xn_ready = m.sem("xn_ready")
        turned = m.sem("turned")
        turned_hi = m.sem("turned_hi")
        turned_lo = m.sem("turned_lo")
        dst_in = m.sem("dst_in")
        src_in = m.sem("src_in")
        next_in = m.sem("next_in")
        pad_set = m.sem("pad_set")
        padded = m.sem("padded")
        counted = m.sem("counted")
        summed = m.sem("summed")
        flag_set = m.sem("flag_set")
        edges_in = [m.sem(f"edges_in{i}") for i in range(len(GROUPS))]
        columns_set = m.sem("columns_set")
        sources_set = m.sem("sources_set")
        dist_ready = m.sem("dist_ready")
        odd_ready = m.sem("odd_ready")
        hot_ready = m.sem("hot_ready")
        hot_used = m.sem("hot_used")
        window_done = m.sem("window_done")
        window_kept = m.sem("window_kept")
        zeroed = m.sem("zeroed")
        stored = m.sem("stored")
        raw_in = m.sem("raw_in")
        total_ready = m.sem("total_ready")
        total_summed = m.sem("total_summed")
        scale_ready = m.sem("scale_ready")
        rounded = m.sem("rounded")
        clipped = m.sem("clipped")
        tern_ready = m.sem("tern_ready")
        w_turned = m.sem("w_turned")
        w_kept = m.sem("w_kept")
        w_out = m.sem("w_out")
        chain = [m.sem(f"chain_{n}") for n in ("common", "short", "general")]
        block = stack.enter_context(nc.Block())
        JOBS = [(0, c, c * D, w1T[:, :, c * P:(c + 1) * P]) for c in range(HC)]
        JOBS += [(1, c, c * HID, w2T[:, :, c * P:(c + 2) * P]) for c in range(0, KC, 2)]
        HALF = NT // 2
        rows = lambda t: t.rearrange("(p c) -> p c", c=ER)

        @block.sync
        def _(sp):
            sp.dma_start(dst_i[0:M, :], rows(dst)).then_inc(dst_in, 16)
            with nc.allow_non_contiguous_dma(reason="one word of each row"):
                sp.dma_start(next_i[0:M - 1, :], rows(dst)[1:M, 0:1]).then_inc(next_in, 16)
            sp.dma_start(raw[:, :].rearrange("p (c k) -> p c k", k=D),
                         w1.rearrange("(c p) k -> p c k", p=P)).then_inc(raw_in, 16)
            for b in range(2):
                spread_dma(sp, x_all[:, b * HALF:(b + 1) * HALF, :],
                           x[b * HALF * M:(b + 1) * HALF * M, :].rearrange("(t p) d -> p t d", p=M), x_loaded[b])
            sp.dma_start(src_i[0:M, :], rows(src)).then_inc(src_in, 16)
            sp.dma_start(rows(edges_pad[0, 0:E]), rows(dst)).then_inc(padded, 16)
            sp.dma_start(rows(edges_pad[1, 0:E]), rows(src)).then_inc(padded, 16)
            sp.wait_ge(pad_set, 1)
            for i in range(2):
                sp.dma_start(edges_pad[i:i + 1, E:E + ECAP], pad_i[:, :]).then_inc(padded, 16)
            sp.wait_ge(padded, 64)
            sp.wait_ge(flag_set, 1)
            every = sp.value_load(flag_i[0:1, 0:1], min_val=0, max_val=1)

            def load_windows(i, a, b):
                with sp.If(every < 1):
                    with sp.Fori(a, b) as j:
                        first = sp.value_load(start_i[0:1, ds(j, 1)], min_val=0, max_val=E)
                        sp.dma_start(edges[:, :, ds(j, 1), :].rearrange("p i a c -> p i (a c)"),
                                     edges_pad[:, ds(first, ECAP)].rearrange("i (p c) -> p i c", c=EC)
                                     ).then_inc(edges_in[i], 16)

            load_windows(0, *GROUPS[0])
            sp.wait_ge(tern_ready, 1)
            sp.dma_start(raw[:, :].rearrange("p (c k) -> p c k", k=HID),
                         w2.rearrange("(c p) k -> p c k", p=P)).then_inc(raw_in, 16)
            load_windows(1, *GROUPS[1])
            load_windows(2, *GROUPS[2])
            sp.wait_ge(zeroed, 1)
            for first, end in ((0, NW // 2), (NW // 2, LAST_W), (LAST_W, NW)):
                sp.wait_ge(window_kept, end + 2)
                cols = slice(first * W, end * W if end < NW else NP)
                if first == 0:
                    sp.wait_ge(w_kept, HC + 2)
                    sp.dma_start(w1T_dram, w1T[:, :, :]).then_inc(w_out, 16)
                spread_dma(sp, adj_dram[:, :, cols], adj[:, :, cols].bitcast(F32), stored)
            sp.wait_ge(w_kept, len(JOBS) + 2)
            sp.dma_start(w2T_dram, w2T[:, :, :]).then_inc(w_out, 16)
            sp.wait_ge(src_in, 16)
            sp.wait_ge(w_out, 32)
            sp.wait_ge(stored, 96)

        @block.gpsimd
        def _(pool):
            pool.iota(limit[:, :], [[W, NW + 1]], base=0, channel_multiplier=0,
                      allow_small_or_imprecise_dtypes=True).then_inc(const_ready, 1)
            pool.iota(pad_i[:, :], [[0, ECAP]], base=-1, channel_multiplier=0).then_inc(pad_set, 1)
            pool.memset(ident[:, :], 0.0).then_inc(const_ready, 1)
            pool.wait_ge(const_ready, 2)
            pool.affine_select(out=ident[:, :], in_=ident[:, :], compare_op=ALU.not_equal, fill=1.0,
                               base=0, pattern=[[-1, P]], channel_multiplier=1).then_inc(const_ready, 1)
            pool.wait_ge(const_ready, 3)
            pool.tensor_copy(ident_b[:, :], ident[:, :]).then_inc(const_ready, 1)
            pool.iota(iota_b[:, :], [[1, P]], base=0, channel_multiplier=0,
                      allow_small_or_imprecise_dtypes=True).then_inc(iota_ready, 1)
            pool.iota(iota_c[:, :], [[1, WC]], base=0, channel_multiplier=0,
                      allow_small_or_imprecise_dtypes=True).then_inc(iota_ready, 1)
            for i in range(2):
                pool.wait_ge(rounded, i + 1)
                nc.gpsimd.tensor_scalar(raw[:, :], raw[:, :], ROUND - 1.0, ROUND + 1.0, ALU.max,
                                        ALU.min).then_inc(clipped, 1)

        @block.vector
        def _(dve):
            at = [0, 0, 0]

            def link(ins, c=0):
                at[c] += 1
                ins.then_inc(chain[c], 1)
                dve.wait_ge(chain[c], at[c])

            nc.vector.memset(ones_r[:, :].bitcast(F32), 1.0)
            nc.vector.memset(one[:, :], 1.0)
            nc.vector.memset(xT_hi[:, :, N:NP].bitcast(F32), 0.0)
            nc.vector.memset(xT_lo[:, :, N:NP].bitcast(F32), 0.0)
            nc.vector.memset(adj[:, :, N:NP].bitcast(F32), 0.0).then_inc(zeroed, 1)

            link(nc.vector.memset(part[:, :], 0.0))
            dve.wait_ge(const_ready, 1)
            dve.wait_ge(dst_in, 16)
            dve.wait_ge(next_in, 16)
            link(nc.vector.tensor_copy(dst_f[0:M, :], dst_i[0:M, :]))
            link(nc.vector.tensor_copy(next_f[0:M - 1, :], next_i[0:M - 1, :]))
            for a, b in ((0, HALF_W), (HALF_W, NW + 1)):
                link(nc.vector.tensor_tensor(below[0:M, 0:b - a, :],
                                             dst_f[0:M, :].unsqueeze(1).to_broadcast([M, b - a, ER]),
                                             limit[0:M, a:b].unsqueeze(2).to_broadcast([M, b - a, ER]), ALU.is_lt))
                link(nc.vector.tensor_reduce(part[0:M, a:b], below[0:M, 0:b - a, :], AX_X, ALU.add))
            link(nc.vector.tensor_tensor(back[0:M, 0:ER - 1], dst_f[0:M, 0:ER - 1], dst_f[0:M, 1:ER], ALU.is_gt))
            link(nc.vector.tensor_reduce(part[0:M, NW + 1:NW + 2], back[0:M, 0:ER - 1], AX_X, ALU.add))
            nc.vector.tensor_tensor(part[0:M - 1, NW + 2:NW + 3], dst_f[0:M - 1, ER - 1:ER],
                                    next_f[0:M - 1, :], ALU.is_gt).then_inc(counted, 1)

            def step_of(i):
                dve.wait_ge(total_summed, i + 1)
                link(nc.vector.tensor_scalar(unit[:, i:i + 1], ps_total[:, 2 * i + 64:2 * i + 65], 1.0 / (HID * D), EPS_Q,
                                             ALU.mult, ALU.max))
                nc.vector.reciprocal(scale[:, i:i + 1], unit[:, i:i + 1]).then_inc(scale_ready, 1)

            step_of(0)
            dve.wait_ge(summed, 1)
            link(nc.vector.tensor_copy(start_f[:, :], ps_sum[:, 0:NW + 4]))
            link(nc.vector.tensor_copy(start_i[:, :], start_f[:, :]))
            link(nc.vector.tensor_tensor(load_f[:, :], start_f[:, 1:NW + 1], start_f[:, 0:NW], ALU.subtract))
            link(nc.vector.tensor_reduce(flag_f[:, 0:1], load_f[:, :], AX_X, ALU.max))
            link(nc.vector.tensor_scalar(flag_f[:, 0:1], flag_f[:, 0:1], float(ECAP), None, ALU.is_gt))
            link(nc.vector.tensor_tensor(flag_f[:, 0:1], flag_f[:, 0:1], start_f[:, NW + 1:NW + 2], ALU.add))
            link(nc.vector.tensor_tensor(flag_f[:, 0:1], flag_f[:, 0:1], start_f[:, NW + 2:NW + 3], ALU.add))
            nc.vector.tensor_scalar(flag_i[:, :], flag_f[:, 0:1], 1.0, None, ALU.min).then_inc(flag_set, 1)

            for b in range(2):
                dve.wait_ge(x_loaded[b], 32)
                dve.sem_inc(held, 1)
                with dve.Fori(b * HALF, (b + 1) * HALF) as t:
                    for h in range(2):
                        nc.vector.bn_stats(stats[0:M, ds(t, 1), h, :].rearrange("p t s -> p (t s)"),
                                           x_all[0:M, ds(t, 1), h * 512:(h + 1) * 512].rearrange("p t d -> p (t d)")
                                           ).then_inc(stats_ready, 1)
            dve.wait_ge(stats_ready, 2 * NT)
            dve.sem_inc(held, 1)
            for t in range(NT):
                last = nc.vector.bn_aggr(mv[0:M, t, :], stats[0:M, t, :, :])
            link(last)
            r = lambda i: rs[0:M, i, :]
            nc.vector.tensor_scalar(r(0), mv[0:M, :, 1], EPS_LN, None, ALU.add).then_inc(var_ready, 1)
            dve.wait_ge(root_ready, 1)
            link(nc.vector.reciprocal(r(2), r(1)))
            link(nc.vector.tensor_tensor(r(3), r(2), r(2), ALU.mult))
            link(nc.vector.tensor_tensor(r(4), r(3), r(0), ALU.mult))
            link(nc.vector.tensor_scalar(r(4), r(4), -0.5, 1.5, ALU.mult, ALU.add))
            link(nc.vector.tensor_tensor(r(5), r(4), r(2), ALU.mult))

            def normalise(t):
                nc.vector.tensor_scalar(x_all[0:M, t, :], x_all[0:M, t, :], mv[0:M, t, 0:1], rs[0:M, 5, t:t + 1],
                                        ALU.subtract, ALU.mult).then_inc(xn_ready, 1)

            normalise(0)
            normalise(1)
            for t in range(NT):
                if t + 2 < NT:
                    normalise(t + 2)
                nodes = slice(t * M, (t + 1) * M)
                for h in range(2):
                    dve.wait_ge(turned_hi, 2 * t + h + 1)
                    nc.vector.tensor_tensor(xT_lo[:, 4 * h:4 * h + 4, nodes], tp[2 * (t % 2) + h][:, :, :],
                                            xT_hi[:, 4 * h:4 * h + 4, nodes].bitcast(F32), ALU.subtract).then_inc(turned_lo, 1)

            def split_source(c, a, b, s):
                link(nc.vector.tensor_scalar(a, s, 1.0 / M, 0.5 / M - 0.5, ALU.mult, ALU.add), c)
                link(nc.vector.tensor_scalar(a, a, ROUND, ROUND, ALU.add, ALU.subtract), c)
                link(nc.vector.scalar_tensor_tensor(b, a, -float(M), s, ALU.mult, ALU.add), c)

            dve.wait_ge(iota_ready, 2)
            every = dve.value_load(flag_i[0:1, 0:1], min_val=0, max_val=1)
            dve.sem_inc(hot_used, 2 * GC)

            def short(i, a, b):
                w = slice(a, b)
                dve.wait_ge(edges_in[i], 16 * (b - a))
                link(nc.vector.tensor_copy(s_f[:, w, :], edges[:, 1, w, :]), 1)
                link(nc.vector.tensor_copy(d_f[:, w, :], edges[:, 0, w, :]), 1)
                split_source(1, a_f[:, w, :], b_f[:, w, :], s_f[:, w, :])
                nc.vector.tensor_scalar(neg_b[:, w, :], b_f[:, w, :], -1.0, None, ALU.mult).then_inc(sources_set, 1)
                link(nc.vector.tensor_tensor(d_f[:, w, :], d_f[:, w, :],
                                             limit[:, w].unsqueeze(2).to_broadcast([P, b - a, EC]), ALU.subtract), 1)
                link(nc.vector.tensor_scalar(in_f[:, w, :], d_f[:, w, :], 0.0, None, ALU.is_ge), 1)
                link(nc.vector.scalar_tensor_tensor(in_f[:, w, :], d_f[:, w, :], W - 1.0, in_f[:, w, :],
                                                    ALU.is_le, ALU.mult), 1)
                link(nc.vector.scalar_tensor_tensor(col_f[:, w, :], a_f[:, w, :], float(W), d_f[:, w, :],
                                                    ALU.mult, ALU.add), 1)
                link(nc.vector.scalar_tensor_tensor(col_f[:, w, :], col_f[:, w, :], 1.0, in_f[:, w, :],
                                                    ALU.add, ALU.mult), 1)
                link(nc.vector.tensor_scalar(col_f[:, w, :], col_f[:, w, :], -1.0, None, ALU.add), 1)
                with dve.Fori(a // 4, b // 4) as q:
                    for w in range(4):
                        dve.wait_ge(hot_used, q * (2 * GC) + (w * EC + EC))
                        for c in range(EC):
                            h = w * EC + c
                            if c % 2 == 0:
                                nc.vector.tensor_scalar(hot_b[:, h, :], iota_b[:, :],
                                                        b_f[:, ds(q * 4 + w, 1), c:c + 1].rearrange("p a c -> p (a c)"),
                                                        None, ALU.is_equal)
                            nc.vector.tensor_scalar(hot_c[:, h, :], iota_c[:, :],
                                                    col_f[:, ds(q * 4 + w, 1), c:c + 1].rearrange("p a c -> p (a c)"),
                                                    None, ALU.is_equal).then_inc(hot_ready, 1)
                for w in range(b // 4 * 4, b):
                    for c in range(EC):
                        h = (w % 4) * EC + c
                        dve.wait_ge(hot_used, w // 4 * 2 * GC + h + 1)
                        if c % 2 == 0:
                            nc.vector.tensor_scalar(hot_b[:, h, :], iota_b[:, :], b_f[:, w, c:c + 1],
                                                    None, ALU.is_equal)
                        nc.vector.tensor_scalar(hot_c[:, h, :], iota_c[:, :], col_f[:, w, c:c + 1],
                                                None, ALU.is_equal).then_inc(hot_ready, 1)

            flat = lambda t: t[0:M, :, :].rearrange("p a c -> p (a c)")[:, 0:ER]

            def general(a, b):
                with dve.Fori(a, b) as j:
                    c0 = j * 5 + at[2]
                    nc.vector.tensor_scalar(flat(d_f), dst_f[0:M, :], limit[0:M, ds(j, 1)], None,
                                            ALU.subtract).then_inc(chain[2], 1)
                    dve.wait_ge(chain[2], c0 + 1)
                    nc.vector.tensor_scalar(flat(in_f), flat(d_f), 0.0, None, ALU.is_ge).then_inc(chain[2], 1)
                    dve.wait_ge(chain[2], c0 + 2)
                    nc.vector.scalar_tensor_tensor(flat(in_f), flat(d_f), W - 1.0, flat(in_f),
                                                   ALU.is_le, ALU.mult).then_inc(chain[2], 1)
                    nc.vector.scalar_tensor_tensor(flat(col_f), flat(a_f), float(W), flat(d_f),
                                                   ALU.mult, ALU.add).then_inc(chain[2], 1)
                    dve.wait_ge(chain[2], c0 + 4)
                    nc.vector.scalar_tensor_tensor(flat(col_f), flat(col_f), 1.0, flat(in_f),
                                                   ALU.add, ALU.mult).then_inc(chain[2], 1)
                    dve.wait_ge(chain[2], c0 + 5)
                    dve.sem_inc(columns_set, 1)
                    with dve.Fori(0, ER // (2 * GC)) as g:
                        for h in range(2 * GC):
                            dve.wait_ge(hot_used, j * ER + g * (2 * GC) + (h + 1))
                            nc.vector.tensor_scalar(hot_b[0:M, h, :], iota_b[0:M, :],
                                                    flat(b_f)[:, ds(g * (2 * GC) + h, 1)], None, ALU.is_equal)
                            nc.vector.tensor_scalar(hot_c[0:M, h, :], iota_c[0:M, :], 1.0,
                                                    flat(col_f)[:, ds(g * (2 * GC) + h, 1)],
                                                    ALU.add, ALU.is_equal).then_inc(hot_ready, 1)

            with dve.If(every < 1):
                short(0, *GROUPS[0])
            with dve.If(every > 0):
                dve.wait_ge(src_in, 16)
                link(nc.vector.tensor_copy(flat(s_f), src_i[0:M, :]), 2)
                split_source(2, flat(a_f), flat(b_f), flat(s_f))
                general(*GROUPS[0])
            step_of(1)
            with dve.If(every < 1):
                short(1, *GROUPS[1])
                short(2, *GROUPS[2])
            with dve.If(every > 0):
                general(GROUPS[1][0], NW)

        @block.scalar
        def _(act):
            def total_of(i):
                act.wait_ge(raw_in, 16 * (i + 1))
                nc.scalar.activation(tern[:, :], raw[:, :], ACT.Abs, accum_out=total[:, i:i + 1]).then_inc(total_ready, 1)

            def round_w(i):
                act.wait_ge(scale_ready, i + 1)
                act.wait_ge(total_ready, i + 1)
                nc.scalar.activation(raw[:, :], raw[:, :], ACT.Copy, bias=ROUND, scale=scale[:, i:i + 1]).then_inc(rounded, 1)

            def ternary(i):
                act.wait_ge(clipped, i + 1)
                nc.scalar.activation(tern[:, :], raw[:, :], ACT.Copy, bias=-ROUND).then_inc(tern_ready, 1)

            def keep_w(i):
                for n in range(HC * i, HC * (i + 1)):
                    act.wait_ge(w_turned, n + 1)
                    nc.scalar.copy(JOBS[n][3], ps_t[n % 2][:, :].rearrange("p (c n) -> p c n", c=(KC, HC)[i])
                                   ).then_inc(w_kept, 1)

            def keep_window(w, i):
                act.wait_ge(window_done, w + 1)
                nc.scalar.copy(adj[0:M, :, ds(w * W, W)], ps_w[i][0:M, :, :]).then_inc(window_kept, 1)

            def short_window(w, slot, i, keep=True):
                act.wait_ge(hot_used, w * EC + EC)
                for c in range(1, EC, 2):
                    last = nc.scalar.activation(dist[:, slot, c // 2, :], iota_b[:, :], ACT.Abs,
                                                bias=neg_b[:, ds(w, 1), c:c + 1].rearrange("p a c -> p (a c)"))
                last.then_inc(dist_ready, 1)
                if keep:
                    keep_window(w - 2, i)
                act.wait_ge(dist_ready, w + 1)
                nc.scalar.activation(hot_b[:, slot * EC:(slot + 1) * EC, :].rearrange("p (c o) b -> p c o b", o=2)[:, :, 1, :],
                                     dist[:, slot, :, :], ACT.Relu, bias=one[:, :], scale=-1.0).then_inc(odd_ready, 1)

            def windows(g):
                a, b = GROUPS[g]
                with act.If(every < 1):
                    act.wait_ge(sources_set, g + 1)
                    act.sem_inc(held, 1)
                    if g == 0:
                        for w in range(4):
                            short_window(w, w, w % 2, keep=w >= 2)
                    with act.Fori(a // 4 + (g == 0), b // 4) as q:
                        for w in range(4):
                            short_window(q * 4 + w, w, w % 2)
                    for w in range(b // 4 * 4, b):
                        short_window(w, w % 4, w % 2)
                    if b == NW:
                        for w in (NW - 2, NW - 1):
                            keep_window(w, w % 2)
                with act.If(every > 0):
                    with act.Fori(a // 2, b // 2) as q:
                        for i in range(2):
                            keep_window(q * 2 + i, i)

            total_of(0)
            round_w(0)
            act.wait_ge(var_ready, 1)
            nc.scalar.activation(rs[0:M, 1, :], rs[0:M, 0, :], ACT.Sqrt).then_inc(root_ready, 1)
            ternary(0)
            with act.Fori(0, HALF) as i:
                for b in range(2):
                    for h in range(2):
                        act.wait_ge(turned, i * 4 + (2 * b + h + 1))
                        nc.scalar.copy(xT_hi[:, 4 * h:4 * h + 4, ds(i * (2 * M) + b * M, M)],
                                       tp[2 * b + h][:, :, :]).then_inc(turned_hi, 1)
            keep_w(0)
            total_of(1)
            act.wait_ge(flag_set, 1)
            act.wait_ge(iota_ready, 2)
            every = act.value_load(flag_i[0:1, 0:1], min_val=0, max_val=1)
            windows(0)
            round_w(1)
            windows(1)
            ternary(1)
            windows(2)
            keep_w(1)

        @block.tensor
        def _(pe):
            def sum_up(i):
                pe.wait_ge(total_ready, i + 1)
                nc.tensor.matmul(ps_total[:, 2 * i + 64:2 * i + 66], ones_r[:, :].bitcast(F32),
                                 total[:, i:i + 1].to_broadcast([P, 2]), start=True, stop=True).then_inc(total_summed, 1)

            def turn_w(i):
                for n in range(HC * i, HC * (i + 1)):
                    _, c, first, _ = JOBS[n]
                    pe.wait_ge(tern_ready, i + 1)
                    pe.wait_ge(w_kept, n + 1)
                    for u in range(8):
                        col = u if i == 0 else (u % HC) * 2 + u // HC
                        last = nc.tensor.transpose(ps_t[n % 2][:, col * P:(col + 1) * P],
                                                   tern[:, first + u * P:first + (u + 1) * P], ident_b[:, :])
                    last.then_inc(w_turned, 1)

            pe.wait_ge(counted, 1)
            nc.tensor.matmul(ps_sum[:, 0:NW + 4], ones_r[0:M, :].bitcast(F32), part[0:M, :],
                             start=True, stop=True).then_inc(summed, 1)
            sum_up(0)
            pe.wait_ge(const_ready, 4)
            pe.sem_inc(turned_lo, 4)
            for t in range(NT):
                pe.wait_ge(xn_ready, t + 1)
                for h in range(2):
                    pe.wait_ge(turned_lo, 2 * t + h + 1)
                    for c in range(4):
                        k = 4 * h + c
                        last = nc.tensor.transpose(tp[2 * (t % 2) + h][:, c, :], x_all[0:M, t, k * P:(k + 1) * P],
                                                   ident[0:M, 0:M])
                    last.then_inc(turned, 1)
            pe.sem_inc(w_kept, 2)
            turn_w(0)
            sum_up(1)
            pe.wait_ge(flag_set, 1)
            every = pe.value_load(flag_i[0:1, 0:1], min_val=0, max_val=1)
            pe.wait_ge(turned_lo, 2 * NT + 4)
            pe.sem_inc(window_kept, 2)

            def window(w, kept, ready):
                pe.wait_ge(window_kept, kept)
                for c in range(EC):
                    h = w * EC + c
                    if c == 1:
                        pe.wait_ge(odd_ready, kept)
                    pe.wait_ge(hot_ready, ready + (h + 1))
                    nc.tensor.matmul(ps_w[w % 2][:, :, :], hot_b[:, h, :], hot_c[:, h, :],
                                     start=(c == 0), stop=(c == EC - 1)).then_inc(hot_used, 1)
                pe.wait_ge(hot_used, ready + (2 * GC + w * EC + EC))
                pe.sem_inc(window_done, 1)

            def group(b, ready, first, final):
                for h in range(2 * GC):
                    pe.wait_ge(hot_ready, ready + (h + 1))
                    nc.tensor.matmul(ps_w[b][:, :, :], hot_b[0:M, h, :], hot_c[0:M, h, :],
                                     start=(first and h == 0), stop=(final and h == 2 * GC - 1)).then_inc(hot_used, 1)

            def windows(a, b):
                with pe.If(every < 1):
                    with pe.Fori(a // 4, b // 4) as q:
                        for w in range(4):
                            window(w, q * 4 + (w + 1), q * (2 * GC))
                    for w in range(b // 4 * 4, b):
                        window(w % 4, w + 1, w // 4 * 2 * GC)
                with pe.If(every > 0):
                    with pe.Fori(a // 2, b // 2) as q:
                        for i in range(2):
                            pe.wait_ge(window_kept, q * 2 + (i + 1))
                            base = q * (2 * ER) + i * ER
                            group(i, base, True, False)
                            with pe.Fori(1, ER // (2 * GC) - 1) as g:
                                group(i, base + g * (2 * GC), False, False)
                            group(i, base + (ER - 2 * GC), False, True)
                            pe.wait_ge(hot_used, base + (ER + 2 * GC))
                            pe.sem_inc(window_done, 1)

            windows(*GROUPS[0])
            windows(*GROUPS[1])
            windows(*GROUPS[2])
            turn_w(1)




def panel(w, j, width=P):
    return w[:, ds(j * width, width)].rearrange("(c p) n -> p c n", p=P)


class Panel:

    def __init__(self, m):
        self.raw = m.sb("raw", [P, KC, P], F32)
        self.hi = m.sb("hi", [P, KC, P], F32R)
        self.lo = m.sb("lo", [P, KC, P], F32R)


def exact_product(pe, out, pairs):
    for n, (lh, ll, rh, rl) in enumerate(pairs):
        first, final = n == 0, n == len(pairs) - 1
        pe.matmul(out, lh, rh, start=first, stop=False)
        pe.matmul(out, lh, rl, start=False, stop=False)
        last = pe.matmul(out, ll, rh, start=False, stop=final)
    return last


def stage_sage0(nc, w_neigh, w_self, bias, xT_hi, xT_lo, adj_dram, adj, inv_row, inv_col, ident, ones_r,
                hT_hi_dram, hT_lo_dram, panel_n, panel_s, pT, next_panel, w_next):
    with ExitStack() as stack:
        m = Pool(nc, stack, "sage0")
        raw_n, wn_hi, wn_lo = panel_n.raw, panel_n.hi, panel_n.lo
        raw_s, ws_hi, ws_lo = panel_s.raw, panel_s.hi, panel_s.lo
        b_col = m.sb("b_col", [P, KC], F32)
        p_hi = m.sb("p_hi", [P, NT, P], F32R)
        p_lo = m.sb("p_lo", [P, NT, P], F32R)
        mean = m.sb("mean", [P, CT, CW], F32)
        pre = m.sb("pre", [P, CT, CW], F32)
        h_hi = m.sb("h_hi", [P, CT, CW], F32R)
        h_lo = m.sb("h_lo", [P, CT, CW], F32R)
        ps_n = [m.psum(f"ps_n{t}", [P, BANK]) for t in range(CT)]
        ps_s = [m.psum(f"ps_s{t}", [P, BANK]) for t in range(CT)]
        ps_t = [m.psum(f"ps_t{i}", [P, 4, P]) for i in range(2)]
        bias_in = m.sem("bias_in")
        adj_in = [m.sem(f"adj_in{t}") for t in range(CT)]
        next_in = m.sem("next_in")
        deg_ready = m.sem("deg_ready")
        inv_ready = m.sem("inv_ready")
        clamped = m.sem("clamped")
        col_ready = m.sem("col_ready")
        raw_n_in = m.sem("raw_n_in")
        raw_s_in = m.sem("raw_s_in")
        wn_hi_ready = m.sem("wn_hi_ready")
        wn_ready = m.sem("wn_ready")
        ws_hi_ready = m.sem("ws_hi_ready")
        ws_ready = m.sem("ws_ready")
        n_done = m.sem("n_done")
        s_done = m.sem("s_done")
        pT_ready = m.sem("pT_ready")
        turned = m.sem("turned")
        p_hi_ready = m.sem("p_hi_ready")
        p_ready = m.sem("p_ready")
        agg_done = m.sem("agg_done")
        mean_ready = m.sem("mean_ready")
        pre_ready = m.sem("pre_ready")
        h_hi_ready = m.sem("h_hi_ready")
        h_ready = m.sem("h_ready")
        h_out = [m.sem(f"h_out{t}") for t in range(CT)]
        block = stack.enter_context(nc.Block())
        cols = lambda t: slice(t * CW, (t + 1) * CW)

        @block.sync
        def _(sp):
            with nc.allow_non_contiguous_dma(reason="a bias, one word a partition"):
                sp.dma_start(b_col[:, :], bias.rearrange("(c p) -> p c", p=P)).then_inc(bias_in, 16)
            sp.sem_inc(raw_n_in, 16)
            sp.sem_inc(raw_s_in, 16)

            def chunk(j, first=False, last=False):
                if not last:
                    sp.wait_ge(wn_ready, j + 1)
                    sp.dma_start(raw_n[:, :, :], panel(w_neigh, j + 1)).then_inc(raw_n_in, 16)
                    sp.wait_ge(ws_ready, j + 1)
                    sp.dma_start(raw_s[:, :, :], panel(w_self, j + 1)).then_inc(raw_s_in, 16)
                if first:
                    for t in range(CT):
                        spread_dma(sp, adj[:, :, cols(t)].bitcast(F32), adj_dram[:, :, cols(t)], adj_in[t])
                    sp.dma_start(next_panel[:, :, :], panel(w_next, 0, PW)).then_inc(next_in, 16)
                for t in range(CT):
                    sp.wait_ge(h_ready, j * CT + (t + 1))
                    sp.dma_start(hT_hi_dram[ds(j * P, P), cols(t)], h_hi[:, t, :].bitcast(F32)).then_inc(h_out[t], 16)
                    sp.dma_start(hT_lo_dram[ds(j * P, P), cols(t)], h_lo[:, t, :].bitcast(F32)).then_inc(h_out[t], 16)

            chunk(0, first=True)
            with sp.Fori(1, KC - 1) as j:
                chunk(j)
            chunk(KC - 1, last=True)
            sp.wait_ge(next_in, 16)
            for t in range(CT):
                sp.wait_ge(h_out[t], 32 * KC + 32)

        @block.scalar
        def _(act):
            def split_n(j):
                act.wait_ge(raw_n_in, j * 16 + 16)
                nc.scalar.copy(wn_hi[:, :, :], raw_n[:, :, :]).then_inc(wn_hi_ready, 1)

            def split_s(j):
                act.wait_ge(raw_s_in, j * 16 + 16)
                nc.scalar.copy(ws_hi[:, :, :], raw_s[:, :, :]).then_inc(ws_hi_ready, 1)

            def chunk(j, first=False, last=False):
                for t in range(0 if first else CT):
                    act.wait_ge(n_done, j * CT + (t + 1))
                    nc.scalar.copy(pT[:, cols(t)], ps_n[t][:, 0:CW]).then_inc(pT_ready, 1)
                if not last:
                    split_n(j + 1)
                for g, (a, b) in enumerate(TURNS):
                    act.wait_ge(turned, j * 3 + (g + 1))
                    nc.scalar.copy(p_hi[0:M, a:b, :], ps_t[g % 2][0:M, 0:b - a, :]).then_inc(p_hi_ready, 1)
                if not last:
                    act.wait_ge(s_done, j * CT + CT)
                    split_s(j + 1)
                for t in range(CT):
                    act.wait_ge(pre_ready, j * CT + (CT + t + 1))
                    act.wait_ge(h_out[t], j * 32 + 32)
                    nc.scalar.activation(h_hi[:, t, :], pre[:, t, :], ACT.Relu).then_inc(h_hi_ready, 1)

            for t in range(CT):
                act.sem_inc(h_out[t], 32)
            act.sem_inc(wn_hi_ready, 1)
            act.sem_inc(ws_hi_ready, 1)
            act.sem_inc(pT_ready, CT)
            chunk(0, first=True)
            with act.Fori(1, KC - 1) as j:
                chunk(j)
            chunk(KC - 1, last=True)

        @block.vector
        def _(dve):
            def split_n(j):
                dve.wait_ge(wn_hi_ready, j + 1)
                nc.vector.tensor_tensor(wn_lo[:, :, :], raw_n[:, :, :], wn_hi[:, :, :].bitcast(F32),
                                        ALU.subtract).then_inc(wn_ready, 1)

            def split_s(j):
                dve.wait_ge(ws_hi_ready, j + 1)
                nc.vector.tensor_tensor(ws_lo[:, :, :], raw_s[:, :, :], ws_hi[:, :, :].bitcast(F32),
                                        ALU.subtract).then_inc(ws_ready, 1)

            def chunk(j, first=False, last=False):
                if not last:
                    split_n(j + 1)
                for g, (a, b) in enumerate(TURNS):
                    dve.wait_ge(p_hi_ready, j * 3 + (g + 1))
                    nc.vector.tensor_tensor(p_lo[0:M, a:b, :], ps_t[g % 2][0:M, 0:b - a, :],
                                            p_hi[0:M, a:b, :].bitcast(F32), ALU.subtract).then_inc(p_ready, 1)
                if first:
                    for t in range(CT):
                        dve.wait_ge(deg_ready, t + 1)
                        nc.vector.tensor_scalar(inv_row[:, cols(t)], ps_n[t][:, 0:CW], 1.0, None, ALU.max).then_inc(clamped, 1)
                    for t in range(CT):
                        dve.wait_ge(clamped, t + 1)
                        nc.vector.reciprocal(inv_row[:, cols(t)], inv_row[:, cols(t)]).then_inc(inv_ready, 1)
                    dve.wait_ge(inv_ready, CT)
                if not last:
                    split_s(j + 1)
                for t in range(CT):
                    dve.wait_ge(agg_done, j * CT + (t + 1))
                    nc.vector.tensor_tensor(mean[:, t, :], ps_n[t][:, 0:CW], inv_row[:, cols(t)],
                                            ALU.mult).then_inc(mean_ready, 1)
                    dve.wait_ge(mean_ready, j * CT + (CT + t + 1))
                    nc.vector.scalar_tensor_tensor(pre[:, t, :], ps_s[t][:, 0:CW], b_col[:, ds(j, 1)],
                                                   mean[:, t, :], ALU.add, ALU.add).then_inc(pre_ready, 1)
                for t in range(CT):
                    dve.wait_ge(h_hi_ready, j * CT + (t + 1))
                    nc.vector.scalar_tensor_tensor(h_lo[:, t, :], pre[:, t, :], 0.0, h_hi[:, t, :].bitcast(F32),
                                                   ALU.max, ALU.subtract).then_inc(h_ready, 1)
                if first:
                    dve.wait_ge(col_ready, 1)
                    nc.vector.tensor_copy(inv_col[0:M, :], ps_t[1][0:M, 0, 0:NT]).then_inc(inv_ready, 1)

            dve.sem_inc(mean_ready, CT)
            dve.sem_inc(pre_ready, CT)
            dve.sem_inc(p_ready, 1)
            dve.wait_ge(bias_in, 16)
            dve.sem_inc(wn_ready, 1)
            dve.sem_inc(ws_ready, 1)
            chunk(0, first=True)
            with dve.Fori(1, KC - 1) as j:
                chunk(j)
            chunk(KC - 1, last=True)

        @block.tensor
        def _(pe):
            def degrees():
                for t in range(CT):
                    pe.wait_ge(adj_in[t], 32)
                    for a in range(NT):
                        last = pe.matmul(ps_n[t][:, 0:CW], ones_r[0:M, :], adj[0:M, a, cols(t)],
                                         start=(a == 0), stop=(a == NT - 1))
                    last.then_inc(deg_ready, 1)

            def turn_degrees():
                pe.wait_ge(inv_ready, CT)
                for a in range(NT):
                    last = pe.transpose(ps_t[1][0:M, 0, a:a + 1], inv_row[0:1, a * M:(a + 1) * M], ident[0:1, 0:1])
                last.then_inc(col_ready, 1)

            def chunk(j, first=False):
                if first:
                    pe.sem_inc(n_done, CT)
                else:
                    pe.wait_ge(wn_ready, j + 1)
                for t in range(0 if first else CT):
                    pe.wait_ge(mean_ready, j * CT + (t + 1))
                    exact_product(pe, ps_n[t][:, 0:CW],
                                  [(wn_hi[:, k, :], wn_lo[:, k, :], xT_hi[:, k, cols(t)], xT_lo[:, k, cols(t)])
                                   for k in range(KC)]).then_inc(n_done, 1)
                pe.wait_ge(ws_ready, j + 1)

                def self_product(t):
                    pe.wait_ge(pre_ready, j * CT + (t + 1))
                    exact_product(pe, ps_s[t][:, 0:CW],
                                  [(ws_hi[:, k, :], ws_lo[:, k, :], xT_hi[:, k, cols(t)], xT_lo[:, k, cols(t)])
                                   for k in range(KC)]).then_inc(s_done, 1)

                def turn(g):
                    pe.wait_ge(p_ready, j * 3 + (1, 1, 2)[g])
                    if g == 1 and not first:
                        pe.wait_ge(inv_ready, CT + 1)
                    a, b = TURNS[g]
                    for n in range(a, b):
                        last = pe.transpose(ps_t[g % 2][0:M, n - a, :], pT[:, n * M:(n + 1) * M], ident[:, :])
                    last.then_inc(turned, 1)

                self_product(0)
                pe.wait_ge(pT_ready, j * CT + CT)
                turn(0)
                turn(1)
                self_product(1)
                turn(2)
                self_product(2)
                if first:
                    degrees()
                pe.wait_ge(p_ready, j * 3 + 4)
                for t in range(CT):
                    if first:
                        pe.wait_ge(clamped, t + 1)
                    for a in range(NT):
                        pe.matmul(ps_n[t][:, 0:CW], p_hi[0:M, a, :], adj[0:M, a, cols(t)],
                                  start=(a == 0), stop=False)
                        last = pe.matmul(ps_n[t][:, 0:CW], p_lo[0:M, a, :], adj[0:M, a, cols(t)],
                                         start=False, stop=(a == NT - 1))
                    last.then_inc(agg_done, 1)
                if first:
                    turn_degrees()

            chunk(0, first=True)
            with pe.Fori(1, KC) as j:
                chunk(j)


HEADS, HD, NF = 16, 64, 256
HP = HEADS // 2
VW = HD + 2
PAIR = 2 * M
STEPS = NT // 2
EPS_Z = 1e-6


def stage_attention(nc, w_qkv, proj, xT_hi, xT_lo, ident, oT_hi_dram, oT_lo_dram, panel_k, panel_v, vT,
                    w_neigh, w_self):
    with ExitStack() as stack:
        m = Pool(nc, stack, "att")
        panels = {"q": Panel(m), "k": panel_k, "v": panel_v}
        raw, w_hi, w_lo = ({n: part(w) for n, w in panels.items()}
                           for part in (lambda w: w.raw, lambda w: w.hi, lambda w: w.lo))
        headT = {n: [m.sb(f"{n}T_{h}", [P, NP], F32R) for h in range(2)] for n in "qk"}
        v_hi = m.sb("v_hi", [P, NT, 2, VW], F32R)
        v_lo = m.sb("v_lo", [P, NT, 2, VW], F32R)
        raw_p = m.sb("raw_p", [P, 2 * NF], F32)
        pj_hi = m.sb("pj_hi", [P, 2 * NF], F32R)
        pj_lo = m.sb("pj_lo", [P, 2 * NF], F32R)
        neg_max = m.sb("neg_max", [P, 2, 2], F32)
        feat = m.sb("feat", [P, 2, 2 * NF], F32)
        k_hi = m.sb("k_hi", [P, 2, 2 * NF], F32R)
        k_lo = m.sb("k_lo", [P, 2, 2 * NF], F32R)
        qf_hi = m.sb("qf_hi", [P, 2, 4, PAIR], F32R)
        qf_lo = m.sb("qf_lo", [P, 2, 4, PAIR], F32R)
        kvT = m.sb("kvT", [VW, 2 * NF], F32)
        kv_hi = m.sb("kv_hi", [P, 4, P], F32R)
        kv_lo = m.sb("kv_lo", [P, 4, P], F32R)
        den = m.sb("den", [P, PAIR], F32)
        att = m.sb("att", [P, PAIR], F32)
        att_hi = m.sb("att_hi", [P, PAIR], F32R)
        att_lo = m.sb("att_lo", [P, PAIR], F32R)
        ps_g = [m.psum(f"ps_g{i}", [P, BANK]) for i in range(2)]
        ps_z = [m.psum(f"ps_z{i}", [P, BANK]) for i in range(2)]
        ps_t = [m.psum(f"ps_t{i}", [P, BANK]) for i in range(2)]
        ps_kv = m.psum("ps_kv", [P, BANK])
        ps_o = m.psum("ps_o", [P, BANK])
        raw_in = {n: m.sem(f"raw_{n}_in") for n in "qkvp"}
        w_hi_ready = {n: m.sem(f"w{n}_hi_ready") for n in "qkv"}
        w_ready = {n: m.sem(f"w{n}_ready") for n in "qkv"}
        pj_hi_ready = m.sem("pj_hi_ready")
        pj_ready = m.sem("pj_ready")
        g_done = {n: m.sem(f"{n}_done") for n in "qkv"}
        t_hi_ready = {n: m.sem(f"{n}T_hi_ready") for n in "qk"}
        t_ready = {n: m.sem(f"{n}T_ready") for n in "qkv"}
        z_done = m.sem("z_done")
        max_ready = m.sem("max_ready")
        feat_ready = m.sem("feat_ready")
        k_hi_ready = m.sem("k_hi_ready")
        k_ready = m.sem("k_ready")
        kv_added = m.sem("kv_added")
        kvT_ready = m.sem("kvT_ready")
        kv_turned = m.sem("kv_turned")
        kv_hi_ready = m.sem("kv_hi_ready")
        kv_ready = m.sem("kv_ready")
        q_turned = m.sem("q_turned")
        qf_hi_ready = m.sem("qf_hi_ready")
        qf_ready = m.sem("qf_ready")
        v_turned = m.sem("v_turned")
        v_hi_ready = m.sem("v_hi_ready")
        v_ready = m.sem("v_ready")
        out_done = m.sem("out_done")
        den_ready = m.sem("den_ready")
        inv_ready = m.sem("inv_ready")
        att_ready = m.sem("att_ready")
        att_hi_ready = m.sem("att_hi_ready")
        att_split = m.sem("att_split")
        att_out = m.sem("att_out")
        n_done = m.sem("n_done")
        n_kept = m.sem("n_kept")
        blank = m.sem("blank")
        held = m.sem("held")
        block = stack.enter_context(nc.Block())
        cols = lambda t: slice(t * CW, (t + 1) * CW)
        tile = lambda t: slice(t * M, (t + 1) * M)
        half = lambda t: slice((t % 2) * M, (t % 2) * M + M)
        HALVES = (slice(0, HD), slice(HD, P))
        OFF = {"q": 0, "k": 1, "v": 2}
        BANKS = {"q": ((1, "k", 0, 3), (0, "k", 0, 2), (1, "q", 0, 1)),
                 "v": ((0, "q", -1, 2), (1, "q", -1, 3), (0, "v", 0, 1)),
                 "k": ((1, "v", 0, 2), (0, "v", 0, 3), (1, "k", 0, 1))}

        READY = {"q": 2, "k": 2, "v": 1}

        @block.sync
        def _(sp):
            def load_w(n, hp):
                sp.dma_start(raw[n][:, :, :], panel(w_qkv[:, OFF[n] * D:(OFF[n] + 1) * D], hp)).then_inc(raw_in[n], 16)

            def load_p(hp):
                for r in HALVES:
                    sp.dma_start(raw_p[r, :].rearrange("d (h f) -> d h f", h=2),
                                 proj[ds(hp * 2, 2), :, :].rearrange("h d f -> d h f")).then_inc(raw_in["p"], 16)

            def store(hp, s):
                sp.wait_ge(att_split, hp * STEPS + (s + 2))
                sp.dma_start(oT_hi_dram[ds(hp * P, P), s * PAIR:(s + 1) * PAIR], att_hi[:, :].bitcast(F32)).then_inc(att_out, 16)
                sp.dma_start(oT_lo_dram[ds(hp * P, P), s * PAIR:(s + 1) * PAIR], att_lo[:, :].bitcast(F32)).then_inc(att_out, 16)

            def pair(hp, after_next, first=False, last=False):
                if not first:
                    for s in (STEPS - 2, STEPS - 1):
                        store(hp - 1, s)
                if not last:
                    sp.wait_ge(w_ready["q"], hp + 1)
                    load_w("q", hp + 1)
                    sp.wait_ge(pj_ready, hp + 1)
                    load_p(hp + 1)
                    for n in "vk":
                        sp.wait_ge(w_ready[n], hp + 2)
                        if after_next is None:
                            sp.dma_start(raw[n][:, :, :], panel(w_neigh if n == "k" else w_self, 0)).then_inc(raw_in[n], 16)
                        else:
                            load_w(n, after_next)
                for s in range(STEPS - 2):
                    store(hp, s)

            for n in "vkq":
                load_w(n, 0)
            load_p(0)
            for n in "vk":
                sp.wait_ge(w_ready[n], 1)
                load_w(n, 1)
            pair(0, 2, first=True)
            with sp.Fori(1, HP - 2) as hp:
                pair(hp, hp + 2)
            pair(HP - 2, None)
            pair(HP - 1, None, last=True)
            for s in (STEPS - 2, STEPS - 1):
                store(HP - 1, s)
            sp.wait_ge(att_out, 32 * HP * STEPS + 32)

        @block.gpsimd
        def _(pool):
            def split_w(n, hp):
                pool.wait_ge(raw_in[n], hp * 16 + 16)
                pool.sem_inc(held, 1)
                nc.gpsimd.tensor_copy(w_hi[n][:, :, :], raw[n][:, :, :]).then_inc(w_hi_ready[n], 1)

            def split_att(hp, s):
                pool.wait_ge(att_ready, hp * STEPS + (s + 2))
                pool.wait_ge(att_out, hp * (32 * STEPS) + 32 * (s + 1))
                pool.sem_inc(held, 1)
                nc.gpsimd.tensor_copy(att_hi[:, :], att[:, :]).then_inc(att_hi_ready, 1)
                pool.wait_ge(att_hi_ready, hp * STEPS + (s + 1))
                nc.gpsimd.tensor_tensor(att_lo[:, :], att[:, :], att_hi[:, :].bitcast(F32),
                                        ALU.subtract).then_inc(att_split, 1)

            def pair(hp, first=False, last=False):
                if not first:
                    for s in (STEPS - 2, STEPS - 1):
                        split_att(hp - 1, s)
                for s in range(1, STEPS):
                    if not last and s == 1:
                        pool.wait_ge(g_done["q"], hp * CT + CT)
                        split_w("q", hp + 1)
                    if not last and s == 3:
                        pool.wait_ge(g_done["v"], hp * CT + 2 * CT)
                        split_w("v", hp + 2)
                    if s >= 2:
                        split_att(hp, s - 2)
                if not last:
                    pool.wait_ge(g_done["k"], hp * CT + 2 * CT)
                    split_w("k", hp + 2)

            pool.sem_inc(att_split, 1)
            pool.sem_inc(att_out, 32)
            for n in "vk":
                pool.wait_ge(g_done[n], CT)
                split_w(n, 1)
            pair(0, first=True)
            with pool.Fori(1, HP - 1) as hp:
                pair(hp)
            pair(HP - 1, last=True)
            for s in (STEPS - 2, STEPS - 1):
                split_att(HP - 1, s)

        @block.scalar
        def _(act):
            def keep(n, hp, t):
                act.wait_ge(g_done[n], hp * CT + (t + 1))
                src = ps_g[BANKS[n][t][0]][:, 0:CW]
                if n == "v":
                    nc.scalar.copy(vT[:, cols(t)], src).then_inc(t_ready["v"], 1)
                else:
                    for h, r in enumerate(HALVES):
                        nc.scalar.copy(headT[n][h][r, cols(t)], ps_g[BANKS[n][t][0]][r, 0:CW]).then_inc(t_hi_ready[n], 1)

            def features(hp, t, i):
                act.wait_ge(max_ready, hp * (2 * NT) + (i + 1))
                if i < NT:
                    act.wait_ge(k_ready, hp * NT + (t + 1))
                    if t < 2:
                        act.wait_ge(q_turned, hp * NT + 2)
                else:
                    act.wait_ge(q_turned, hp * NT + (t + 1))
                    if t < 2:
                        act.wait_ge(k_ready, hp * NT + (NT + 2))
                for h in range(2):
                    last = nc.scalar.activation(feat[0:M, t % 2, h * NF:(h + 1) * NF],
                                                ps_z[t % 2][0:M, h * NF:(h + 1) * NF], ACT.Exp,
                                                bias=neg_max[0:M, t % 2, h:h + 1])
                last.then_inc(feat_ready, 1)
                if i < NT:
                    act.wait_ge(feat_ready, hp * (2 * NT) + (t + 3))
                    act.wait_ge(kv_added, hp * NT + (t + 1))
                    nc.scalar.copy(k_hi[0:M, t % 2, :], feat[0:M, t % 2, :]).then_inc(k_hi_ready, 1)

            def split_p(hp):
                act.wait_ge(raw_in["p"], hp * 32 + 32)
                nc.scalar.copy(pj_hi[:, :], raw_p[:, :]).then_inc(pj_hi_ready, 1)

            def keep_kvT(hp):
                act.wait_ge(kv_added, hp * NT + (NT + 2))
                nc.scalar.copy(kvT[:, :], ps_kv[0:VW, :]).then_inc(kvT_ready, 1)

            def keep_kv(hp):
                act.wait_ge(kv_turned, hp + 1)
                kv = ps_o[:, 0:4 * VW].rearrange("p (c w) -> p c w", w=VW)
                for h in range(2):
                    here, there = slice(h * HD, (h + 1) * HD), slice((1 - h) * HD, (2 - h) * HD)
                    nc.scalar.copy(kv_hi[:, 2 * h:2 * h + 2, here], kv[:, 2 * h:2 * h + 2, 0:HD])
                    last = nc.scalar.copy(kv_hi[:, 2 * h:2 * h + 2, there],
                                          kv[:, 2 * h:2 * h + 2, HD:HD + 1].to_broadcast([P, 2, HD]))
                last.then_inc(kv_hi_ready, 1)

            def keep_turned(hp, t):
                act.wait_ge(q_turned, hp * NT + (t + 3))
                s = t // 2
                act.wait_ge(out_done, hp * STEPS + max(s, 1))
                nc.scalar.copy(qf_hi[:, s % 2, :, half(t)], ps_t[t % 2][:, 0:4 * M].rearrange("p (c n) -> p c n", n=M)
                               ).then_inc(qf_hi_ready, 1)

            def keep_v(hp, g):
                a, b = TURNS[g]
                act.wait_ge(v_turned, hp * 3 + (g + 1))
                nc.scalar.copy(v_hi[0:M, a:b, :, 0:HD],
                               ps_kv[0:M, 0:(b - a) * P].rearrange("p (a h d) -> p a h d", h=2, d=HD)
                               ).then_inc(v_hi_ready, 1)

            def denominators(hp, s):
                act.wait_ge(out_done, hp * STEPS + (s + 2))
                nc.scalar.activation(den[0:HD, :], ps_o[HD:P, 0:PAIR], ACT.Copy, bias=EPS_Z)
                nc.scalar.activation(den[HD:P, :], ps_o[0:HD, PAIR:2 * PAIR], ACT.Copy,
                                     bias=EPS_Z).then_inc(den_ready, 1)

            def pair(hp, first=False, last=False):
                for s in range(STEPS):
                    features(hp, 2 * s, 2 * s)
                    features(hp, 2 * s + 1, 2 * s + 1)
                    for t in {1: (0,), 3: (1,), 4: (2,)}.get(s, ()):
                        keep("q", hp, t)
                    if s == 1 and not first:
                        denominators(hp - 1, STEPS - 1)
                for s in range(STEPS):
                    features(hp, 2 * s, NT + 2 * s)
                    features(hp, 2 * s + 1, NT + 2 * s + 1)
                    if s == 0:
                        keep_kvT(hp)
                    else:
                        if s == STEPS - 1 and not last:
                            act.wait_ge(z_done, hp * (2 * NT) + 2 * NT)
                            split_p(hp + 1)
                        keep_turned(hp, 2 * s - 2)
                        keep_turned(hp, 2 * s - 1)
                    if not last:
                        if s >= 3:
                            keep_v(hp + 1, s - 3)
                        for n, t in {0: (("v", 0),), 1: (("v", 1),), 2: (("v", 2),), 3: (("k", 0), ("k", 1)),
                                     4: (("k", 2),)}[s]:
                            keep(n, hp + 1, t)
                    else:
                        for t in {1: (0,), 3: (1,), 4: (2,)}.get(s, ()):
                            act.wait_ge(n_done, t + 1)
                            nc.scalar.copy(vT[:, cols(t)], ps_g[t % 2][:, 0:CW]).then_inc(n_kept, 1)
                    if s == 0:
                        keep_kv(hp)
                    else:
                        denominators(hp, s - 1)
                if not last:
                    keep_v(hp + 1, 2)
                keep_turned(hp, NT - 2)
                keep_turned(hp, NT - 1)

            for n in "vkq":
                act.wait_ge(raw_in[n], 16)
                nc.scalar.copy(w_hi[n][:, :, :], raw[n][:, :, :]).then_inc(w_hi_ready[n], 1)
            act.wait_ge(blank, 2)
            split_p(0)
            for n in "vk":
                for t in range(CT):
                    keep(n, 0, t)
            for g in range(3):
                keep_v(0, g)
            pair(0, first=True)
            with act.Fori(1, HP - 1) as hp:
                pair(hp)
            pair(HP - 1, last=True)
            denominators(HP - 1, STEPS - 1)

        @block.vector
        def _(dve):
            def split_w(n, hp):
                dve.wait_ge(w_hi_ready[n], hp + 1)
                nc.vector.tensor_tensor(w_lo[n][:, :, :], raw[n][:, :, :], w_hi[n][:, :, :].bitcast(F32),
                                        ALU.subtract).then_inc(w_ready[n], 1)

            def keep(n, hp, t):
                for h, r in enumerate(HALVES):
                    dve.wait_ge(t_hi_ready[n], hp * (2 * CT) + (2 * t + h + 1))
                    nc.vector.tensor_tensor(headT[n][h][HALVES[1 - h], cols(t)], ps_g[BANKS[n][t][0]][r, 0:CW],
                                            headT[n][h][r, cols(t)].bitcast(F32), ALU.subtract).then_inc(t_ready[n], 1)

            def maximum(hp, t, i):
                dve.wait_ge(z_done, hp * (2 * NT) + (i + 1))
                nc.vector.tensor_reduce(neg_max[0:M, t % 2, :], ps_z[t % 2][0:M, :].rearrange("p (h f) -> p h f", h=2),
                                        AX_X, ALU.max, negate=True).then_inc(max_ready, 1)

            def split_k(hp, t):
                dve.wait_ge(k_hi_ready, hp * NT + (t + 1))
                nc.vector.tensor_tensor(k_lo[0:M, t % 2, :], feat[0:M, t % 2, :], k_hi[0:M, t % 2, :].bitcast(F32),
                                        ALU.subtract).then_inc(k_ready, 1)

            def split_p(hp):
                dve.wait_ge(pj_hi_ready, hp + 1)
                nc.vector.tensor_tensor(pj_lo[:, :], raw_p[:, :], pj_hi[:, :].bitcast(F32), ALU.subtract).then_inc(pj_ready, 1)

            def keep_kv(hp):
                dve.wait_ge(kv_hi_ready, hp + 1)
                kv = ps_o[:, 0:4 * VW].rearrange("p (c w) -> p c w", w=VW)
                for h in range(2):
                    here, there = slice(h * HD, (h + 1) * HD), slice((1 - h) * HD, (2 - h) * HD)
                    nc.vector.tensor_tensor(kv_lo[:, 2 * h:2 * h + 2, here], kv[:, 2 * h:2 * h + 2, 0:HD],
                                            kv_hi[:, 2 * h:2 * h + 2, here].bitcast(F32), ALU.subtract)
                    last = nc.vector.tensor_tensor(kv_lo[:, 2 * h:2 * h + 2, there],
                                                   kv[:, 2 * h:2 * h + 2, HD:HD + 1].to_broadcast([P, 2, HD]),
                                                   kv_hi[:, 2 * h:2 * h + 2, there].bitcast(F32), ALU.subtract)
                last.then_inc(kv_ready, 1)

            def keep_turned(hp, t):
                dve.wait_ge(qf_hi_ready, hp * NT + (t + 1))
                s = t // 2
                nc.vector.tensor_tensor(qf_lo[:, s % 2, :, half(t)], ps_t[t % 2][:, 0:4 * M].rearrange("p (c n) -> p c n", n=M),
                                        qf_hi[:, s % 2, :, half(t)].bitcast(F32), ALU.subtract).then_inc(qf_ready, 1)

            def keep_v(hp, g):
                a, b = TURNS[g]
                dve.wait_ge(v_hi_ready, hp * 3 + (g + 1))
                nc.vector.tensor_tensor(v_lo[0:M, a:b, :, 0:HD],
                                        ps_kv[0:M, 0:(b - a) * P].rearrange("p (a h d) -> p a h d", h=2, d=HD),
                                        v_hi[0:M, a:b, :, 0:HD].bitcast(F32), ALU.subtract).then_inc(v_ready, 1)

            def divide(hp, s):
                dve.wait_ge(den_ready, hp * STEPS + (s + 1))
                nc.vector.reciprocal(den[:, :], den[:, :]).then_inc(inv_ready, 1)
                dve.wait_ge(inv_ready, hp * STEPS + (s + 1))
                dve.wait_ge(att_split, hp * STEPS + (s + 1))
                nc.vector.tensor_tensor(att[0:HD, :], ps_o[0:HD, 0:PAIR], den[0:HD, :], ALU.mult)
                nc.vector.tensor_tensor(att[HD:P, :], ps_o[HD:P, PAIR:2 * PAIR], den[HD:P, :],
                                        ALU.mult).then_inc(att_ready, 1)

            def pair(hp, first=False, last=False):
                for s in range(STEPS):
                    maximum(hp, 2 * s, 2 * s)
                    maximum(hp, 2 * s + 1, 2 * s + 1)
                    if s in (0, 2) and not first:
                        divide(hp - 1, STEPS - 2 + s // 2)
                    split_k(hp, 2 * s)
                    split_k(hp, 2 * s + 1)
                    for t in {1: (0,), 3: (1,), 4: (2,)}.get(s, ()):
                        keep("q", hp, t)
                    if s == 1 and not first:
                        split_w("k", hp + 1)
                for s in range(STEPS):
                    maximum(hp, 2 * s, NT + 2 * s)
                    maximum(hp, 2 * s + 1, NT + 2 * s + 1)
                    if s >= 2:
                        divide(hp, s - 2)
                    if s == 0:
                        keep_kv(hp)
                    else:
                        keep_turned(hp, 2 * s - 2)
                        keep_turned(hp, 2 * s - 1)
                    if not last:
                        if s == 1:
                            split_w("q", hp + 1)
                        if s >= 3:
                            keep_v(hp + 1, s - 3)
                        if s == STEPS - 1:
                            split_p(hp + 1)
                        if s == 3:
                            keep("k", hp + 1, 0)
                            split_w("v", hp + 2)
                            keep("k", hp + 1, 1)
                        if s == 4:
                            keep("k", hp + 1, 2)
                if not last:
                    keep_v(hp + 1, 2)
                keep_turned(hp, NT - 2)
                keep_turned(hp, NT - 1)

            nc.vector.memset(v_hi[:, :, :, HD:HD + 1].bitcast(F32), 1.0)
            nc.vector.memset(v_hi[:, :, :, HD + 1:VW].bitcast(F32), 0.0).then_inc(blank, 1)
            nc.vector.memset(v_lo[:, :, :, HD:VW].bitcast(F32), 0.0).then_inc(blank, 1)
            dve.sem_inc(k_ready, 2)
            dve.sem_inc(att_ready, 1)
            for n in "vkq":
                split_w(n, 0)
            split_p(0)
            for t in range(CT):
                keep("k", 0, t)
            for g in range(3):
                keep_v(0, g)
            for n in "vk":
                split_w(n, 1)
            pair(0, first=True)
            with dve.Fori(1, HP - 1) as hp:
                pair(hp)
            pair(HP - 1, last=True)
            for s in (STEPS - 2, STEPS - 1):
                divide(HP - 1, s)

        @block.tensor
        def _(pe):
            def gemm(n, hp, first, count, start_up=False):
                for u in range(first, first + count):
                    t, k = divmod(u, KC)
                    bank, whose, ahead, c = BANKS[n][t]
                    if u == 0:
                        pe.wait_ge(w_ready[n], hp + 1)
                    if k == 0 and not (start_up and whose == "q"):
                        n_of = READY[whose]
                        pe.wait_ge(t_ready[whose], hp * (n_of * CT) + n_of * (ahead * CT + c))
                    out = ps_g[bank][:, 0:CW]
                    pe.matmul(out, w_hi[n][:, k, :], xT_hi[:, k, cols(t)], start=(k == 0), stop=False)
                    pe.matmul(out, w_hi[n][:, k, :], xT_lo[:, k, cols(t)], start=False, stop=False)
                    last = pe.matmul(out, w_lo[n][:, k, :], xT_hi[:, k, cols(t)], start=False, stop=(k == KC - 1))
                    if k == KC - 1:
                        last.then_inc(g_done[n], 1)

            def neighbours(u):
                t, k = divmod(u, KC)
                if u == 0:
                    pe.wait_ge(w_ready["k"], HP + 1)
                    pe.wait_ge(t_ready["q"], HP * 2 * CT)
                if u == 2 * KC:
                    pe.wait_ge(n_kept, 1)
                out = ps_g[t % 2][:, 0:CW]
                pe.matmul(out, w_hi["k"][:, k, :], xT_hi[:, k, cols(t)], start=(k == 0), stop=False)
                pe.matmul(out, w_hi["k"][:, k, :], xT_lo[:, k, cols(t)], start=False, stop=False)
                last = pe.matmul(out, w_lo["k"][:, k, :], xT_hi[:, k, cols(t)], start=False, stop=(k == KC - 1))
                if k == KC - 1:
                    last.then_inc(n_done, 1)

            def project(n, hp, t, i):
                pe.wait_ge(feat_ready, hp * (2 * NT) + (i + 1))
                if t % 4 == 0 or t == NT - 1:
                    pe.wait_ge(t_ready[n], hp * (2 * CT) + 2 * min(CT, ((t + 4) * M - 1) // CW + 1))
                for h in range(2):
                    at = slice(h * NF, (h + 1) * NF)
                    pe.matmul(ps_z[t % 2][0:M, at], headT[n][h][:, tile(t)], pj_hi[:, at], start=True, stop=False)
                    last = pe.matmul(ps_z[t % 2][0:M, at], headT[n][h][:, tile(t)], pj_lo[:, at], start=False, stop=True)
                last.then_inc(z_done, 1)

            def add_kv(hp, t):
                pe.wait_ge(k_ready, hp * NT + (t + 3))
                for h in range(2):
                    at = slice(h * NF, (h + 1) * NF)
                    for n, (l, r) in enumerate(((v_hi, k_hi), (v_lo, k_hi), (v_hi, k_lo))):
                        last = pe.matmul(ps_kv[0:VW, at], l[0:M, t, h, :], r[0:M, t % 2, at],
                                         start=(t == 0 and h == 0 and n == 0), stop=(t == NT - 1 and n == 2),
                                         skip_group_check=True)
                last.then_inc(kv_added, 1)

            def turn_kv(hp):
                pe.wait_ge(kvT_ready, hp + 1)
                pe.wait_ge(att_ready, hp * STEPS + 1)
                for f in range(4):
                    last = pe.transpose(ps_o[:, f * VW:(f + 1) * VW], kvT[:, f * P:(f + 1) * P], ident[0:VW, 0:VW])
                last.then_inc(kv_turned, 1)

            def turn_q(hp, t):
                pe.wait_ge(feat_ready, hp * (2 * NT) + (NT + t + 3))
                if t >= 2:
                    pe.wait_ge(qf_ready, hp * NT + (t - 1))
                for f in range(4):
                    last = pe.transpose(ps_t[t % 2][:, f * M:(f + 1) * M], feat[0:M, t % 2, f * P:(f + 1) * P],
                                        ident[0:M, 0:M])
                last.then_inc(q_turned, 1)

            def turn_v(hp, g):
                if g == 0:
                    pe.wait_ge(t_ready["v"], hp * CT + CT)
                else:
                    pe.wait_ge(v_ready, hp * 3 + g)
                a, b = TURNS[g]
                for n in range(a, b):
                    last = pe.transpose(ps_kv[0:M, (n - a) * P:(n - a + 1) * P], vT[:, tile(n)], ident[:, :])
                last.then_inc(v_turned, 1)

            def multiply(hp, s):
                pe.wait_ge(qf_ready, hp * NT + (2 * s + 2))
                if s == 0:
                    pe.wait_ge(kv_ready, hp + 1)
                pe.wait_ge(att_ready, hp * STEPS + (s + 1))
                for h in range(2):
                    last = exact_product(pe, ps_o[:, h * PAIR:(h + 1) * PAIR],
                                         [(kv_hi[:, f, :], kv_lo[:, f, :], qf_hi[:, s % 2, f, :], qf_lo[:, s % 2, f, :])
                                          for f in (2 * h, 2 * h + 1)])
                last.then_inc(out_done, 1)

            def pair(hp, first=False, last=False):
                for s in range(STEPS):
                    if s == 0:
                        pe.wait_ge(pj_ready, hp + 1)
                    project("k", hp, 2 * s, 2 * s)
                    project("k", hp, 2 * s + 1, 2 * s + 1)
                    if s == 1:
                        pe.wait_ge(v_ready, hp * 3 + 3)
                    if s:
                        add_kv(hp, 2 * s - 2)
                        add_kv(hp, 2 * s - 1)
                    gemm("q", hp, 5 * s, min(5, CT * KC - 5 * s))
                    if s == 1 and not first:
                        multiply(hp - 1, STEPS - 1)
                units = [("v", u) for u in range(CT * KC)] + [("k", u) for u in range(CT * KC)]
                for s in range(STEPS):
                    project("q", hp, 2 * s, NT + 2 * s)
                    project("q", hp, 2 * s + 1, NT + 2 * s + 1)
                    if s == 0:
                        add_kv(hp, NT - 2)
                        add_kv(hp, NT - 1)
                    else:
                        turn_q(hp, 2 * s - 2)
                        turn_q(hp, 2 * s - 1)
                    if not last:
                        if s >= 3:
                            turn_v(hp + 1, s - 3)
                        for n, u in units[10 * s:10 * s + 10]:
                            gemm(n, hp + 1, u, 1)
                    else:
                        for u in range(5 * s, min(5 * s + 5, CT * KC)):
                            neighbours(u)
                    if s == 0:
                        turn_kv(hp)
                    else:
                        multiply(hp, s - 1)
                if not last:
                    turn_v(hp + 1, 2)
                turn_q(hp, NT - 2)
                turn_q(hp, NT - 1)

            pe.sem_inc(feat_ready, 2)
            pe.sem_inc(kv_added, 2)
            pe.sem_inc(q_turned, 2)
            pe.sem_inc(out_done, 1)
            pe.wait_ge(blank, 2)
            gemm("v", 0, 0, CT * KC, start_up=True)
            gemm("k", 0, 0, CT * KC, start_up=True)
            for g in range(3):
                turn_v(0, g)
            pair(0, first=True)
            with pe.Fori(1, HP - 1) as hp:
                pair(hp)
            pair(HP - 1, last=True)
            multiply(HP - 1, STEPS - 1)


def stage_sage1(nc, w_neigh, w_self, hT_hi_dram, hT_lo_dram, adj, inv_col, mid_dram, raw_n):
    with ExitStack() as stack:
        m = Pool(nc, stack, "sage1")
        hT_hi = m.sb("hT_hi", [P, KC, N], F32R)
        hT_lo = m.sb("hT_lo", [P, KC, N], F32R)
        raw = {"n": raw_n, "s": m.sb("raw_s", [P, KC, PW], F32)}
        w_hi = {n: m.sb(f"w{n}_hi", [P, KC, PW], F32R) for n in "ns"}
        w_lo = {n: m.sb(f"w{n}_lo", [P, KC, PW], F32R) for n in "ns"}
        p_hi = m.sb("p_hi", [P, NT, PW], F32R)
        p_lo = m.sb("p_lo", [P, NT, PW], F32R)
        mean = m.sb("mean", [P, 2, PW], F32)
        mid = m.sb("mid", [P, 2, PW], F32)
        ps_p = [m.bank(f"ps_p{i}") for i in range(2)]
        ps_a = [m.bank(f"ps_a{i}") for i in range(2)]
        ps_s = [m.bank(f"ps_s{i}") for i in range(2)]
        h_in = [m.sem(f"h_in{i}") for i in range(PAIRS)]
        raw_in = {n: m.sem(f"raw_{n}_in") for n in "ns"}
        w_hi_ready = {n: m.sem(f"w{n}_hi_ready") for n in "ns"}
        w_ready = {n: m.sem(f"w{n}_ready") for n in "ns"}
        p_done = m.sem("p_done")
        p_hi_ready = m.sem("p_hi_ready")
        p_ready = m.sem("p_ready")
        agg_done = m.sem("agg_done")
        self_done = m.sem("self_done")
        mean_ready = m.sem("mean_ready")
        mid_ready = m.sem("mid_ready")
        mid_out = [m.sem(f"mid_out{i}") for i in range(2)]
        block = stack.enter_context(nc.Block())
        NPAN = D // PW
        tile = lambda t: slice(t * M, (t + 1) * M)

        @block.sync
        def _(sp):
            def load_w(n, j):
                sp.dma_start(raw[n][:, :, :], panel(w_neigh if n == "n" else w_self, j, PW)).then_inc(raw_in[n], 16)

            sp.sem_inc(raw_in["n"], 16)
            for i in range(PAIRS):
                at = slice(2 * i * M, 2 * (i + 1) * M)
                for part, dram in ((hT_hi, hT_hi_dram), (hT_lo, hT_lo_dram)):
                    sp.dma_start(part[:, :, at].bitcast(F32), dram[:, at].rearrange("(c p) n -> p c n", p=P)
                                 ).then_inc(h_in[i], 16)
                if i == 1:
                    load_w("s", 0)

            def step(j, last=False):
                if not last:
                    for n in "ns":
                        sp.wait_ge(w_ready[n], j + 1)
                        load_w(n, j + 1)
                for t in range(NT):
                    sp.wait_ge(mid_ready, j * NT + (t + 3))
                    sp.dma_start(mid_dram[tile(t), ds(j * PW, PW)], mid[0:M, t % 2, :]).then_inc(mid_out[t % 2], 16)

            with sp.Fori(0, NPAN - 1) as j:
                step(j)
            step(NPAN - 1, last=True)
            for i in range(2):
                sp.wait_ge(mid_out[i], 16 * (NPAN * NT // 2 + 1))

        @block.scalar
        def _(act):
            def split_w(n, j):
                act.wait_ge(raw_in[n], j * 16 + 16)
                nc.scalar.copy(w_hi[n][:, :, :], raw[n][:, :, :]).then_inc(w_hi_ready[n], 1)

            def step(j, last=False):
                for t in range(NT):
                    act.wait_ge(p_done, j * NT + (t + 1))
                    nc.scalar.copy(p_hi[0:M, t, :], ps_p[t % 2][0:M, 0:PW]).then_inc(p_hi_ready, 1)
                    if t == NT // 2:
                        split_w("s", j)
                if not last:
                    split_w("n", j + 1)
                for t in range(NT):
                    act.wait_ge(agg_done, j * NT + (t + 1))
                    act.wait_ge(mid_ready, j * NT + (t + 1))
                    nc.scalar.activation(mean[0:M, t % 2, :], ps_a[t % 2][0:M, 0:PW], ACT.Copy,
                                         scale=inv_col[0:M, t:t + 1]).then_inc(mean_ready, 1)

            split_w("n", 0)
            with act.Fori(0, NPAN - 1) as j:
                step(j)
            step(NPAN - 1, last=True)

        @block.vector
        def _(dve):
            def split_w(n, j):
                dve.wait_ge(w_hi_ready[n], j + 1)
                nc.vector.tensor_tensor(w_lo[n][:, :, :], raw[n][:, :, :], w_hi[n][:, :, :].bitcast(F32),
                                        ALU.subtract).then_inc(w_ready[n], 1)

            def step(j, last=False):
                for t in range(NT):
                    dve.wait_ge(p_hi_ready, j * NT + (t + 1))
                    nc.vector.tensor_tensor(p_lo[0:M, t, :], ps_p[t % 2][0:M, 0:PW], p_hi[0:M, t, :].bitcast(F32),
                                            ALU.subtract).then_inc(p_ready, 1)
                    if t == NT // 2:
                        split_w("s", j)
                if not last:
                    split_w("n", j + 1)
                for t in range(NT):
                    dve.wait_ge(self_done, j * NT + (t + 1))
                    dve.wait_ge(mean_ready, j * NT + (t + 1))
                    dve.wait_ge(mid_out[t % 2], j * (16 * NT // 2) + 16 * (t // 2 + 1))
                    nc.vector.tensor_tensor(mid[0:M, t % 2, :], ps_s[t % 2][0:M, 0:PW], mean[0:M, t % 2, :],
                                            ALU.add).then_inc(mid_ready, 1)

            dve.sem_inc(p_ready, 2)
            dve.sem_inc(mid_ready, 2)
            for i in range(2):
                dve.sem_inc(mid_out[i], 16)
            split_w("n", 0)
            with dve.Fori(0, NPAN - 1) as j:
                step(j)
            step(NPAN - 1, last=True)

        @block.tensor
        def _(pe):
            def dense(out, n, t):
                return exact_product(pe, out, [(hT_hi[:, k, tile(t)], hT_lo[:, k, tile(t)], w_hi[n][:, k, :],
                                                w_lo[n][:, k, :]) for k in range(KC)])

            with pe.Fori(0, NPAN) as j:
                pe.wait_ge(w_ready["n"], j + 1)
                for t in range(NT):
                    if t % 2 == 0:
                        pe.wait_ge(h_in[t // 2], 32)
                    pe.wait_ge(p_ready, j * NT + (t + 1))
                    dense(ps_p[t % 2][0:M, 0:PW], "n", t).then_inc(p_done, 1)
                pe.wait_ge(w_ready["s"], j + 1)
                for t in range(NT):
                    pe.wait_ge(mid_ready, j * NT + (t + 1))
                    dense(ps_s[t % 2][0:M, 0:PW], "s", t).then_inc(self_done, 1)
                    if t == 0:
                        pe.wait_ge(p_ready, j * NT + (NT + 2))
                    for a in range(NT):
                        pe.matmul(ps_a[t % 2][0:M, 0:PW], adj[0:M, a, tile(t)], p_hi[0:M, a, :],
                                  start=(a == 0), stop=False)
                        last = pe.matmul(ps_a[t % 2][0:M, 0:PW], adj[0:M, a, tile(t)], p_lo[0:M, a, :],
                                         start=False, stop=(a == NT - 1))
                    last.then_inc(agg_done, 1)


def stage_mix(nc, w_out, b_graph, b_out, x, oT_hi_dram, oT_lo_dram, mid_dram, ident_b, x1_dram, qT, unit_x,
              w1T, w1T_dram, w2T, w2T_dram):
    with ExitStack() as stack:
        m = Pool(nc, stack, "mix")
        raw = m.sb("raw", [P, D // PW, KC, PW], F32)
        w_hi = m.sb("w_hi", [P, KC, D], F32R)
        w_lo = m.sb("w_lo", [P, KC, D], F32R)
        bias = m.sb("bias", [P, 2, D], F32)
        o_hi = m.sb("o_hi", [P, 2, KC, M], F32R)
        o_lo = m.sb("o_lo", [P, 2, KC, M], F32R)
        mid = m.sb("mid", [P, 2, D], F32)
        x_in = m.sb("x_in", [P, 2, D], F32)
        x1 = m.sb("x1", [P, 2, D], F32)
        y = m.sb("y", [P, D], F32)
        code = m.sb("code", [P, 2, D], BF16)
        stats = m.sb("stats", [P, 2, 6], F32)
        mv = m.sb("mv", [P, 2], F32)
        rs = m.sb("rs", [P, 6], F32)
        big = m.sb("big", [P, 3], F32)
        ps_x = [m.bank(f"ps_x{i}") for i in range(4)]
        ps_t = m.psum("ps_t", [P, 2 * BANK], BF16)
        ffn_in = m.sem("ffn_in")
        raw_in = [m.sem(f"raw_in{i}") for i in range(D // PW)]
        bias_in = m.sem("bias_in")
        bias_ready = m.sem("bias_ready")
        w_hi_ready = m.sem("w_hi_ready")
        w_ready = m.sem("w_ready")
        o_in = [m.sem(f"o_in{b}") for b in range(2)]
        m_in = [m.sem(f"m_in{b}") for b in range(2)]
        sum_ready = m.sem("sum_ready")
        base_ready = m.sem("base_ready")
        x_done = m.sem("x_done")
        x1_ready = m.sem("x1_ready")
        x1_out = [m.sem(f"x1_out{b}") for b in range(2)]
        var_ready = m.sem("var_ready")
        root_ready = m.sem("root_ready")
        seen = m.sem("seen")
        code_ready = m.sem("code_ready")
        turned = m.sem("turned")
        kept = m.sem("kept")
        chain = m.sem("chain")
        block = stack.enter_context(nc.Block())
        NPAN = D // PW
        row = lambda v: v.rearrange("(a n) -> a n", a=1).to_broadcast([P, D])

        @block.sync
        def _(sp):
            def load_w(j):
                sp.dma_start(raw[:, j, :, :], panel(w_out, j, PW)).then_inc(raw_in[j], 16)

            def load_o(t, b):
                sp.dma_start(o_hi[:, b, :, :].bitcast(F32), oT_hi_dram[:, ds(t * M, M)].rearrange("(c p) n -> p c n", p=P)).then_inc(o_in[b], 16)
                sp.dma_start(o_lo[:, b, :, :].bitcast(F32), oT_lo_dram[:, ds(t * M, M)].rearrange("(c p) n -> p c n", p=P)).then_inc(o_in[b], 16)

            def load_m(t, b):
                spread_dma(sp, mid[:, b, :], mid_dram[ds(t * M, M), :], m_in[b])
                spread_dma(sp, x_in[:, b, :], x[ds(t * M, M), :], m_in[b])

            load_w(0)
            load_w(1)
            load_o(0, 0)
            load_w(2)
            load_w(3)
            load_o(1, 1)
            for i, v in enumerate((b_graph, b_out)):
                sp.dma_start(bias[:, i, :], row(v)).then_inc(bias_in, 16)
            for b in range(2):
                load_m(b, b)
            for to, what in ((w1T, w1T_dram), (w2T, w2T_dram)):
                sp.dma_start(to[:, :, :], what).then_inc(ffn_in, 16)

            def pair(i, last=False):
                for b in range(2):
                    sp.wait_ge(x1_ready, i * 4 + (2 * b + 6))
                    spread_dma(sp, x1_dram[ds(i * (2 * M) + b * M, M), :], x1[:, b, :], x1_out[b])
                    if not last:
                        load_o(i * 2 + (b + 2), b)
                        load_m(i * 2 + (b + 2), b)

            with sp.Fori(0, PAIRS - 1) as i:
                pair(i)
            pair(PAIRS - 1, last=True)
            sp.wait_ge(ffn_in, 32)
            for b in range(2):
                sp.wait_ge(x1_out[b], 32 * PAIRS + 16)

        @block.gpsimd
        def _(pool):
            pool.wait_ge(bias_in, 32)
            nc.gpsimd.tensor_tensor(bias[:, 0, :], bias[:, 0, :], bias[:, 1, :], ALU.add).then_inc(bias_ready, 1)
            pool.wait_ge(bias_ready, 1)
            with pool.Fori(0, PAIRS) as i:
                for b in range(2):
                    pool.wait_ge(m_in[b], i * 64 + 64)
                    nc.gpsimd.tensor_tensor(mid[0:M, b, :], mid[0:M, b, :], x_in[0:M, b, :], ALU.add).then_inc(sum_ready, 1)
                    pool.wait_ge(sum_ready, i * 2 + (b + 1))
                    nc.gpsimd.tensor_tensor(mid[0:M, b, :], mid[0:M, b, :], bias[0:M, 0, :], ALU.add).then_inc(base_ready, 1)

        @block.scalar
        def _(act):
            for j in range(NPAN):
                act.wait_ge(raw_in[j], 16)
                nc.scalar.copy(w_hi[:, :, j * PW:(j + 1) * PW], raw[:, j, :, :]).then_inc(w_hi_ready, 1)

            def root(t):
                act.wait_ge(var_ready, t + 1)
                nc.scalar.activation(rs[0:M, 1:2], rs[0:M, 0:1], ACT.Sqrt).then_inc(root_ready, 1)

            def keep(t):
                act.wait_ge(turned, t + 3)
                nc.scalar.copy(qT[:, :, ds(t * M, M)], ps_t[:, :].rearrange("p (c n) -> p c n", n=P)[:, :, 0:M]).then_inc(kept, 1)

            root(0)
            root(1)
            keep(0)
            with act.Fori(1, PAIRS) as i:
                for b in range(2):
                    root(i * 2 + b)
                    keep(i * 2 + (b - 1))
            keep(NT - 1)

        @block.vector
        def _(dve):
            for b in range(2):
                dve.sem_inc(x1_out[b], 16)
            for j in range(NPAN):
                dve.wait_ge(w_hi_ready, j + 1)
                nc.vector.tensor_tensor(w_lo[:, :, j * PW:(j + 1) * PW], raw[:, j, :, :],
                                        w_hi[:, :, j * PW:(j + 1) * PW].bitcast(F32), ALU.subtract).then_inc(w_ready, 1)
            LINKS = 15
            with dve.Fori(0, PAIRS) as i:
                for b in range(2):
                    c0 = i * (2 * LINKS) + b * LINKS
                    at = [0]

                    def link(ins):
                        at[0] += 1
                        ins.then_inc(chain, 1)
                        dve.wait_ge(chain, c0 + at[0])

                    dve.wait_ge(base_ready, i * 2 + (b + 1))
                    dve.wait_ge(x1_out[b], i * 32 + 16)
                    for h in range(2):
                        dve.wait_ge(x_done, i * 4 + (2 * b + h + 1))
                        nc.vector.tensor_tensor(x1[0:M, b, h * BANK:(h + 1) * BANK], ps_x[2 * b + h][0:M, :],
                                                mid[0:M, b, h * BANK:(h + 1) * BANK], ALU.add).then_inc(x1_ready, 1)
                        dve.wait_ge(x1_ready, i * 4 + (2 * b + h + 5))
                        nc.vector.bn_stats(stats[0:M, h, :], x1[0:M, b, h * BANK:(h + 1) * BANK]).then_inc(chain, 1)
                        at[0] += 1
                    dve.wait_ge(chain, c0 + 2)
                    dve.sem_inc(seen, 1)
                    link(nc.vector.bn_aggr(mv[0:M, :], stats[0:M, :, :]))
                    nc.vector.tensor_scalar(rs[0:M, 0:1], mv[0:M, 1:2], EPS_LN, None, ALU.add).then_inc(var_ready, 1)
                    dve.wait_ge(root_ready, i * 2 + (b + 1))
                    link(nc.vector.reciprocal(rs[0:M, 2:3], rs[0:M, 1:2]))
                    link(nc.vector.tensor_tensor(rs[0:M, 3:4], rs[0:M, 2:3], rs[0:M, 2:3], ALU.mult))
                    link(nc.vector.tensor_tensor(rs[0:M, 4:5], rs[0:M, 3:4], rs[0:M, 0:1], ALU.mult))
                    link(nc.vector.tensor_scalar(rs[0:M, 4:5], rs[0:M, 4:5], -0.5, 1.5, ALU.mult, ALU.add))
                    link(nc.vector.tensor_tensor(rs[0:M, 5:6], rs[0:M, 4:5], rs[0:M, 2:3], ALU.mult))
                    link(nc.vector.tensor_scalar(y[0:M, :], x1[0:M, b, :], mv[0:M, 0:1], rs[0:M, 5:6],
                                                 ALU.subtract, ALU.mult))
                    link(nc.vector.tensor_reduce(big[0:M, 0:1], y[0:M, :], AX_X, ALU.max, apply_absolute_value=True))
                    link(nc.vector.tensor_scalar(big[0:M, 1:2], big[0:M, 0:1], EPS_Q, None, ALU.max))
                    link(nc.vector.reciprocal(big[0:M, 2:3], big[0:M, 1:2]))
                    link(nc.vector.tensor_scalar(big[0:M, 2:3], big[0:M, 2:3], 127.0, None, ALU.mult))
                    nc.vector.tensor_scalar(unit_x[0:M, ds(i * 2 + b, 1)], big[0:M, 1:2], 1.0 / 127.0, None, ALU.mult)
                    link(nc.vector.tensor_scalar(y[0:M, :], y[0:M, :], big[0:M, 2:3], ROUND, ALU.mult, ALU.add))
                    link(nc.vector.tensor_scalar(y[0:M, :], y[0:M, :], ROUND, 127.0, ALU.subtract, ALU.min))
                    dve.wait_ge(turned, i * 2 + (b + 1))
                    nc.vector.tensor_scalar(code[0:M, b, :], y[0:M, :], -128.0, None, ALU.max).then_inc(code_ready, 1)
                    assert at[0] == LINKS

        @block.tensor
        def _(pe):
            def products(i, b):
                pe.wait_ge(o_in[b], i * 32 + 32)
                for h in range(2):
                    pe.wait_ge(w_ready, NPAN // 2 * (h + 1))
                    pe.wait_ge(x1_ready, i * 4 + (2 * b + h + 1))
                    exact_product(pe, ps_x[2 * b + h][0:M, :],
                                  [(o_hi[:, b, k, :], o_lo[:, b, k, :], w_hi[:, k, h * BANK:(h + 1) * BANK],
                                    w_lo[:, k, h * BANK:(h + 1) * BANK]) for k in range(KC)]).then_inc(x_done, 1)

            def turn(t, b):
                pe.wait_ge(code_ready, t + 1)
                pe.wait_ge(kept, t + 1)
                for k in range(KC):
                    last = pe.transpose(ps_t[:, k * P:k * P + M], code[0:M, b, k * P:(k + 1) * P], ident_b[0:M, 0:M])
                last.then_inc(turned, 1)

            pe.sem_inc(x1_ready, 4)
            pe.sem_inc(turned, 2)
            pe.sem_inc(kept, 1)
            products(0, 0)
            products(0, 1)
            products(1, 0)
            turn(0, 0)
            with pe.Fori(1, PAIRS - 1) as i:
                products(i, 1)
                turn(i * 2 - 1, 1)
                products(i + 1, 0)
                turn(i * 2, 0)
            products(PAIRS - 1, 1)
            for t in range(NT - 3, NT):
                turn(t, t % 2)


def stage_ffn(nc, conv_w, conv_b, x1_dram, out, ident, ident_b, w1T, w2T, unit_w, qT, unit_x):
    with ExitStack() as stack:
        m = Pool(nc, stack, "ffn")
        cw = m.sb("cw", [P, HC, 3], F32)
        cb = m.sb("cb", [P, HC], F32)
        x1 = m.sb("x1", [P, NT, D], F32)
        step_x = m.sb("step_x", [P, NT], F32)
        step_row = m.sb("step_row", [P, N], F32)
        h = m.sb("h", [P, HC, N + 2], F32)
        mixed = m.sb("mixed", [P, 2, N], F32)
        s = m.sb("s", [P, HC, N], F32)
        big = m.sb("big", [P, 4, 4], F32)
        y = m.sb("y", [P, 2, HID], F32)
        code = m.sb("code", [P, 2, HID], BF16)
        codeT = m.sb("codeT", [P, 2, HC, M], BF16)
        res = m.sb("res", [P, 2, D], F32)
        ps_h = [m.bank(f"ps_h{i}") for i in range(CT)]
        ps_s = [m.bank(f"ps_s{i}") for i in range(2)]
        ps_c = m.psum("ps_c", [P, 2 * BANK], BF16)
        ps_o = [[m.bank(f"ps_o{i}") for i in range(2)], ps_h[0:2]]
        w_in = m.sem("w_in")
        x1_in = m.sem("x1_in")
        step_ready = m.sem("step_ready")
        spread = m.sem("spread")
        row_ready = m.sem("row_ready")
        edge_ready = m.sem("edge_ready")
        h_done = m.sem("h_done")
        h_ready = m.sem("h_ready")
        mid_ready = m.sem("mid_ready")
        conv_ready = m.sem("conv_ready")
        s_ready = m.sem("s_ready")
        s_turned = m.sem("s_turned")
        scale_ready = m.sem("scale_ready")
        y_ready = m.sem("y_ready")
        code_ready = m.sem("code_ready")
        c_turned = m.sem("c_turned")
        c_kept = m.sem("c_kept")
        o_done = m.sem("o_done")
        res_ready = m.sem("res_ready")
        part_ready = m.sem("part_ready")
        added = m.sem("added")
        res_out = [m.sem(f"res_out{b}") for b in range(2)]
        chain = m.sem("chain")
        block = stack.enter_context(nc.Block())
        WIDTH = (CW, CW, N - 2 * CW)
        HALVES = (slice(0, N // 2), slice(N // 2, N))
        shifted = lambda piece, by: slice(piece.start + by, piece.stop + by)
        cols = lambda t, off=0: slice(t * CW + off, t * CW + off + WIDTH[t])

        @block.sync
        def _(sp):
            with nc.allow_non_contiguous_dma(reason="a few words a partition"):
                sp.dma_start(cw[:, :, :], conv_w.rearrange("(c p) a w -> p c (a w)", p=P)).then_inc(w_in, 16)
                sp.dma_start(cb[:, :], conv_b.rearrange("(c p) -> p c", p=P)).then_inc(w_in, 16)
            spread_dma(sp, x1[:, :, :], x1_dram.rearrange("(t p) d -> p t d", p=M), x1_in)
            for t in range(NT):
                sp.wait_ge(res_ready, t + 3)
                sp.wait_ge(added, t + 1)
                spread_dma(sp, out[t * M:(t + 1) * M, :], res[:, t % 2, :], res_out[t % 2])
            for b in range(2):
                sp.wait_ge(res_out[b], 32 * PAIRS + 16)

        @block.tensor
        def _(pe):
            pe.wait_ge(step_ready, 1)
            for t in range(NT):
                g = t // 4
                last = pe.matmul(ps_h[g][:, (t % 4) * M:(t % 4 + 1) * M], step_x[0:M, t:t + 1].to_broadcast([M, P]),
                                 ident[0:M, 0:M], start=True, stop=True)
                if t % 4 == 3 or t == NT - 1:
                    last.then_inc(spread, 1)
            for c in range(HC):
                for t in range(CT):
                    if c == 0:
                        pe.wait_ge(row_ready, t + 1)
                    else:
                        pe.wait_ge(h_ready, (c - 1) * CT + t + 1)
                    for k in range(KC):
                        last = pe.matmul(ps_h[t][:, 0:WIDTH[t]], w1T[:, k, c * P:(c + 1) * P], qT[:, k, cols(t)],
                                         start=(k == 0), stop=(k == KC - 1))
                    last.then_inc(h_done, 1)

            def turn_s(t):
                pe.wait_ge(y_ready, t + 1)
                if t == NT // 2:
                    pe.wait_ge(s_ready, 2 * HC)
                for c in range(HC):
                    last = pe.transpose(ps_s[t % 2][0:M, c * P:(c + 1) * P], s[:, c, t * M:(t + 1) * M], ident[:, :])
                last.then_inc(s_turned, 1)

            def turn_code(t):
                pe.wait_ge(code_ready, t + 1)
                pe.wait_ge(c_kept, t + 1)
                for c in range(HC):
                    last = pe.transpose(ps_c[:, c * P:c * P + M], code[0:M, t % 2, c * P:(c + 1) * P],
                                        ident_b[0:M, 0:M])
                last.then_inc(c_turned, 1)

            def products(t):
                pe.wait_ge(c_kept, t + 2)
                for half in range(2):
                    pe.wait_ge((res_ready, part_ready)[half], t + 1)
                    for c in range(HC):
                        last = pe.matmul(ps_o[t % 2][half][0:M, :], codeT[:, t % 2, c, :], w2T[:, c, half * BANK:(half + 1) * BANK],
                                         start=(c == 0), stop=(c == HC - 1))
                    last.then_inc(o_done, 1)

            pe.wait_ge(s_ready, 2 * HC - 1)
            turn_s(0)
            turn_s(1)
            for t in range(NT):
                turn_code(t)
                if t + 2 < NT:
                    turn_s(t + 2)
                products(t)

        @block.scalar
        def _(act):
            act.sem_inc(c_kept, 1)
            act.sem_inc(y_ready, 2)

            def silu(c):
                for i, piece in enumerate(HALVES):
                    act.wait_ge(conv_ready, 2 * c + i + 1)
                    nc.scalar.activation(s[:, c, piece], mixed[:, c % 2, piece], ACT.Silu).then_inc(s_ready, 1)

            for g, (a, b) in enumerate(TURNS):
                act.wait_ge(spread, g + 1)
                nc.scalar.copy(step_row[:, a * M:b * M], ps_h[g][:, 0:(b - a) * M]).then_inc(row_ready, 1)
            act.wait_ge(w_in, 32)
            for c in range(HC):
                for i, piece in enumerate(HALVES):
                    act.wait_ge(h_ready, c * CT + 2 + i)
                    if c >= 2:
                        act.wait_ge(s_ready, 2 * c - 3 + i)
                    nc.scalar.activation(mixed[:, c % 2, piece], h[:, c, shifted(piece, 1)], ACT.Identity,
                                         bias=cb[:, c:c + 1], scale=cw[:, c, 1:2]).then_inc(mid_ready, 1)
                if c >= 1:
                    silu(c - 1)
            silu(HC - 1)

            def steps(t):
                act.wait_ge(scale_ready, t + 1)
                nc.scalar.activation(y[0:M, t % 2, :], ps_s[t % 2][0:M, :], ACT.Copy, bias=ROUND,
                                     scale=big[0:M, t % 4, 2:3]).then_inc(y_ready, 1)

            def second_half(t):
                act.wait_ge(res_out[t % 2], 32 * (t // 2) + 16)
                act.wait_ge(o_done, 2 * t + 2)
                nc.scalar.activation(res[0:M, t % 2, BANK:D], ps_o[t % 2][1][0:M, :], ACT.Copy,
                                     scale=big[0:M, t % 4, 3:4]).then_inc(part_ready, 1)

            steps(0)
            for t in range(NT):
                act.wait_ge(c_turned, t + 1)
                nc.scalar.copy(codeT[:, t % 2, :, :],
                               ps_c[:, 0:HC * P].rearrange("p (c n) -> p c n", n=P)[:, :, 0:M]).then_inc(c_kept, 1)
                if t:
                    second_half(t - 1)
                if t + 1 < NT:
                    steps(t + 1)
            second_half(NT - 1)

        @block.gpsimd
        def _(pool):
            pool.wait_ge(x1_in, 32)
            for t in range(NT):
                pool.wait_ge(part_ready, t + 3)
                nc.gpsimd.tensor_tensor(res[0:M, t % 2, BANK:D], res[0:M, t % 2, BANK:D], x1[0:M, t, BANK:D],
                                        ALU.add).then_inc(added, 1)

        @block.vector
        def _(dve):
            link = chained(dve, chain)
            link(nc.vector.tensor_scalar(step_x[0:M, :], unit_x[0:M, :], unit_w[0:M, 0:1], None, ALU.mult))
            dve.sem_inc(step_ready, 1)
            nc.vector.memset(h[:, :, 0:1], 0.0)
            link(nc.vector.memset(h[:, :, N + 1:N + 2], 0.0))
            dve.sem_inc(res_ready, 2)
            dve.sem_inc(part_ready, 2)
            for b in range(2):
                dve.sem_inc(res_out[b], 16)
            dve.wait_ge(w_in, 32)
            dve.wait_ge(row_ready, CT)

            def scale_h(c):
                for t in range(CT):
                    dve.wait_ge(h_done, c * CT + t + 1)
                    nc.vector.tensor_tensor(h[:, c, cols(t, 1)], ps_h[t][:, 0:WIDTH[t]], step_row[:, cols(t)],
                                            ALU.mult).then_inc(h_ready, 1)

            def convolve(c):
                for i, piece in enumerate(HALVES):
                    to = mixed[:, c % 2, piece]
                    dve.wait_ge(mid_ready, 2 * c + i + 1)
                    link(nc.vector.scalar_tensor_tensor(to, h[:, c, shifted(piece, 0)], cw[:, c, 0:1], to,
                                                        ALU.mult, ALU.add))
                    nc.vector.scalar_tensor_tensor(to, h[:, c, shifted(piece, 2)], cw[:, c, 2:3], to,
                                                   ALU.mult, ALU.add).then_inc(conv_ready, 1)

            scale_h(0)
            for c in range(HC):
                if c + 1 < HC:
                    scale_h(c + 1)
                convolve(c)

            def scale(t):
                b = t % 4
                dve.wait_ge(s_turned, t + 1)
                link(nc.vector.tensor_reduce(big[0:M, b, 0:1], ps_s[t % 2][0:M, :], AX_X, ALU.max,
                                             apply_absolute_value=True))
                link(nc.vector.tensor_scalar(big[0:M, b, 1:2], big[0:M, b, 0:1], EPS_Q, None, ALU.max))
                link(nc.vector.reciprocal(big[0:M, b, 2:3], big[0:M, b, 1:2]))
                nc.vector.tensor_scalar(big[0:M, b, 2:3], big[0:M, b, 2:3], 127.0, None, ALU.mult).then_inc(scale_ready, 1)
                link(nc.vector.tensor_scalar(big[0:M, b, 3:4], big[0:M, b, 1:2], unit_w[0:M, 1:2], 1.0 / 127.0,
                                             ALU.mult, ALU.mult))

            def codes(t):
                b = t % 2
                dve.wait_ge(y_ready, t + 3)
                link(nc.vector.tensor_scalar(y[0:M, b, :], y[0:M, b, :], ROUND, 127.0, ALU.subtract, ALU.min))
                nc.vector.tensor_scalar(code[0:M, b, :], y[0:M, b, :], -128.0, None, ALU.max).then_inc(code_ready, 1)

            def result(t):
                b = t % 2
                dve.wait_ge(res_out[b], 32 * (t // 2) + 16)
                dve.wait_ge(o_done, t * 2 + 1)
                nc.vector.scalar_tensor_tensor(res[0:M, b, 0:BANK], ps_o[t % 2][0][0:M, :], big[0:M, t % 4, 3:4],
                                               x1[0:M, t, 0:BANK], ALU.mult, ALU.add).then_inc(res_ready, 1)

            scale(0)
            codes(0)
            dve.wait_ge(x1_in, 32)
            for t in range(NT):
                if t + 1 < NT:
                    scale(t + 1)
                if t:
                    result(t - 1)
                if t + 1 < NT:
                    codes(t + 1)
            result(NT - 1)




def program(nc, x, src, dst, W_self0, W_neigh0, b0, W_self1, W_neigh1, b1, w_qkv, w_out, b_out, proj,
            ffn_w1, ffn_conv_w, ffn_conv_b, ffn_w2, out):
    def dram(name, shape, dt=F32):
        return nc.dram_tensor(name, shape, dt, kind="Internal").ap()

    edges_pad = dram("edges_pad", (2, E + ECAP), I32)
    adj_dram = dram("adj_dram", (M, NT, NP))
    hT_hi, hT_lo = dram("hT_hi", (D, NP)), dram("hT_lo", (D, NP))
    oT_hi, oT_lo = dram("oT_hi", (D, N)), dram("oT_lo", (D, N))
    mid, x1 = dram("mid", (N, D)), dram("x1", (N, D))
    w1T_dram, w2T_dram = dram("w1T", (P, KC, HID), BF16), dram("w2T", (P, HC, D), BF16)
    with ExitStack() as stack:
        m = Pool(nc, stack, "all")
        ident = m.sb("ident", [P, P], F32)
        ident_b = m.sb("ident_b", [P, P], BF16)
        ones_r = m.sb("ones_r", [P, P], F32R)
        unit_w = m.sb("unit_w", [P, 2], F32)
        with ExitStack() as graph:
            with ExitStack() as nodes:
                m = Pool(nc, nodes, "xn")
                xT_hi = m.sb("xT_hi", [P, KC, NP], F32R)
                xT_lo = m.sb("xT_lo", [P, KC, NP], F32R)
                stage_prepare(nc, x, src, dst, edges_pad, ffn_w1, ffn_w2, ident, ident_b, ones_r, xT_hi, xT_lo,
                              w1T_dram, w2T_dram, unit_w, adj_dram)
                panel_n, panel_s = Panel(Pool(nc, nodes, "panel_n")), Panel(Pool(nc, nodes, "panel_s"))
                pT = m.sb("pT", [P, NP], F32)
                stage_attention(nc, w_qkv, proj, xT_hi, xT_lo, ident, oT_hi, oT_lo, panel_n, panel_s, pT,
                                W_neigh0, W_self0)
                m = Pool(nc, graph, "graph")
                inv_row = m.sb("inv_row", [P, NP], F32, side="right")
                inv_col = m.sb("inv_col", [P, NT], F32, side="right")
                adj = m.sb("adj", [P, NT, NP], F32R, side="right")
                raw_n = m.sb("raw_n", [P, KC, PW], F32, side="right")
                stage_sage0(nc, W_neigh0, W_self0, b0, xT_hi, xT_lo, adj_dram, adj, inv_row, inv_col, ident, ones_r,
                            hT_hi, hT_lo,
                            panel_n, panel_s, pT, raw_n, W_neigh1)
            stage_sage1(nc, W_neigh1, W_self1, hT_hi, hT_lo, adj, inv_col, mid, raw_n)
        m = Pool(nc, stack, "codes")
        qT = m.sb("qT", [P, KC, N], BF16)
        unit_x = m.sb("unit_x", [P, NT], F32)
        w1T = m.sb("w1T", [P, KC, HID], BF16)
        w2T = m.sb("w2T", [P, HC, D], BF16)
        stage_mix(nc, w_out, b1, b_out, x, oT_hi, oT_lo, mid, ident_b, x1, qT, unit_x,
                  w1T, w1T_dram, w2T, w2T_dram)
        stage_ffn(nc, ffn_conv_w, ffn_conv_b, x1, out, ident, ident_b, w1T, w2T, unit_w, qT, unit_x)


INPUTS = ["x", "src", "dst", "L0_gnn_W_self0", "L0_gnn_W_neigh0", "L0_gnn_b0", "L0_gnn_W_self1", "L0_gnn_W_neigh1",
          "L0_gnn_b1", "L0_mix_w_qkv", "L0_mix_w_out", "L0_mix_b_out", "L0_mix_proj", "L0_ffn_w1", "L0_ffn_conv_w",
          "L0_ffn_conv_b", "L0_ffn_w2"]


def kernel(**inputs):
    import numpy as np
    import concourse.bacc as bacc
    from concourse.bass_utils import run_bass_kernel_spmd

    nc = bacc.Bacc("TRN2", target_bir_lowering=False, num_devices=1)
    arrays = {f"in_{name}": np.ascontiguousarray(inputs[name]) for name in INPUTS}
    args = [nc.dram_tensor(name, a.shape, mybir.dt.from_np(a.dtype), kind="ExternalInput").ap()
            for name, a in arrays.items()]
    out = nc.dram_tensor("out", (N, D), F32, kind="ExternalOutput").ap()
    program(nc, *args, out)
    run = run_bass_kernel_spmd(nc, [arrays], core_ids=[0])
    return run.results[0]["out"]
```
